# Optimizing a Trainium2 kernel written in Bass

```python
import numpy as np
import jax
import jax.numpy as jnp

def _softmax(x, axis=-1):
    return jax.nn.softmax(x, axis=axis)
def _gelu(x):
    return jax.nn.gelu(x, approximate=True)
def _silu(x):
    return jax.nn.silu(x)
def _sigmoid(x):
    return jax.nn.sigmoid(x)
def _layernorm(x, axis=-1, eps=1e-5):
    m = jnp.mean(x, axis=axis, keepdims=True)
    v = jnp.var(x, axis=axis, keepdims=True)
    return (x - m) / jnp.sqrt(v + eps)
def _scatter_add(tgt, idx, src, axis=0):
    return tgt.at[idx].add(src)
def _segment_sum(src, seg, n):
    return jax.ops.segment_sum(src, seg, n)

kernel_name = 'mk_conv_seq_d2_conv_nchw256_e588f0'

def setup_inputs(seed: int = 0):
    np.random.seed(seed)
    _w = jnp.asarray
    def _rec_inputs():
        import jax
        import jax.numpy as jnp
        _gk = jax.random.key(seed)
        x = -0.000125 + 0.9999 * jax.random.normal(jax.random.fold_in(_gk, 1), (8, 256, 128, 128), jnp.float32)
        return x
    x = _rec_inputs()
    def _L0_conv_setup():
        import jax, jax.numpy as jnp
        import numpy as np

        def _dw_conv(x, w, ks):
            pad = (ks - 1) // 2
            return jax.lax.conv_general_dilated(x, w, window_strides=(1, 1), padding=[(pad, pad), (pad, pad)], feature_group_count=x.shape[1], dimension_numbers=('NCHW', 'OIHW', 'NCHW'))
        key = jax.random.key(seed)
        ks = jax.random.split(key, 12)
        B, Cin, M, O, H, W = (8, 256, 256, 256, 128, 128)
        k = 128
        inp = {'x': jax.random.normal(ks[0], (B, Cin, H, W), jnp.float32), 'pw1_w': jax.random.normal(ks[1], (M, Cin), jnp.float32) * 0.02, 'pw1_b': jnp.zeros((M,), jnp.float32), 'fc1_w': jax.random.normal(ks[2], (2 * M, M), jnp.float32) * 0.02, 'fc1_b': jnp.zeros((2 * M,), jnp.float32), 'fc2_w': jax.random.normal(ks[3], (M, 2 * M), jnp.float32) * 0.02, 'fc2_b': jnp.zeros((M,), jnp.float32), 'off_w': jax.random.normal(ks[4], (6, M), jnp.float32) * 0.02, 'off_b': jnp.zeros((6,), jnp.float32), 'dw3': jax.random.normal(ks[5], (M, 1, 3, 3), jnp.float32) * 0.1, 'dw5': jax.random.normal(ks[6], (M, 1, 5, 5), jnp.float32) * 0.1, 'dw7': jax.random.normal(ks[7], (M, 1, 7, 7), jnp.float32) * 0.1, 'pw_w': jax.random.normal(ks[8], (O, 3 * M), jnp.float32) * 0.02, 'pw_b': jnp.zeros((O,), jnp.float32), 'k': k}
        return inp
    _L0_conv_all = _L0_conv_setup()
    _L0_conv_in = {k: v for k, v in _L0_conv_all.items() if k in ('pw1_w', 'pw1_b', 'fc1_w', 'fc1_b', 'fc2_w', 'fc2_b', 'off_w', 'off_b', 'dw3', 'dw5', 'dw7', 'pw_w', 'pw_b', )}
    del _L0_conv_all

    def _L1_conv_setup():
        import jax, jax.numpy as jnp
        import numpy as np
        from jax import lax
        K_PEAKS = 2
        N_BINS = 180
        BW = float(np.radians(15.0))
        HIGH_RATIO = 0.3
        ALPHA = 1.2
        BETA = 0.8
        PI = float(np.pi)

        def _forward(x, w_in, w_out):
            B, C, H, W = x.shape
            cy, cx = (H // 2, W // 2)
            r_max = float(min(cy, cx))
            yy, xx = jnp.meshgrid(jnp.arange(H), jnp.arange(W), indexing='ij')
            dy = (yy - cy).astype(jnp.float32)
            dx = (xx - cx).astype(jnp.float32)
            r = jnp.sqrt(dy * dy + dx * dx)
            theta = jnp.arctan2(dy, dx) + PI
            x_proj = jnp.einsum('bchw,mc->bmhw', x, w_in)
            f = jnp.fft.fftshift(jnp.fft.fft2(x_proj, norm='ortho'), axes=(-2, -1))
            mag = jnp.abs(f)
            high_mask = r > HIGH_RATIO * r_max
            weighted = mag.mean(axis=1) * high_mask.astype(mag.dtype)
            theta_mod = theta % PI
            edges = jnp.linspace(0.0, PI, N_BINS + 1)
            bin_idx = jnp.clip(jnp.searchsorted(edges, theta_mod.reshape(-1), side='left') - 1, 0, N_BINS - 1)
            hist = jax.vmap(lambda e: jax.ops.segment_sum(e, bin_idx, num_segments=N_BINS))(weighted.reshape(B, -1))
            hp = jnp.pad(hist, ((0, 0), (1, 1)))
            e_smooth = 0.25 * hp[:, :-2] + 0.5 * hp[:, 1:-1] + 0.25 * hp[:, 2:]
            centers = (edges[:-1] + edges[1:]) * 0.5

            def peaks_of(e):
                mean_e = e.mean()
                is_peak = (e > mean_e) & (e > jnp.roll(e, 1)) & (e > jnp.roll(e, -1))
                npk = is_peak.sum()
                masked = jnp.where(is_peak, e, -jnp.inf)
                _, topi = lax.top_k(masked, K_PEAKS)
                cnt = jnp.clip(npk, 1, K_PEAKS)
                sel = jnp.minimum(jnp.arange(K_PEAKS), cnt - 1)
                picked = jnp.where(npk > 0, topi[sel], jnp.argmax(e))
                return centers[picked]
            peak_angles = jax.vmap(peaks_of)(e_smooth)
            d = jnp.abs(theta[None, None, :, :] - peak_angles[:, :, None, None])
            d = jnp.minimum(d, PI - d)
            enh = jnp.any((d <= BW) & high_mask[None, None], axis=1)
            gain = jnp.where(enh, ALPHA, jnp.where(high_mask[None] & ~enh, BETA, 1.0))
            gain = gain.astype(jnp.float32)
            f_enh = f * gain[:, None].astype(f.dtype)
            x_enh = jnp.fft.ifft2(jnp.fft.ifftshift(f_enh, axes=(-2, -1)), norm='ortho').real
            out = jnp.einsum('bmhw,cm->bchw', x_enh, w_out)
            return x + out
        key = jax.random.key(seed)
        k1, k2, k3 = jax.random.split(key, 3)
        x = jax.random.normal(k1, (4, 256, 128, 128), dtype=jnp.float32)
        w_in = jax.random.normal(k2, (16, 256), dtype=jnp.float32) * (1.0 / np.sqrt(256.0))
        w_out = jax.random.normal(k3, (256, 16), dtype=jnp.float32) * (1.0 / np.sqrt(16.0))
        return {'x': x, 'w_in': w_in, 'w_out': w_out}
    _L1_conv_all = _L1_conv_setup()
    _L1_conv_in = {k: v for k, v in _L1_conv_all.items() if k in ('w_in', 'w_out', )}
    del _L1_conv_all

    return {
        "x": x,
        "L0_conv_pw1_w": _L0_conv_in["pw1_w"],
        "L0_conv_pw1_b": _L0_conv_in["pw1_b"],
        "L0_conv_fc1_w": _L0_conv_in["fc1_w"],
        "L0_conv_fc1_b": _L0_conv_in["fc1_b"],
        "L0_conv_fc2_w": _L0_conv_in["fc2_w"],
        "L0_conv_fc2_b": _L0_conv_in["fc2_b"],
        "L0_conv_off_w": _L0_conv_in["off_w"],
        "L0_conv_off_b": _L0_conv_in["off_b"],
        "L0_conv_dw3": _L0_conv_in["dw3"],
        "L0_conv_dw5": _L0_conv_in["dw5"],
        "L0_conv_dw7": _L0_conv_in["dw7"],
        "L0_conv_pw_w": _L0_conv_in["pw_w"],
        "L0_conv_pw_b": _L0_conv_in["pw_b"],
        "L1_conv_w_in": _L1_conv_in["w_in"],
        "L1_conv_w_out": _L1_conv_in["w_out"],
    }

def reference(x, L0_conv_pw1_w, L0_conv_pw1_b, L0_conv_fc1_w, L0_conv_fc1_b, L0_conv_fc2_w, L0_conv_fc2_b, L0_conv_off_w, L0_conv_off_b, L0_conv_dw3, L0_conv_dw5, L0_conv_dw7, L0_conv_pw_w, L0_conv_pw_b, L1_conv_w_in, L1_conv_w_out):
    import jax
    import jax.numpy as jnp
    def _L0_conv_ref(x, pw1_w, pw1_b, fc1_w, fc1_b, fc2_w, fc2_b, off_w, off_b, dw3, dw5, dw7, pw_w, pw_b, k):
        import jax, jax.numpy as jnp
        import numpy as np

        def _dw_conv(x, w, ks):
            pad = (ks - 1) // 2
            return jax.lax.conv_general_dilated(x, w, window_strides=(1, 1), padding=[(pad, pad), (pad, pad)], feature_group_count=x.shape[1], dimension_numbers=('NCHW', 'OIHW', 'NCHW'))
        B, _, H, W = x.shape
        residual = x
        h = jnp.einsum('bchw,oc->bohw', x, pw1_w) + pw1_b[None, :, None, None]
        gap = h.mean(axis=(2, 3))
        hid = jax.nn.relu(gap @ fc1_w.T + fc1_b)
        scores = jax.nn.sigmoid(hid @ fc2_w.T + fc2_b)
        _, idx = jax.lax.top_k(scores, k)
        mask = jnp.zeros_like(scores).at[jnp.arange(B)[:, None], idx].set(1.0)
        h = jax.nn.relu(h)
        gap2 = h.mean(axis=(2, 3))
        offsets = jnp.tanh(gap2 @ off_w.T + off_b).reshape(B, 3, 2)
        sel = (h * mask[:, :, None, None])[:, :k]
        conv_in = sel.reshape(1, B * k, H, W)
        outs = []
        for i, (ksz, base) in enumerate([(3, dw3), (5, dw5), (7, dw7)]):
            scale = jax.nn.sigmoid(offsets[:, i, 0]).reshape(B, 1, 1, 1, 1)
            shift = jnp.tanh(offsets[:, i, 1]).reshape(B, 1, 1, 1, 1)
            w = base[:k][None] * (1.0 + scale) + shift
            y = _dw_conv(conv_in, w.reshape(B * k, 1, ksz, ksz), ksz)
            outs.append(y.reshape(B, k, H, W))
        fused = jnp.concatenate(outs, axis=1)
        sel_pw = pw_w[:, :3 * k]
        out = jnp.einsum('bchw,oc->bohw', fused, sel_pw) + pw_b[None, :, None, None]
        return out + residual

    def _L1_conv_ref(x, w_in, w_out):
        import jax, jax.numpy as jnp
        import numpy as np
        from jax import lax
        K_PEAKS = 2
        N_BINS = 180
        BW = float(np.radians(15.0))
        HIGH_RATIO = 0.3
        ALPHA = 1.2
        BETA = 0.8
        PI = float(np.pi)

        def _forward(x, w_in, w_out):
            B, C, H, W = x.shape
            cy, cx = (H // 2, W // 2)
            r_max = float(min(cy, cx))
            yy, xx = jnp.meshgrid(jnp.arange(H), jnp.arange(W), indexing='ij')
            dy = (yy - cy).astype(jnp.float32)
            dx = (xx - cx).astype(jnp.float32)
            r = jnp.sqrt(dy * dy + dx * dx)
            theta = jnp.arctan2(dy, dx) + PI
            x_proj = jnp.einsum('bchw,mc->bmhw', x, w_in)
            f = jnp.fft.fftshift(jnp.fft.fft2(x_proj, norm='ortho'), axes=(-2, -1))
            mag = jnp.abs(f)
            high_mask = r > HIGH_RATIO * r_max
            weighted = mag.mean(axis=1) * high_mask.astype(mag.dtype)
            theta_mod = theta % PI
            edges = jnp.linspace(0.0, PI, N_BINS + 1)
            bin_idx = jnp.clip(jnp.searchsorted(edges, theta_mod.reshape(-1), side='left') - 1, 0, N_BINS - 1)
            hist = jax.vmap(lambda e: jax.ops.segment_sum(e, bin_idx, num_segments=N_BINS))(weighted.reshape(B, -1))
            hp = jnp.pad(hist, ((0, 0), (1, 1)))
            e_smooth = 0.25 * hp[:, :-2] + 0.5 * hp[:, 1:-1] + 0.25 * hp[:, 2:]
            centers = (edges[:-1] + edges[1:]) * 0.5

            def peaks_of(e):
                mean_e = e.mean()
                is_peak = (e > mean_e) & (e > jnp.roll(e, 1)) & (e > jnp.roll(e, -1))
                npk = is_peak.sum()
                masked = jnp.where(is_peak, e, -jnp.inf)
                _, topi = lax.top_k(masked, K_PEAKS)
                cnt = jnp.clip(npk, 1, K_PEAKS)
                sel = jnp.minimum(jnp.arange(K_PEAKS), cnt - 1)
                picked = jnp.where(npk > 0, topi[sel], jnp.argmax(e))
                return centers[picked]
            peak_angles = jax.vmap(peaks_of)(e_smooth)
            d = jnp.abs(theta[None, None, :, :] - peak_angles[:, :, None, None])
            d = jnp.minimum(d, PI - d)
            enh = jnp.any((d <= BW) & high_mask[None, None], axis=1)
            gain = jnp.where(enh, ALPHA, jnp.where(high_mask[None] & ~enh, BETA, 1.0))
            gain = gain.astype(jnp.float32)
            f_enh = f * gain[:, None].astype(f.dtype)
            x_enh = jnp.fft.ifft2(jnp.fft.ifftshift(f_enh, axes=(-2, -1)), norm='ortho').real
            out = jnp.einsum('bmhw,cm->bchw', x_enh, w_out)
            return x + out
        return _forward(x, w_in, w_out)

    def _gn(v, G=32, eps=1e-5):
        B_, C_, H_, W_ = v.shape
        g = v.reshape(B_, G, C_ // G, H_, W_)
        m = jnp.mean(g, axis=(2, 3, 4), keepdims=True)
        s = jnp.var(g, axis=(2, 3, 4), keepdims=True)
        return ((g - m) / jnp.sqrt(s + eps)).reshape(v.shape)

    def _ln_c(v, eps=1e-6):
        m = jnp.mean(v, axis=1, keepdims=True)
        s = jnp.var(v, axis=1, keepdims=True)
        return (v - m) / jnp.sqrt(s + eps)

    def _ln_t(v, eps=1e-5):
        m = jnp.mean(v, axis=-1, keepdims=True)
        s = jnp.var(v, axis=-1, keepdims=True)
        return (v - m) / jnp.sqrt(s + eps)

    def _to_tokens(v):
        B_, C_, H_, W_ = v.shape
        return v.reshape(B_, C_, H_ * W_).transpose(0, 2, 1)
    def _from_tokens(t, like):
        B_, C_, H_, W_ = like.shape
        return t.transpose(0, 2, 1).reshape(B_, C_, H_, W_)

    x = _L0_conv_ref(x, L0_conv_pw1_w, L0_conv_pw1_b, L0_conv_fc1_w, L0_conv_fc1_b, L0_conv_fc2_w, L0_conv_fc2_b, L0_conv_off_w, L0_conv_off_b, L0_conv_dw3, L0_conv_dw5, L0_conv_dw7, L0_conv_pw_w, L0_conv_pw_b, 128)
    x = _L1_conv_ref(x, L1_conv_w_in, L1_conv_w_out)
    return x


_drawn_inputs = setup_inputs


def setup_inputs(seed=0):
    import zlib

    import numpy as np

    out = dict(_drawn_inputs(seed))
    spreads = {'L0_conv_pw1_b': (0.0, 0.1),
     'L0_conv_fc1_b': (0.0, 0.1),
     'L0_conv_fc2_b': (0.0, 0.1),
     'L0_conv_off_b': (0.0, 0.1),
     'L0_conv_pw_b': (0.0, 0.1)}
    factors = {'L0_conv_fc1_w': 2.756, 'L0_conv_dw3': 3.318}
    for name, (base, spread) in spreads.items():
        noise = np.random.default_rng([zlib.crc32(name.encode()), seed]).standard_normal(out[name].shape)
        drawn = base * np.exp(spread * noise) if base else spread * noise
        out[name] = jnp.asarray(drawn.astype(out[name].dtype))
    for name, factor in factors.items():
        out[name] = (out[name] * factor).astype(out[name].dtype)
    return out
```

```python
from contextlib import ExitStack

import numpy as np

import concourse.bass as bass
from concourse import mybir

F32 = mybir.dt.float32
F16 = mybir.dt.float16
ALU = mybir.AluOpType
ACT = mybir.ActivationFunctionType
AX = mybir.AxisListType

P = 128
B, C = 8, 256
KH = C // P
PIX = P * P
ROWS = 4
CHUNK = ROWS * P
NCH = P // ROWS
XSLOTS = 4
PAD = 3
YP = P + 2 * PAD
TAP_ROWS = [(0, 3), (-1, 3), (1, 3), (-2, 2), (2, 2), (-3, 1), (3, 1)]
TSLOTS = sum(k for _, k in TAP_ROWS)
TCOLS = TSLOTS * P
PERIOD = 8
VCH = 8
NV = P // VCH
HID = 2 * C
M = 16
NBINS = 180
OUT3 = 3 * P
PW_SCALE = 64.0
SATURATED = 16.63553

XQ = 3 * NCH
FD, FA = 38, 3
LP, LA, LD = 31, 18, 77


def build(nc, t):
    with ExitStack() as ctx:
        def sb(name, shape, dt=F32):
            return ctx.enter_context(nc.sbuf_tensor(name, shape, dt))

        def sem(name):
            return ctx.enter_context(nc.semaphore(name))

        names = ["w1T", "b1col", "fc1T", "fc1b", "fc2T", "fc2bB", "offT", "offbB", "pwT", "pwb", "winT",
                 "woT", "dft_fwd", "dft_c", "dft_s", "dft_ns", "inv_cs", "inv_nsc", "inv_c", "inv_ns",
                 "ident", "lower", "theta", "gain_lo", "gain_d", "high16", "band", "istap", "binrow", "centers"]
        k = {}
        for name in names:
            src = t[name]
            k[name] = sb("k_" + name, list(src.shape), F16 if name == "band" else F32)
        b1row = sb("b1row", [1, CHUNK])
        b1h = sb("b1h", [1, CHUNK], F16)
        b1l = sb("b1l", [1, CHUNK], F16)
        ones16 = sb("ones16", [P, P], F16)
        ones = sb("ones", [P, P])
        wo16 = sb("wo16", [3 * M, C], F16)
        wol = sb("wol", [3 * M, C], F16)

        arena = sb("arena", [P, 2 * P * YP], F16)
        hT = [arena[:, i * P * YP:(i + 1) * P * YP].rearrange("p (c y) -> p c y", y=YP) for i in range(2)]
        OHC = P * NBINS
        onehot = arena[:, 0:OHC].rearrange("p (u b) -> p u b", b=NBINS)
        enh_in = arena[0:3 * M, 0:PIX]
        xproj = arena[:, OHC:OHC + 2 * M * P].bitcast(F32).rearrange("p (m y) -> p m y", m=M)
        mag_a = arena[:, OHC:OHC + 2 * M * P].bitcast(F32)
        enh_hl = arena[:, OHC:OHC + 2 * M * P].rearrange("p (t m x) -> p t m x", t=2, m=M)
        mag_b = arena[:, OHC + 2 * M * P:OHC + 4 * M * P].bitcast(F32)

        work2 = sb("work2", [P, 2 * 2 * TCOLS + 4 * OUT3 * 2], F16)
        toep = [[work2[:, (2 * u + h) * TCOLS:(2 * u + h + 1) * TCOLS] for h in range(2)] for u in range(2)]
        gst0 = 4 * TCOLS
        gst = [work2[:, gst0 + 2 * OUT3 * s:gst0 + 2 * OUT3 * (s + 1)].bitcast(F32) for s in range(4)]
        f1 = work2[:, 0:2 * M * 2 * P].bitcast(F32).rearrange("p (m c) -> p m c", m=M)

        G = ROWS * OUT3
        work3 = sb("work3", [P, 8 * G], F16)
        gl = [work3[:, 2 * G * g:2 * G * (g + 1)].bitcast(F32) for g in range(2)]
        gh = [work3[:, 4 * G + G * g:4 * G + G * (g + 1)] for g in range(2)]
        glo = [work3[:, 6 * G + G * g:6 * G + G * (g + 1)] for g in range(2)]
        f2 = work3[:, 0:4 * M * P].bitcast(F32).rearrange("p (r m u) -> p r m u", r=2, m=M)

        at = [0]

        def temp(*shape):
            size = int(np.prod(shape))
            a = work3[:, at[0]:at[0] + 2 * size].bitcast(F32)
            at[0] += 2 * size
            return a.rearrange("p (a b) -> p a b", a=shape[0]) if len(shape) == 2 else a

        hidb, g2b, pwm = temp(HID // P, P), temp(KH, P), temp(3, C)
        z, zm, gt, eq, zd = temp(C), temp(C), temp(C), temp(C), temp(P)
        bins = arena[0:1, OHC + 2 * M * P:OHC + 2 * M * P + 16 * (NBINS + 2)].bitcast(F32).rearrange("p (i b) -> p i b", i=8)

        vbase = [sb(f"vbase{i}", [P, VCH, TSLOTS, PERIOD]) for i in range(2)]
        vsum = sb("vsum", [P, VCH, TSLOTS, PERIOD])
        vhl = [[sb(f"v{'hl'[h]}{i}", [P, VCH, TSLOTS, PERIOD], F16) for h in range(2)] for i in range(2)]
        xr = [sb(f"xr{s}", [P, KH, CHUNK]) for s in range(XSLOTS)]
        yst = [sb(f"yst{s}", [P, KH, CHUNK]) for s in range(2)]
        relu_out = sb("relu_out", [P, 2, CHUNK], F16)
        xs = sb("xs", [P, KH, NCH])
        relu_hi = sb("relu_hi", [P, NCH])
        xsum = sb("xsum", [P, KH])
        gap = sb("gap", [P, KH])
        hid_raw = sb("hid_raw", [P, HID // P])
        hid = sb("hid", [P, HID // P])
        zc = sb("zc", [P, 1])
        rank = sb("rank", [P, 1])
        mask = sb("mask", [P, 1])
        s1row = sb("s1row", [1, P])
        g2 = sb("g2", [P, KH])
        g2s = sb("g2s", [P, KH])
        off = sb("off", [P, 6])
        offt = sb("offt", [P, 6])
        th = sb("th", [P, 6])
        s1p = sb("s1p", [P, 3])
        rs = sb("rs", [P, 3])
        rq = sb("rq", [P, 3])
        R = sb("R", [P, TSLOTS])
        shifts = sb("shifts", [P, TSLOTS, PERIOD])
        sc = sb("sc", [P, 3])
        pwh = sb("pwh", [P, 3, C], F16)
        pwl = sb("pwl", [P, 3, C], F16)
        mag = sb("mag", [P, P])
        magm = sb("magm", [P, P])
        ms = sb("ms", [P, P, 2], F16)
        h2 = sb("h2", [2, NBINS])
        hp = sb("hp", [1, NBINS + 2])
        pc = sb("pc", [1, 16])
        pkb = sb("pkb", [P, 2])
        gn = sb("gn", [P, 4, P])
        gain = sb("gain", [P, P])

        ps = [ctx.enter_context(nc.psum_tensor(f"ps{i}", [P, 512], F32)) for i in range(8)]

        g_dram = nc.dram_tensor("conv_out", [P, P, OUT3], F32, kind="Internal").ap()
        y_dram = nc.dram_tensor("block_out", [KH, P, PIX], F32, kind="Internal").ap()
        e_dram = nc.dram_tensor("enhanced", [2 * M, P, P], F16, kind="Internal").ap()
        x_in_d, out_d = t["x"], t["out"]

        consts_in = sem("consts_in")
        setup = sem("setup")
        x_in = [sem(f"x_in{s}") for s in range(XSLOTS)]
        x_used = sem("x_used")
        pads = sem("pads")
        ha_ready, ha_out = sem("ha_ready"), sem("ha_out")
        hb_ready, hi_done, lo_done = sem("hb_ready"), sem("hi_done"), sem("lo_done")
        fc_pe, fc_act, fc_dve = sem("fc_pe"), sem("fc_act"), sem("fc_dve")
        v_in = [sem(f"v_in{i}") for i in range(2)]
        v_step = sem("v_step")
        t_ready = sem("t_ready")
        conv_ready, conv_out = sem("conv_ready"), sem("conv_out")
        g_out = [sem(f"g_out{s}") for s in range(4)]
        g_in = [sem(f"g_in{s}") for s in range(2)]
        gh_done, glo_done = sem("gh_done"), sem("glo_done")
        xb_done, pw_ready = sem("xb_done"), sem("pw_ready")
        y_out = [sem(f"y_out{s}") for s in range(2)]
        xp_ready, xp_out = sem("xp_ready"), sem("xp_out")
        oh_in = sem("oh_in")
        l_pe, l_act, l_dve = sem("l_pe"), sem("l_act"), sem("l_dve")
        e_out, e_in = sem("e_out"), sem("e_in")
        mix_ready = sem("mix_ready")
        passed = {e: sem("passed_" + e) for e in ("sp", "pool", "dve", "pe")}
        CX, C2, CV, CM = XSLOTS, 2, 2 * VCH, 1

        XI = 16 * XQ // XSLOTS
        XI1 = 16 * NCH // XSLOTS
        YI = 16 * NCH
        J4, J2 = NCH // 4, NCH // 2

        block = ctx.enter_context(nc.Block())

        @block.sync
        def _(sp):
            for name in names:
                sp.dma_start(k[name][:], t[name]).then_inc(consts_in, 16)
            sp.dma_start(b1row[:, :], t["b1row"]).then_inc(consts_in, 16)

            def load_x(n, phase, chunk, s):
                sp.wait_ge(x_used, n * XQ + (phase * NCH + 1) + chunk)
                src = x_in_d[bass.ds(n, 1), :, :, bass.ds(chunk * CHUNK, CHUNK)].rearrange("n h p x -> p (n h) x")
                sp.dma_start(xr[s][:], src).then_inc(x_in[s], 16)

            with sp.Fori(0, B) as n:
                with sp.Fori(0, J4) as j:
                    for s in range(XSLOTS):
                        sp.wait_ge(hb_ready, n * NCH + j * 4 + (s + 1))
                        sp.sem_inc(passed["sp"], 1)
                        load_x(n, 0, j * 4 + s, s)
                with sp.Fori(0, P // 4) as j:
                    for s in range(4):
                        sp.wait_ge(conv_out, n * P + j * 4 + (s + 1 + C2))
                        sp.dma_start(g_dram[bass.ds(j * 4 + s, 1)].rearrange("c y f -> (c y) f"), gst[s])\
                            .then_inc(g_out[s], 16)
                for s in range(4):
                    sp.wait_ge(g_out[s], n * (16 * P // 4) + 16 * (P // 4 + 1))
                sp.wait_ge(hb_ready, n * NCH + (NCH + CX))
                sp.sem_inc(passed["sp"], 1)

                def load_d(j, s):
                    sp.wait_ge(glo_done, n * NCH + j * 4 + (s + 1))
                    sp.dma_start(gl[s % 2].rearrange("p (y f) -> p y f", y=ROWS),
                                 g_dram[:, bass.ds((j * 4 + s) * ROWS, ROWS), :]).then_inc(g_in[s % 2], 16)
                    load_x(n, 1, j * 4 + s, s)

                def store_y(j, s):
                    sp.wait_ge(x_used, n * XQ + j * 4 + (s + 1 + NCH + CX))
                    sp.sem_inc(passed["sp"], 1)
                    sp.dma_start(y_dram[:, :, bass.ds((j * 4 + s) * CHUNK, CHUNK)].rearrange("h p x -> p h x"),
                                 yst[s % 2][:]).then_inc(y_out[s % 2], 16)

                def load_onehot(j):
                    sp.dma_start(onehot[:, bass.ds(j * (P // J4), P // J4), :],
                                 t["onehot"][:, bass.ds(j * (P // J4), P // J4), :]).then_inc(oh_in, 16)

                load_d(0, 0)
                load_d(0, 1)
                with sp.Fori(0, J4 - 1) as j:
                    for s in range(4):
                        load_d(j + (s + 2) // 4, (s + 2) % 4)
                        store_y(j, s)
                    load_onehot(j)
                load_onehot(J4 - 1)
                for s in range(4):
                    if s < 2:
                        load_d(J4 - 1, s + 2)
                    store_y(J4 - 1, s)
                for s in range(2):
                    sp.wait_ge(y_out[s], n * YI + (YI // 2 + 16))

                def load_y(j, s):
                    sp.wait_ge(x_used, n * XQ + j * 4 + (s + 1 + 2 * NCH))
                    sp.sem_inc(passed["sp"], 1)
                    sp.dma_start(xr[s][:], y_dram[:, :, bass.ds((j * 4 + s) * CHUNK, CHUNK)].rearrange("h p x -> p h x"))\
                        .then_inc(x_in[s], 16)

                def store_out(j, s):
                    sp.wait_ge(x_used, n * XQ + j * 4 + (s + 1 + 2 * NCH + CX))
                    sp.dma_start(out_d[bass.ds(n, 1), :, :, bass.ds((j * 4 + s) * CHUNK, CHUNK)]
                                 .rearrange("n h p x -> p (n h) x"), yst[s % 2][:]).then_inc(y_out[s % 2], 16)

                for s in range(4):
                    load_y(0, s)
                sp.wait_ge(l_dve, n * LD + LD)
                sp.wait_ge(l_act, n * LA + LA)
                sp.dma_start(e_dram.rearrange("m y x -> y m x"), enh_hl.rearrange("p t m x -> p (t m) x"))\
                    .then_inc(e_out, 16)
                sp.wait_ge(e_out, n * 16 + 16)
                sp.dma_start(enh_in[0:2 * M, :], e_dram.rearrange("m y x -> m (y x)")).then_inc(e_in, 16)
                sp.dma_start(enh_in[2 * M:3 * M, :], e_dram[0:M].rearrange("m y x -> m (y x)")).then_inc(e_in, 16)
                with sp.Fori(0, J4 - 1) as j:
                    for s in range(4):
                        store_out(j, s)
                        load_y(j + 1, s)
                for s in range(4):
                    store_out(J4 - 1, s)
            for s in range(2):
                sp.wait_ge(y_out[s], 16 + B * YI)

        @block.gpsimd
        def _(pool):
            pool.sem_inc(glo_done, C2)
            pool.sem_inc(v_step, 1)
            with pool.Fori(0, B) as n:
                pool.wait_ge(mix_ready, n * NCH + CM)
                pool.sem_inc(passed["pool"], 1)
                for h in range(2):
                    nc.gpsimd.memset(hT[h][:, :, 0:PAD], 0.0).then_inc(pads, 1)
                    nc.gpsimd.memset(hT[h][:, :, PAD + P:YP], 0.0).then_inc(pads, 1)
                pool.wait_ge(fc_dve, n * FD + 32)
                pool.sem_inc(passed["pool"], 1)
                with pool.Fori(0, NV // 2) as c:
                    pool.wait_ge(v_step, n * (3 * NV) + c * 6 + 1)
                    for i in range(2):
                        pool.dma_start(vbase[i][:], t["taps"][:, bass.ds((c * 2 + i) * VCH, VCH), :, :])\
                            .then_inc(v_in[i], 16)
                    for i in range(2):
                        pool.wait_ge(v_in[i], n * (16 * NV // 2) + c * 16 + 16)
                        pool.wait_ge(v_step, n * (3 * NV) + c * 6 + (3 * i + 1))
                        nc.gpsimd.tensor_tensor(
                            vsum[:], vbase[i][:],
                            shifts[:].unsqueeze(1).to_broadcast([P, VCH, TSLOTS, PERIOD]),
                            ALU.add).then_inc(v_step, 1)
                        pool.wait_ge(t_ready, n * P + c * (2 * VCH) + (i * VCH + CV - VCH))
                        pool.wait_ge(v_step, n * (3 * NV) + c * 6 + (3 * i + 2))
                        pool.sem_inc(passed["pool"], 1)
                        nc.gpsimd.tensor_copy(vhl[i][0][:], vsum[:]).then_inc(v_step, 1)
                        pool.wait_ge(v_step, n * (3 * NV) + c * 6 + (3 * i + 3))
                        nc.gpsimd.tensor_tensor(vhl[i][1][:], vsum[:], vhl[i][0][:], ALU.subtract).then_inc(v_step, 1)
                with pool.Fori(0, J4) as j:
                    for s in range(4):
                        pool.wait_ge(gh_done, n * NCH + j * 4 + (s + 1))
                        nc.gpsimd.tensor_tensor(glo[s % 2], gl[s % 2], gh[s % 2], ALU.subtract).then_inc(glo_done, 1)

        @block.scalar
        def _(act):
            for s in range(4):
                act.sem_inc(g_out[s], 16)
            for s in range(2):
                act.sem_inc(y_out[s], 16)
            act.sem_inc(ha_out, C2)
            act.sem_inc(conv_out, C2)
            act.wait_ge(consts_in, 16 * (len(names) + 1))
            nc.scalar.copy(b1h[:, :], b1row[:, :]).then_inc(setup, 1)
            nc.scalar.copy(wo16[:, :], k["woT"][:]).then_inc(setup, 1)
            with act.Fori(0, B) as n:
                act.wait_ge(pads, n * 4 + 4)
                with act.Fori(0, J2) as j:
                    for s in range(2):
                        act.wait_ge(ha_ready, n * NCH + j * 2 + (s + 1))
                        act.wait_ge(ha_out, n * NCH + j * 2 + (s + 1))
                        nc.scalar.activation(relu_out[:, s, :], ps[s][:, :], ACT.Relu, bias=k["b1col"][:, 1:2],
                                             accum_out=relu_hi[:, bass.ds(j * 2 + s, 1)]).then_inc(ha_out, 1)
                        act.wait_ge(hb_ready, n * NCH + j * 2 + (s + 1 + CX))
                        nc.scalar.activation(
                            hT[0][:, :, bass.ds((j * 2 + s) * ROWS + PAD, ROWS)].rearrange("p c y -> p y c"),
                            ps[2 + s][:, :].rearrange("p (y c) -> p y c", y=ROWS), ACT.Relu).then_inc(hi_done, 1)
                act.wait_ge(fc_dve, n * FD + 25)
                nc.scalar.activation(offt[:, :], off[:, :], ACT.Tanh).then_inc(fc_act, 1)
                act.wait_ge(fc_act, n * FA + 1)
                nc.scalar.activation(th[:, 0:3], offt[:, 0:3], ACT.Tanh, scale=0.5).then_inc(fc_act, 1)
                nc.scalar.activation(th[:, 3:6], offt[:, 3:6], ACT.Tanh).then_inc(fc_act, 1)
                with act.Fori(0, P // 4) as j:
                    for s in range(4):
                        act.wait_ge(conv_ready, n * P + j * 4 + (s + 1 + C2))
                        act.wait_ge(g_out[s], n * (16 * P // 4) + j * 16 + 16)
                        nc.scalar.copy(gst[s], ps[s % 2][:, 0:OUT3]).then_inc(conv_out, 1)
                with act.Fori(0, J4) as j:
                    for s in range(4):
                        g = s % 2
                        act.wait_ge(g_in[g], n * (16 * J2) + j * 32 + 16 * (s // 2 + 1))
                        act.wait_ge(pw_ready, n * NCH + j * 4 + (s + 1))
                        nc.scalar.copy(gh[g], gl[g]).then_inc(gh_done, 1)
                        act.wait_ge(x_in[s], n * XI + j * 16 + (XI1 + 16))
                        for h in range(KH):
                            nc.scalar.activation(xr[s][:, h, :], xr[s][:, h, :], ACT.Identity,
                                                 bias=k["pwb"][:, h:h + 1]).then_inc(xb_done, 1)
                def flat(ap):
                    return ap.rearrange("p m c -> p (m c)")

                for g in range(0, 8, 2):
                    act.wait_ge(l_pe, n * LP + g + 1)
                    nc.scalar.copy(flat(f1[:, 2 * g:2 * g + 2, :]), ps[g % 4][:, :]).then_inc(l_act, 1)
                for g in range(4):
                    act.wait_ge(l_pe, n * LP + (9 + 2 * g))
                    nc.scalar.copy(flat(f2[:, 0, 4 * g:4 * g + 4, :]), ps[4 + g % 2][:, :]).then_inc(l_act, 1)
                act.wait_ge(l_act, n * LA + 8)
                nc.scalar.activation(mag_a, flat(f2[:, 0, :, :]), ACT.Square).then_inc(l_act, 1)
                act.wait_ge(l_dve, n * LD + 10)
                nc.scalar.activation(mag_b, mag_a, ACT.Sqrt).then_inc(l_act, 1)
                for g in range(0, 8, 2):
                    act.wait_ge(l_pe, n * LP + (20 + g))
                    nc.scalar.copy(flat(f1[:, 2 * g:2 * g + 2, :]), ps[g % 4][:, :]).then_inc(l_act, 1)
                act.wait_ge(l_dve, n * LD + 11)
                for g in range(4):
                    act.wait_ge(l_pe, n * LP + (28 + g))
                    nc.scalar.copy(flat(enh_hl[:, 0, 4 * g:4 * g + 4, :]), ps[4 + g][:, :]).then_inc(l_act, 1)

        @block.vector
        def _(dve):
            V = nc.vector
            dve.sem_inc(x_used, CX)
            dve.sem_inc(lo_done, C2)
            dve.sem_inc(t_ready, CV)
            dve.sem_inc(xp_out, C2)
            V.memset(ones[:, :], 1.0).then_inc(setup, 1)
            V.memset(ones16[:, :], 1.0).then_inc(setup, 1)
            V.memset(hp[:, :], 0.0).then_inc(setup, 1)
            dve.wait_ge(setup, 5)
            V.tensor_tensor(b1l[:, :], b1row[:, :], b1h[:, :], ALU.subtract).then_inc(setup, 1)
            V.tensor_copy(wol[0:2 * M, :], wo16[0:2 * M, :]).then_inc(setup, 1)
            V.tensor_tensor(wol[2 * M:3 * M, :], k["woT"][2 * M:3 * M, :], wo16[2 * M:3 * M, :], ALU.subtract)\
                .then_inc(setup, 1)
            with dve.Fori(0, B) as n:
                with dve.Fori(0, J4) as j:
                    for s in range(4):
                        dve.wait_ge(x_in[s], n * XI + j * 16 + 16)
                        V.tensor_reduce(xs[:, :, bass.ds(j * 4 + s, 1)].rearrange("p h c -> p (h c)"), xr[s][:, :, :],
                                        AX.X, ALU.add).then_inc(x_used, 1)
                        dve.wait_ge(hi_done, n * NCH + j * 4 + (s + 1))
                        rows = bass.ds((j * 4 + s) * ROWS + PAD, ROWS)
                        V.scalar_tensor_tensor(
                            out=hT[1][:, :, rows].rearrange("p c y -> p y c"),
                            in0=ps[2 + s % 2][:, :].rearrange("p (y c) -> p y c", y=ROWS), scalar=0.0,
                            in1=hT[0][:, :, rows].rearrange("p c y -> p y c"),
                            op0=ALU.max, op1=ALU.subtract).then_inc(lo_done, 1)

                steps = [0]

                def fc(ins):
                    steps[0] += 1
                    ins.then_inc(fc_dve, 1)
                    dve.wait_ge(fc_dve, n * FD + steps[0])

                def fc_products(i):
                    dve.wait_ge(fc_pe, n * 6 + i)

                dve.wait_ge(x_used, n * XQ + (CX + NCH))
                fc(V.tensor_reduce(xsum[:, :], xs[:, :, :], AX.X, ALU.add))
                dve.wait_ge(ha_out, n * NCH + (NCH + C2))
                fc(V.tensor_reduce(g2[:, 1:2], relu_hi[:, :], AX.X, ALU.add))
                fc_products(2)
                fc(V.scalar_tensor_tensor(out=gap[:, :], in0=ps[5][:, 0:KH], scalar=1.0 / PIX, in1=k["b1col"][:],
                                          op0=ALU.mult, op1=ALU.add))
                fc_products(3)
                fc(V.tensor_tensor(hid_raw[:, :], ps[5][:, KH:KH + HID // P], k["fc1b"][:], ALU.add))
                fc(V.tensor_scalar(hid[:, :], hid_raw[:, :], 0.0, None, ALU.max))
                for i in range(HID // P):
                    fc(V.tensor_scalar(hidb[:, i, :], ones[:, :], hid[:, i:i + 1], None, ALU.mult))
                fc_products(4)
                fc(V.tensor_tensor(z[:, :], ps[6][:, 0:C], k["fc2bB"][:], ALU.add))
                fc(V.tensor_scalar(zm[:, :], z[:, :], SATURATED, None, ALU.min))
                fc(V.tensor_tensor(zd[:, :], zm[:, 0:P], k["ident"][:], ALU.mult))
                fc(V.tensor_reduce(zc[:, :], zd[:, :], AX.X, ALU.add))
                fc(V.tensor_scalar(gt[:, :], zm[:, :], zc[:, 0:1], None, ALU.is_gt))
                fc(V.tensor_scalar(eq[:, :], zm[:, :], zc[:, 0:1], None, ALU.is_equal))
                fc(V.tensor_tensor(eq[:, :], eq[:, :], k["lower"][:], ALU.mult))
                fc(V.tensor_tensor(gt[:, :], gt[:, :], eq[:, :], ALU.add))
                fc(V.tensor_reduce(rank[:, :], gt[:, :], AX.X, ALU.add))
                fc(V.tensor_scalar(mask[:, :], rank[:, :], float(P) - 0.5, None, ALU.is_lt))
                fc_products(1)
                fc(V.tensor_reduce(s1row[:, :], ps[4][0:1, :].rearrange("p (c y) -> p c y", y=ROWS), AX.X, ALU.add))
                fc_products(5)
                fc(V.tensor_scalar(g2s[:, 0:1], ps[5][:, 6:7], 1.0 / PIX, None, ALU.mult))
                fc(V.tensor_scalar(g2s[:, 1:2], g2[:, 1:2], 1.0 / PIX, None, ALU.mult))
                for i in range(KH):
                    fc(V.tensor_scalar(g2b[:, i, :], ones[:, :], g2s[:, i:i + 1], None, ALU.mult))
                fc_products(6)
                fc(V.tensor_tensor(off[:, :], ps[5][:, 8:14], k["offbB"][:], ALU.add))
                dve.wait_ge(fc_act, n * FA + FA)
                fc(V.tensor_scalar(s1p[:, :], th[:, 0:3], 0.5, 1.5, ALU.mult, ALU.add))
                fc(V.reciprocal(rs[:, :], s1p[:, :]))
                fc(V.tensor_tensor(rq[:, :], th[:, 3:6], rs[:, :], ALU.mult))
                at = 0
                for _, q in TAP_ROWS[0], TAP_ROWS[3], TAP_ROWS[5]:
                    rows_q = {3: 3, 2: 2, 1: 2}[q]
                    fc(V.tensor_copy(R[:, at:at + rows_q * q].rearrange("p (a q) -> p a q", q=q),
                                     rq[:, 0:q].unsqueeze(1).to_broadcast([P, rows_q, q])))
                    at += rows_q * q
                fc(V.tensor_tensor(shifts[:], R[:, :].unsqueeze(2).to_broadcast([P, TSLOTS, PERIOD]), k["istap"][:], ALU.mult))
                fc(V.tensor_scalar(sc[:, :], s1p[:, :], mask[:, 0:1], PW_SCALE, ALU.mult, ALU.mult))
                for q in range(3):
                    fc(V.tensor_scalar(pwm[:, q, :], k["pwT"][:, q, :], sc[:, q:q + 1], None, ALU.mult))
                fc(V.tensor_copy(pwh[:, :, :], pwm[:, :, :]))
                fc(V.tensor_tensor(pwl[:, :, :], pwm[:, :, :], pwh[:, :, :], ALU.subtract))
                assert steps[0] == FD, steps

                dve.sem_inc(passed["dve"], 1)
                with dve.Fori(0, NV // 2) as c:
                    for i in range(2):
                        dve.wait_ge(v_step, n * (3 * NV) + c * 6 + (3 * i + 4))
                        for ci in range(VCH):
                            u = ci % 2
                            dve.wait_ge(conv_ready, n * P + c * (2 * VCH) + (i * VCH + ci + 1))
                            for h in range(2):
                                ins = V.tensor_tensor(
                                    toep[u][h].rearrange("p (t a r) -> p t a r", t=TSLOTS, r=PERIOD),
                                    vhl[i][h][:, ci, :, :].unsqueeze(2).to_broadcast([P, TSLOTS, P // PERIOD, PERIOD]),
                                    k["band"][:].rearrange("p (a r) -> p a r", r=PERIOD).unsqueeze(1)
                                    .to_broadcast([P, TSLOTS, P // PERIOD, PERIOD]), ALU.mult)
                            ins.then_inc(t_ready, 1)

                def block_sum(j, s):
                    g = s % 2
                    dve.wait_ge(pw_ready, n * NCH + j * 4 + (s + 1 + C2))
                    dve.wait_ge(xb_done, n * (KH * NCH) + j * 8 + KH * (s + 1))
                    dve.wait_ge(y_out[g], n * YI + j * 32 + 16 * (s // 2 + 1))
                    dve.wait_ge(xp_ready, n * NCH + j * 4 + (s + 1))
                    for h in range(KH):
                        ins = V.scalar_tensor_tensor(out=yst[g][:, h, :], in0=ps[2 * g + h][:, :], scalar=1.0 / PW_SCALE,
                                                     in1=xr[s][:, h, :], op0=ALU.mult, op1=ALU.add)
                    ins.then_inc(x_used, 1)

                def project_out(j, s):
                    dve.wait_ge(xp_ready, n * NCH + j * 4 + (s + 1 + C2))
                    V.tensor_copy(xproj[:, :, bass.ds((j * 4 + s) * ROWS, ROWS)].rearrange("p m y -> p y m"),
                                  ps[4 + s % 2][:, 0:ROWS * M].rearrange("p (y m) -> p y m", y=ROWS)).then_inc(xp_out, 1)

                block_sum(0, 0)
                with dve.Fori(0, J4 - 1) as j:
                    for s in range(4):
                        block_sum(j + (s + 1) // 4, (s + 1) % 4)
                        project_out(j, s)
                for s in range(4):
                    if s < 3:
                        block_sum(J4 - 1, s + 1)
                    project_out(J4 - 1, s)

                done = [0]

                def flat(ap):
                    return ap.rearrange("p m c -> p (m c)")

                def st(ins):
                    done[0] += 1
                    ins.then_inc(l_dve, 1)

                def link(ins):
                    st(ins)
                    dve.wait_ge(l_dve, n * LD + done[0])

                for g in range(1, 8, 2):
                    dve.wait_ge(l_pe, n * LP + g + 1)
                    st(V.tensor_copy(flat(f1[:, 2 * g:2 * g + 2, :]), ps[g % 4][:, :]))
                for g in range(4):
                    dve.wait_ge(l_pe, n * LP + (10 + 2 * g))
                    link(V.tensor_copy(flat(f2[:, 1, 4 * g:4 * g + 4, :]), ps[6 + g % 2][:, :]))
                link(V.tensor_tensor(mag_b, flat(f2[:, 1, :, :]), flat(f2[:, 1, :, :]), ALU.mult))
                dve.wait_ge(l_act, n * LA + 9)
                link(V.tensor_tensor(mag_a, mag_a, mag_b, ALU.add))
                dve.wait_ge(l_act, n * LA + 10)
                link(V.tensor_reduce(mag[:, :], mag_b.rearrange("p (m u) -> p u m", m=M), AX.X, ALU.add))
                link(V.tensor_tensor(magm[:, :], mag[:, :], k["high16"][:], ALU.mult))
                link(V.tensor_copy(ms[:, :, 0], magm[:, :]))
                link(V.tensor_tensor(ms[:, :, 1], magm[:, :], ms[:, :, 0], ALU.subtract))
                dve.wait_ge(l_pe, n * LP + 17)
                link(V.tensor_copy(h2[:, :], ps[0][0:2, 0:NBINS]))
                dve.wait_ge(l_pe, n * LP + 18)
                link(V.tensor_copy(hp[:, 1:NBINS + 1], ps[1][0:1, 0:NBINS]))
                N = NBINS
                e, ra, rb_, rc = (bins[:, i, :] for i in range(4))
                es = e[:, 1:N + 1]
                a_, b_, c_, oh1 = bins[:, 4, 0:N], bins[:, 5, 0:N], bins[:, 6, 0:N], bins[:, 7, 0:N]
                p1, msk, key = ra[:, 0:N], rb_[:, 0:N], rc[:, 0:N]
                BIG = 1.0e30
                link(V.tensor_scalar(a_, hp[:, 0:N], 0.25, None, ALU.mult))
                link(V.scalar_tensor_tensor(out=b_, in0=hp[:, 1:N + 1], scalar=0.5, in1=a_, op0=ALU.mult, op1=ALU.add))
                link(V.scalar_tensor_tensor(out=es, in0=hp[:, 2:N + 2], scalar=0.25, in1=b_, op0=ALU.mult, op1=ALU.add))
                link(V.tensor_copy(e[:, 0:1], e[:, N:N + 1]))
                link(V.tensor_copy(e[:, N + 1:N + 2], e[:, 1:2]))
                link(V.tensor_reduce(pc[:, 0:1], es, AX.X, ALU.add))
                link(V.tensor_scalar(pc[:, 1:2], pc[:, 0:1], 1.0 / N, None, ALU.mult))
                link(V.tensor_scalar(p1, es, pc[:, 1:2], None, ALU.is_gt))
                link(V.tensor_tensor(a_, es, e[:, 0:N], ALU.is_gt))
                link(V.tensor_tensor(b_, es, e[:, 2:N + 2], ALU.is_gt))
                link(V.tensor_tensor(p1, p1, a_, ALU.mult))
                link(V.tensor_tensor(p1, p1, b_, ALU.mult))
                link(V.tensor_reduce(pc[:, 2:3], p1, AX.X, ALU.add))
                link(V.tensor_scalar(pc[:, 3:4], pc[:, 2:3], 0.5, None, ALU.is_lt))
                link(V.tensor_scalar(p1, p1, pc[:, 3:4], None, ALU.max))
                link(V.tensor_scalar(a_, p1, 1.0, BIG, ALU.subtract, ALU.mult))
                link(V.tensor_tensor(b_, p1, es, ALU.mult))
                link(V.tensor_tensor(msk, b_, a_, ALU.add))
                for i in range(2):
                    link(V.tensor_reduce(pc[:, 4 + i:5 + i], msk, AX.X, ALU.max))
                    link(V.tensor_scalar(a_, msk, pc[:, 4 + i:5 + i], None, ALU.is_equal))
                    link(V.scalar_tensor_tensor(out=key, in0=a_, scalar=-1000.0, in1=k["binrow"][:], op0=ALU.mult, op1=ALU.add))
                    link(V.tensor_reduce(pc[:, 6 + i:7 + i], key, AX.X, ALU.min))
                    link(V.tensor_scalar(oh1, key, pc[:, 6 + i:7 + i], None, ALU.is_equal))
                    link(V.tensor_tensor(c_, oh1, k["centers"][:], ALU.mult))
                    link(V.tensor_reduce(pc[:, 8 + i:9 + i], c_, AX.X, ALU.add))
                    if i == 0:
                        link(V.scalar_tensor_tensor(out=msk, in0=oh1, scalar=-2.0 * BIG, in1=msk, op0=ALU.mult, op1=ALU.add))
                link(V.tensor_scalar(pc[:, 10:11], pc[:, 2:3], 1.5, None, ALU.is_gt))
                link(V.tensor_scalar(pc[:, 11:12], pc[:, 10:11], -1.0, 1.0, ALU.mult, ALU.add))
                link(V.tensor_tensor(pc[:, 12:13], pc[:, 8:9], pc[:, 11:12], ALU.mult))
                link(V.scalar_tensor_tensor(out=pc[:, 9:10], in0=pc[:, 9:10], scalar=pc[:, 10:11], in1=pc[:, 12:13],
                                            op0=ALU.mult, op1=ALU.add))
                assert done[0] == 53, done
                dve.wait_ge(l_pe, n * LP + 19)
                link(V.tensor_copy(pkb[:, :], ps[2][:, 0:2]))
                for i in range(2):
                    link(V.tensor_scalar(gn[:, 2, :], k["theta"][:], pkb[:, i:i + 1], None, ALU.subtract))
                    link(V.scalar_tensor_tensor(out=gn[:, 3, :], in0=gn[:, 2, :], scalar=-1.0, in1=gn[:, 2, :],
                                                op0=ALU.mult, op1=ALU.max))
                    link(V.tensor_scalar(gn[:, 2, :], gn[:, 3, :], -1.0, float(np.float32(np.pi)), ALU.mult, ALU.add))
                    link(V.tensor_tensor(gn[:, 3, :], gn[:, 3, :], gn[:, 2, :], ALU.min))
                    link(V.tensor_scalar(gn[:, i, :], gn[:, 3, :], float(np.float32(np.radians(15.0))), None, ALU.is_le))
                link(V.tensor_tensor(gn[:, 2, :], gn[:, 0, :], gn[:, 1, :], ALU.max))
                link(V.tensor_tensor(gn[:, 3, :], gn[:, 2, :], k["gain_d"][:], ALU.mult))
                link(V.tensor_tensor(gain[:, :], gn[:, 3, :], k["gain_lo"][:], ALU.add))
                for r in range(2):
                    link(V.tensor_tensor(f2[:, r, :, :], f2[:, r, :, :], gain[:, :].unsqueeze(1).to_broadcast([P, M, P]),
                                         ALU.mult))
                for g in range(1, 8, 2):
                    dve.wait_ge(l_pe, n * LP + (20 + g))
                    st(V.tensor_copy(flat(f1[:, 2 * g:2 * g + 2, :]), ps[g % 4][:, :]))
                for g in range(4):
                    dve.wait_ge(l_act, n * LA + (15 + g))
                    st(V.tensor_tensor(flat(enh_hl[:, 1, 4 * g:4 * g + 4, :]), ps[4 + g][:, :],
                                       flat(enh_hl[:, 0, 4 * g:4 * g + 4, :]), ALU.subtract))
                assert done[0] == LD, done

                with dve.Fori(0, J4) as j:
                    for s in range(4):
                        g = s % 2
                        dve.wait_ge(mix_ready, n * NCH + j * 4 + (s + 1 + CM))
                        dve.wait_ge(x_in[s], n * XI + j * 16 + (2 * XI1 + 16))
                        dve.wait_ge(y_out[g], n * YI + j * 32 + (YI // 2 + 16 * (s // 2 + 1)))
                        for h in range(KH):
                            ins = V.tensor_tensor(yst[g][:, h, :], ps[2 * g + h][:, :], xr[s][:, h, :], ALU.add)
                        ins.then_inc(x_used, 1)

        @block.tensor
        def _(pe):
            T = nc.tensor
            pe.sem_inc(hb_ready, CX)
            pe.sem_inc(conv_ready, C2)
            pe.sem_inc(pw_ready, C2)
            pe.sem_inc(xp_ready, C2)
            pe.sem_inc(mix_ready, CM)
            pe.wait_ge(setup, 8)
            with pe.Fori(0, B) as n:
                pe.wait_ge(x_used, n * XQ + CX)
                pe.sem_inc(passed["pe"], 1)
                with pe.Fori(0, J4) as j:
                    for s in range(4):
                        g = s % 2
                        pe.wait_ge(x_in[s], n * XI + j * 16 + 16)
                        pe.wait_ge(ha_out, n * NCH + j * 4 + (s + 1))
                        for h in range(KH):
                            mm = T.matmul(ps[g][:, :], k["w1T"][:, h, P:C], xr[s][:, h, :], start=(h == 0), stop=(h == KH - 1))
                        mm.then_inc(ha_ready, 1)
                        pe.wait_ge(lo_done, n * NCH + j * 4 + (s + 1))
                        T.matmul(ps[2 + g][:, :], ones16[0:1, :], b1h[:, :], start=True, stop=False, skip_group_check=True)
                        T.matmul(ps[2 + g][:, :], ones16[0:1, :], b1l[:, :], start=False, stop=False, skip_group_check=True)
                        for r in range(ROWS):
                            for h in range(KH):
                                mm = T.matmul(ps[2 + g][:, r * P:(r + 1) * P], xr[s][:, h, r * P:(r + 1) * P],
                                              k["w1T"][:, h, 0:P], start=False, stop=(r == ROWS - 1 and h == KH - 1),
                                              skip_group_check=True)
                        mm.then_inc(hb_ready, 1)
                pe.wait_ge(lo_done, n * NCH + (NCH + C2))

                def pixel_sums(chunk, first, last):
                    for h in range(2):
                        return_mm = T.matmul(ps[4][0:1, :], ones16[:, 0:1], hT[h][:, :, bass.ds(chunk * ROWS + PAD, ROWS)],
                                             start=(first and h == 0), stop=(last and h == 1), skip_group_check=True)
                    return return_mm

                pixel_sums(0, True, False)
                with pe.Fori(1, NCH - 1) as c:
                    pixel_sums(c, False, False)
                pixel_sums(NCH - 1, False, True).then_inc(fc_pe, 1)
                pe.wait_ge(fc_dve, n * FD + 1)
                for o in range(KH):
                    for h in range(KH):
                        mm = T.matmul(ps[5][:, o:o + 1], k["w1T"][:, h, o * P:(o + 1) * P], xsum[:, h:h + 1],
                                      start=(h == 0), stop=(h == KH - 1))
                mm.then_inc(fc_pe, 1)
                pe.wait_ge(fc_dve, n * FD + 3)
                for o in range(HID // P):
                    for h in range(KH):
                        mm = T.matmul(ps[5][:, KH + o:KH + o + 1], k["fc1T"][:, h, o * P:(o + 1) * P], gap[:, h:h + 1],
                                      start=(h == 0), stop=(h == KH - 1))
                mm.then_inc(fc_pe, 1)
                pe.wait_ge(fc_dve, n * FD + 9)
                for i in range(HID // P):
                    mm = T.matmul(ps[6][:, 0:C], hidb[:, i, :], k["fc2T"][:, i, :], start=(i == 0), stop=(i == HID // P - 1))
                mm.then_inc(fc_pe, 1)
                pe.wait_ge(fc_dve, n * FD + 20)
                T.matmul(ps[5][:, 6:7], s1row[:, :], ones[0:1, 0:1], start=True, stop=True).then_inc(fc_pe, 1)
                pe.wait_ge(fc_dve, n * FD + 24)
                for h in range(KH):
                    mm = T.matmul(ps[5][:, 8:14], g2b[:, h, :], k["offT"][:, h, :], start=(h == 0), stop=(h == KH - 1))
                mm.then_inc(fc_pe, 1)

                with pe.Fori(0, P // 2) as j:
                    for u in range(2):
                        pe.wait_ge(t_ready, n * P + j * 2 + (u + 1 + CV))
                        pe.wait_ge(conv_out, n * P + j * 2 + (u + 1))
                        col = 0
                        for i, (dy, q) in enumerate(TAP_ROWS):
                            for hd, hw in ((0, 0), (0, 1), (1, 0)):
                                mm = T.matmul(ps[u][:, 0:q * P],
                                              hT[hd][:, bass.ds(j * 2 + u, 1), PAD + dy:PAD + dy + P].rearrange("p c y -> p (c y)"),
                                              toep[u][hw][:, col:col + q * P],
                                              start=(i == 0 and hd + hw == 0), stop=(i == len(TAP_ROWS) - 1 and hd == 1),
                                              skip_group_check=True)
                            col += q * P
                        mm.then_inc(conv_ready, 1)

                def pointwise(j, s):
                    g = s % 2
                    pe.wait_ge(glo_done, n * NCH + j * 4 + (s + 1 + C2))
                    pe.wait_ge(x_used, n * XQ + j * 4 + (s + CX + NCH - 1))
                    parts = [a.rearrange("p (y q x) -> p q y x", y=ROWS, q=3) for a in (gh[g], glo[g])]
                    for h in range(KH):
                        for i, (w, d) in enumerate(((pwh, 0), (pwl, 0), (pwh, 1))):
                            for q in range(3):
                                mm = T.matmul(ps[2 * g + h][:, :], w[:, q, h * P:(h + 1) * P], parts[d][:, q, :, :],
                                              start=(i == 0 and q == 0), stop=(i == 2 and q == 2))
                    mm.then_inc(pw_ready, 1)

                def project(j, s):
                    g = s % 2
                    pe.wait_ge(x_used, n * XQ + j * 4 + (s + 1 + CX + NCH))
                    pe.wait_ge(xp_out, n * NCH + j * 4 + (s + 1))
                    for r in range(ROWS):
                        for h in range(KH):
                            mm = T.matmul(ps[4 + g][:, r * M:(r + 1) * M], yst[g][:, h, r * P:(r + 1) * P], k["winT"][:, h, :],
                                          start=(h == 0), stop=(h == KH - 1))
                    mm.then_inc(xp_ready, 1)

                pe.wait_ge(fc_dve, n * FD + FD)
                pointwise(0, 0)
                with pe.Fori(0, J4 - 1) as j:
                    for s in range(4):
                        pointwise(j + (s + 1) // 4, (s + 1) % 4)
                        project(j, s)
                for s in range(4):
                    if s < 3:
                        pointwise(J4 - 1, s + 1)
                    project(J4 - 1, s)

                pe.wait_ge(xp_out, n * NCH + (NCH + C2))

                def evacuated(g):
                    return (l_dve, LD, g // 2 + 1) if g % 2 else (l_act, LA, g // 2 + 1)

                for g in range(8):
                    if g >= 4:
                        sm, per, cnt = evacuated(g - 4)
                        pe.wait_ge(sm, n * per + cnt)
                    for i in range(2):
                        mm = T.matmul(ps[g % 4][:, i * 2 * P:(i + 1) * 2 * P], xproj[:, 2 * g + i, :], k["dft_fwd"][:],
                                      start=True, stop=True)
                    mm.then_inc(l_pe, 1)
                pe.wait_ge(l_act, n * LA + 4)
                pe.wait_ge(l_dve, n * LD + 4)
                for g in range(4):
                    re, im = (f1[:, 4 * g:4 * g + 4, r * P:(r + 1) * P] for r in range(2))
                    if g >= 2:
                        pe.wait_ge(l_act, n * LA + (5 + g - 2))
                    T.matmul(ps[4 + g % 2][:, :], k["dft_c"][:], re, start=True, stop=False)
                    T.matmul(ps[4 + g % 2][:, :], k["dft_s"][:], im, start=False, stop=True).then_inc(l_pe, 1)
                    if g >= 2:
                        pe.wait_ge(l_dve, n * LD + (5 + g - 2))
                    T.matmul(ps[6 + g % 2][:, :], k["dft_c"][:], im, start=True, stop=False)
                    T.matmul(ps[6 + g % 2][:, :], k["dft_ns"][:], re, start=False, stop=True).then_inc(l_pe, 1)
                pe.wait_ge(l_dve, n * LD + 14)
                pe.wait_ge(oh_in, n * (16 * J4) + 16 * J4)
                for u in range(P):
                    mm = T.matmul(ps[0][0:2, 0:NBINS], ms[:, u, :], onehot[:, u, :], start=(u == 0), stop=(u == P - 1))
                mm.then_inc(l_pe, 1)
                pe.wait_ge(l_dve, n * LD + 15)
                pe.sem_inc(passed["pe"], 1)
                T.matmul(ps[1][0:1, 0:NBINS], ones[0:2, 0:1], h2[:, :], start=True, stop=True).then_inc(l_pe, 1)
                pe.wait_ge(l_dve, n * LD + 53)
                T.matmul(ps[2][:, 0:2], ones[0:1, :], pc[:, 8:10], start=True, stop=True).then_inc(l_pe, 1)
                pe.wait_ge(l_dve, n * LD + 69)
                for g in range(8):
                    if g >= 4:
                        sm, per, cnt = (l_dve, LD, 70 + (g - 4) // 2) if g % 2 else (l_act, LA, 11 + (g - 4) // 2)
                        pe.wait_ge(sm, n * per + cnt)
                    for i in range(2):
                        m = 2 * g + i
                        T.matmul(ps[g % 4][:, i * 2 * P:(i + 1) * 2 * P], f2[:, 0, m, :], k["inv_cs"][:], start=True, stop=False)
                        mm = T.matmul(ps[g % 4][:, i * 2 * P:(i + 1) * 2 * P], f2[:, 1, m, :], k["inv_nsc"][:], start=False, stop=True)
                    mm.then_inc(l_pe, 1)
                pe.wait_ge(l_act, n * LA + 14)
                pe.wait_ge(l_dve, n * LD + 73)
                for g in range(4):
                    for i in range(4):
                        m = 4 * g + i
                        T.matmul(ps[4 + g][:, i * P:(i + 1) * P], f1[:, m, 0:P], k["inv_c"][:], start=True, stop=False)
                        mm = T.matmul(ps[4 + g][:, i * P:(i + 1) * P], f1[:, m, P:2 * P], k["inv_ns"][:], start=False, stop=True)
                    mm.then_inc(l_pe, 1)

                pe.wait_ge(e_in, n * 32 + 32)
                pe.sem_inc(passed["pe"], 1)
                with pe.Fori(0, J4) as j:
                    for s in range(4):
                        g = s % 2
                        pe.wait_ge(x_used, n * XQ + j * 4 + (s + CX + 2 * NCH - 1))
                        for h in range(KH):
                            mm = T.matmul(ps[2 * g + h][:, :], wol[:, h * P:(h + 1) * P],
                                          enh_in[:, bass.ds((j * 4 + s) * CHUNK, CHUNK)], start=True, stop=True)
                        mm.then_inc(mix_ready, 1)


def geometry():
    f = np.float32
    pi = f(np.pi)
    dy, dx = np.meshgrid(np.arange(-P // 2, P // 2, dtype=f), np.arange(-P // 2, P // 2, dtype=f), indexing="ij")
    angle = np.arctan2(dy.astype(np.float64), dx)
    theta = (angle.astype(f) + pi).astype(f)
    high = np.sqrt(dy * dy + dx * dx) > f(0.3 * (P // 2))
    step = (np.arange(NBINS, dtype=f) / f(NBINS)).astype(f)
    edges = np.concatenate([pi * step, [pi]]).astype(f)
    folded = np.mod((angle + np.pi).astype(f), pi)
    bins = np.clip(np.searchsorted(edges, folded.reshape(-1), side="left") - 1, 0, NBINS - 1).reshape(P, P)
    order = (np.arange(P) + P // 2) % P
    theta, high, bins = (a[np.ix_(order, order)] for a in (theta, high, bins))
    onehot = (bins[:, :, None] == np.arange(NBINS)).astype(np.float16)
    lo = np.where(high, f(0.8), f(1.0)).astype(f)
    hi = np.where(high, f(1.2), f(1.0)).astype(f)
    return {"theta": theta, "gain_lo": lo, "gain_d": (hi - lo).astype(f), "high16": high.astype(f) / f(M),
            "onehot": onehot, "binrow": np.arange(NBINS, dtype=f)[None],
            "centers": ((edges[:-1] + edges[1:]) * f(0.5)).astype(f)[None]}


def tables():
    g = np.arange(P)
    a = 2 * np.pi * np.outer(g, g) / P
    c, s = np.cos(a), np.sin(a)
    out = {"dft_fwd": np.concatenate([c, -s], 1) / P, "dft_c": c, "dft_s": s, "dft_ns": -s,
           "inv_cs": np.concatenate([c, s], 1), "inv_nsc": np.concatenate([-s, c], 1), "inv_c": c / P, "inv_ns": -s / P,
           "ident": np.eye(P), "lower": (np.arange(C)[None, :] < g[:, None])}
    out = {name: np.ascontiguousarray(v, dtype=np.float32) for name, v in out.items()}
    out["band"] = (np.abs(g[:, None] - g[None, :]) <= PAD).astype(np.float16)
    out["istap"] = tap_rows([np.ones((P, 1, size, size), np.float32) for size in (7, 5, 3)])[:, 0]
    out.update(geometry())
    return out


def halves(a):
    return np.ascontiguousarray(np.swapaxes(a.reshape((-1, P) + a.shape[1:]), 0, 1))


def tap_rows(dws):
    padded = []
    for dw in dws:
        size = dw.shape[-1]
        full = np.zeros((P, 2 * PAD + 1, PERIOD), np.float32)
        m = PAD - size // 2
        full[:, m:m + size, m:m + size] = dw[:P, 0]
        padded.append(full)
    rows = np.stack([padded[q][:, PAD + dy] for dy, kinds in TAP_ROWS for q in range(kinds)], 1)
    index = (np.arange(P)[:, None] - np.arange(PERIOD)[None, :] + PAD) % PERIOD
    return np.ascontiguousarray(np.moveaxis(rows[:, :, index], 2, 0))


def kernel(**inputs):
    import concourse.bacc as bacc
    from concourse.bass_utils import run_bass_kernel_spmd

    a = {name: np.asarray(v) for name, v in inputs.items()}
    L0 = "L0_conv_"
    order = [4, 2, 0, 5, 3, 1]
    pw = a[L0 + "pw_w"][:, :3 * P].reshape(C, 3, P)[:, ::-1]
    arrays = {
        "x": a["x"].reshape(B, KH, P, PIX),
        "w1T": halves(a[L0 + "pw1_w"].T), "b1col": halves(a[L0 + "pw1_b"]),
        "b1row": np.tile(a[L0 + "pw1_b"][:P], ROWS)[None],
        "fc1T": halves(a[L0 + "fc1_w"].T), "fc1b": halves(a[L0 + "fc1_b"]),
        "fc2T": halves(a[L0 + "fc2_w"].T), "fc2bB": np.tile(a[L0 + "fc2_b"][None], (P, 1)),
        "offT": halves(a[L0 + "off_w"][order].T), "offbB": np.tile(a[L0 + "off_b"][order][None], (P, 1)),
        "pwT": np.transpose(pw, (2, 1, 0)), "pwb": halves(a[L0 + "pw_b"]),
        "winT": halves(a["L1_conv_w_in"].T), "woT": np.tile(a["L1_conv_w_out"].T, (3, 1)),
        "taps": tap_rows([a[L0 + "dw7"], a[L0 + "dw5"], a[L0 + "dw3"]]),
        **tables(),
    }
    arrays = {name: np.ascontiguousarray(v) for name, v in arrays.items()}
    nc = bacc.Bacc("TRN2", target_bir_lowering=False, num_devices=1)
    t = {name: nc.dram_tensor("in_" + name, v.shape, mybir.dt.from_np(v.dtype), kind="ExternalInput").ap()
         for name, v in arrays.items()}
    t["out"] = nc.dram_tensor("out", (B, KH, P, PIX), F32, kind="ExternalOutput").ap()
    build(nc, t)
    r = run_bass_kernel_spmd(nc, [{"in_" + name: v for name, v in arrays.items()}], core_ids=[0])
    return r.results[0]["out"].reshape(B, C, P, P)
```

```python
from contextlib import ExitStack

import numpy as np

import concourse.bass as bass
from concourse import mybir

F32 = mybir.dt.float32
F16 = mybir.dt.float16
ALU = mybir.AluOpType
ACT = mybir.ActivationFunctionType
AX = mybir.AxisListType

P = 128
B, C = 8, 256
KH = C // P
PIX = P * P
ROWS = 4
CHUNK = ROWS * P
NCH = P // ROWS
XSLOTS = 4
PAD = 3
YP = P + 2 * PAD
TAP_ROWS = [(0, 3), (-1, 3), (1, 3), (-2, 2), (2, 2), (-3, 1), (3, 1)]
TSLOTS = sum(k for _, k in TAP_ROWS)
TCOLS = TSLOTS * P
PERIOD = 8
VCH = 4
CR = 4
NV = P // VCH
HID = 2 * C
M = 16
NBINS = 180
OUT3 = 3 * P
OHU = 16
NOH = P // OHU
PW_SCALE = 64.0
SATURATED = 16.63553

XQ = 3 * NCH
FD, FA = 38, 3
LP, LA, LD = 30, 18, 75


def build(nc, t):
    with ExitStack() as ctx:
        def sb(name, shape, dt=F32):
            return ctx.enter_context(nc.sbuf_tensor(name, shape, dt))

        def sem(name):
            return ctx.enter_context(nc.semaphore(name))

        names = ["w1T", "b1col", "fc1b", "fc2bB", "offT", "offbB", "pwT", "pwb", "winT",
                 "dft_fwd", "dft_c", "dft_s", "dft_ns", "inv_cs", "inv_nsc", "inv_c", "inv_ns",
                 "ident", "lower", "theta", "gain_lo", "gain_d", "high16", "band", "istap", "binrow", "centers"]
        k = {}
        for name in names:
            src = t[name]
            k[name] = sb("k_" + name, list(src.shape), F16 if name == "band" else F32)
        b1h = sb("b1h", [1, CHUNK], F16)
        b1l = sb("b1l", [1, CHUNK], F16)
        ones16 = sb("ones16", [P, P], F16)
        ones = sb("ones", [P, P])
        wo16 = sb("wo16", [3 * M, C], F16)
        wol = sb("wol", [3 * M, C], F16)

        zeros16 = sb("zeros16", [1, NBINS], F16)

        arena = sb("arena", [P, 2 * P * YP], F16)
        hT = [arena[:, i * P * YP:(i + 1) * P * YP].rearrange("p (c y) -> p c y", y=YP) for i in range(2)]

        work2 = sb("work2", [P, 2 * 2 * TCOLS + 4 * OUT3 * 2], F16)
        gst0 = 4 * TCOLS
        gst = [work2[:, gst0 + 2 * OUT3 * s:gst0 + 2 * OUT3 * (s + 1)].bitcast(F32) for s in range(4)]
        MP = M * P
        f1 = work2[:, 0:4 * MP].bitcast(F32).rearrange("p (m c) -> p m c", m=M)
        mag_a = work2[:, 0:2 * MP].bitcast(F32)
        mag_b = work2[:, 2 * MP:4 * MP].bitcast(F32)
        gn = work2[:, 0:8 * P].bitcast(F32).rearrange("p (i u) -> p i u", i=4)
        bins = work2[0:1, 4 * MP:4 * MP + 14 * (NBINS + 2)].bitcast(F32).rearrange("p (i b) -> p i b", i=7)
        b1row = work2[0:1, 0:2 * CHUNK].bitcast(F32)
        woT = work2[0:3 * M, 2 * CHUNK:2 * CHUNK + 2 * C].bitcast(F32)

        G = ROWS * OUT3
        work3 = sb("work3", [P, 8 * G], F16)
        gl = [work3[:, 2 * G * g:2 * G * (g + 1)].bitcast(F32) for g in range(2)]
        gh = [work3[:, 4 * G + G * g:4 * G + G * (g + 1)] for g in range(2)]
        glo = [work3[:, 6 * G + G * g:6 * G + G * (g + 1)] for g in range(2)]
        f2 = work3[:, 0:4 * MP].bitcast(F32).rearrange("p (r m u) -> p r m u", r=2, m=M)
        toep = [[(work2, work3)[u // 2][:, (2 * (u % 2) + h) * TCOLS:(2 * (u % 2) + h + 1) * TCOLS] for h in range(2)]
                for u in range(CR)]
        FC = 2 * KH * HID
        fc1T = work3[:, 4 * MP:4 * MP + FC].bitcast(F32).rearrange("p (h o) -> p h o", h=KH)
        fc2T = work3[:, 4 * MP + FC:4 * MP + 2 * FC].bitcast(F32).rearrange("p (h o) -> p h o", h=HID // P)
        at = [0]

        def temp(*shape):
            size = int(np.prod(shape))
            a = work3[:, at[0]:at[0] + 2 * size].bitcast(F32)
            at[0] += 2 * size
            return a.rearrange("p (a b) -> p a b", a=shape[0]) if len(shape) == 2 else a

        hidb, g2b, pwm = temp(HID // P, P), temp(KH, P), temp(3, C)
        z, zm, gt, eq, zd = temp(C), temp(C), temp(C), temp(C), temp(P)
        assert at[0] <= 4 * MP

        work4 = sb("work4", [P, 2 * MP], F16)
        xproj = work4[:, :].bitcast(F32).rearrange("p (m y) -> p m y", m=M)
        enh_hl = work4[:, :].rearrange("p (t m x) -> p t m x", t=2, m=M)
        onehot = [sb(f"onehot{i}", [P, OHU, NBINS], F16) for i in range(2)]
        enh_in = [sb(f"enh_in{i}", [3 * M, 2 * CHUNK], F16) for i in range(2)]

        vbase = [sb(f"vbase{i}", [P, VCH, TSLOTS, PERIOD]) for i in range(2)]
        vsum = sb("vsum", [P, VCH, TSLOTS, PERIOD])
        vhl = [[sb(f"v{'hl'[h]}{i}", [P, VCH, TSLOTS, PERIOD], F16) for h in range(2)] for i in range(2)]
        xr = [sb(f"xr{s}", [P, KH, CHUNK]) for s in range(XSLOTS)]
        yst = [sb(f"yst{s}", [P, KH, CHUNK]) for s in range(2)]
        relu_out = sb("relu_out", [P, 2, CHUNK], F16)
        xs = sb("xs", [P, KH, NCH])
        relu_hi = sb("relu_hi", [P, NCH])
        xsum = sb("xsum", [P, KH])
        gap = sb("gap", [P, KH])
        hid_raw = sb("hid_raw", [P, HID // P])
        hid = sb("hid", [P, HID // P])
        zc = sb("zc", [P, 1])
        rank = sb("rank", [P, 1])
        mask = sb("mask", [P, 1])
        s1row = sb("s1row", [1, P])
        g2 = sb("g2", [P, KH])
        g2s = sb("g2s", [P, KH])
        off = sb("off", [P, 6])
        offt = sb("offt", [P, 6])
        th = sb("th", [P, 6])
        s1p = sb("s1p", [P, 3])
        rs = sb("rs", [P, 3])
        rq = sb("rq", [P, 3])
        R = sb("R", [P, TSLOTS])
        shifts = sb("shifts", [P, TSLOTS, PERIOD])
        sc = sb("sc", [P, 3])
        pwh = sb("pwh", [P, 3, C], F16)
        pwl = sb("pwl", [P, 3, C], F16)
        mag = sb("mag", [P, P])
        magm = sb("magm", [P, P])
        ms = [sb(f"ms{i}", [P, OHU, 2], F16) for i in range(2)]
        h2 = sb("h2", [2, NBINS])
        hp = sb("hp", [1, NBINS + 2])
        pc = sb("pc", [1, 16])
        pkb = sb("pkb", [P, 2])
        gain = sb("gain", [P, P])

        ps = [ctx.enter_context(nc.psum_tensor(f"ps{i}", [P, 512], F32)) for i in range(8)]

        g_dram = nc.dram_tensor("conv_out", [P, P, OUT3], F32, kind="Internal").ap()
        y_dram = nc.dram_tensor("block_out", [KH, P, PIX], F32, kind="Internal").ap()
        e_dram = nc.dram_tensor("enhanced", [2 * M, P, P], F16, kind="Internal").ap()
        x_in_d, out_d = t["x"], t["out"]

        consts_in = sem("consts_in")
        setup = sem("setup")
        x_in = [sem(f"x_in{s}") for s in range(XSLOTS)]
        x_used = sem("x_used")
        ha_ready, ha_out = sem("ha_ready"), sem("ha_out")
        hb_ready, hi_done, lo_done = sem("hb_ready"), sem("hi_done"), sem("lo_done")
        fc_pe, fc_act, fc_dve = sem("fc_pe"), sem("fc_act"), sem("fc_dve")
        v_in = [sem(f"v_in{i}") for i in range(2)]
        v_step = sem("v_step")
        t_ready = sem("t_ready")
        conv_ready, conv_out = sem("conv_ready"), sem("conv_out")
        g_out = [sem(f"g_out{s}") for s in range(4)]
        g_in = [sem(f"g_in{s}") for s in range(2)]
        gh_done, glo_done = sem("gh_done"), sem("glo_done")
        xb_done, pw_ready = sem("xb_done"), sem("pw_ready")
        y_out = [sem(f"y_out{s}") for s in range(2)]
        xp_ready, xp_out = sem("xp_ready"), sem("xp_out")
        oh_in = [sem(f"oh_in{i}") for i in range(2)]
        ms_done, hist_done = sem("ms_done"), sem("hist_done")
        fcw_in = sem("fcw_in")
        l_pe, l_act, l_dve = sem("l_pe"), sem("l_act"), sem("l_dve")
        e_out, e_in = sem("e_out"), [sem(f"e_in{i}") for i in range(2)]
        mix_ready, mix_out = sem("mix_ready"), sem("mix_out")
        passed = {e: sem("passed_" + e) for e in ("sp", "pool", "dve", "pe")}
        SETUP = 13
        CX, C2, CV, CS = XSLOTS, 2, 2 * VCH, 6

        XI = 16 * XQ // XSLOTS
        XI1 = 16 * NCH // XSLOTS
        YI = 16 * NCH
        J4 = NCH // 4
        VS = 3 * NV

        block = ctx.enter_context(nc.Block())

        @block.sync
        def _(sp):
            for name in names:
                sp.dma_start(k[name][:], t[name]).then_inc(consts_in, 16)
            sp.dma_start(b1row, t["b1row"]).then_inc(consts_in, 16)
            sp.dma_start(woT, t["woT"]).then_inc(consts_in, 16)

            def load_x(n, phase, j, s):
                sp.wait_ge(x_used, n * XQ + j * 4 + (phase * NCH + 1 + s))
                src = x_in_d[bass.ds(n, 1), :, :, bass.ds((j * 4 + s) * CHUNK, CHUNK)].rearrange("n h p x -> p (n h) x")
                sp.dma_start(xr[s][:], src).then_inc(x_in[s], 16)

            def phase_a(n, onehots):
                sp.wait_ge(pw_ready, n * NCH + C2)
                sp.sem_inc(passed["sp"], 1)
                sp.dma_start(fc1T, t["fc1T"]).then_inc(fcw_in, 16)
                sp.dma_start(fc2T, t["fc2T"]).then_inc(fcw_in, 16)
                with sp.Fori(0, J4 // 2) as jj:
                    for i in range(2):
                        if onehots:
                            load_onehot(n, jj, i)
                        for s in range(XSLOTS):
                            sp.wait_ge(hb_ready, n * NCH + jj * 8 + (4 * i + s + 1))
                            sp.sem_inc(passed["sp"], 1)
                            load_x(n, 0, jj * 2 + i, s)
                sp.wait_ge(hb_ready, n * NCH + (NCH + CX))
                sp.wait_ge(x_used, n * XQ + (CX + NCH))
                sp.sem_inc(passed["sp"], 1)

            def load_onehot(n, jj, i):
                sp.wait_ge(hist_done, (n - 1) * NOH + jj * 2 + (i + 1))
                sp.sem_inc(passed["sp"], 1)
                sp.dma_start(onehot[i][:], t["onehot"][:, bass.ds((jj * 2 + i) * OHU, OHU), :]).then_inc(oh_in[i], 16)

            def load_enhanced(j, i):
                px = bass.ds((j * 4 + 2 * i) * CHUNK, 2 * CHUNK)
                sp.dma_start(enh_in[i][0:2 * M, :], e_flat[:, px]).then_inc(e_in[i], 16)
                sp.dma_start(enh_in[i][2 * M:3 * M, :], e_flat[0:M, px]).then_inc(e_in[i], 16)

            def load_y(n, j, s):
                sp.wait_ge(x_used, n * XQ + j * 4 + (NCH + 1 + s))
                sp.sem_inc(passed["sp"], 1)
                sp.dma_start(xr[s][:], y_dram[:, :, bass.ds((j * 4 + s) * CHUNK, CHUNK)].rearrange("h p x -> p h x"))\
                    .then_inc(x_in[s], 16)

            def store_out(n, j, s):
                sp.wait_ge(x_used, n * XQ + j * 4 + (NCH + CX + 1 + s))
                sp.sem_inc(passed["sp"], 1)
                sp.dma_start(out_d[bass.ds(n - 1, 1), :, :, bass.ds((j * 4 + s) * CHUNK, CHUNK)]
                             .rearrange("n h p x -> p (n h) x"), yst[s % 2][:]).then_inc(y_out[s % 2], 16)

            def start_mix(n):
                for i in range(2):
                    sp.wait_ge(y_out[i], (n - 1) * YI + (YI // 2 + 16))
                    sp.sem_inc(passed["sp"], 1)
                for s in range(4):
                    load_y(n, 0, s)
                sp.wait_ge(l_dve, (n - 1) * LD + LD)
                sp.wait_ge(l_act, (n - 1) * LA + LA)
                sp.sem_inc(passed["sp"], 1)
                sp.dma_start(e_dram.rearrange("m y x -> y m x"), enh_hl.rearrange("p t m x -> p (t m) x"))\
                    .then_inc(e_out, 16)
                sp.wait_ge(e_out, (n - 1) * 16 + 16)
                sp.sem_inc(passed["sp"], 1)
                for i in range(2):
                    load_enhanced(0, i)

            def mix_group(n, j, s, more):
                store_out(n, j, s)
                if more:
                    load_y(n, j + 1, s)
                    if s % 2:
                        sp.wait_ge(mix_ready, (n - 1) * NCH + j * 4 + (s + 1))
                        sp.sem_inc(passed["sp"], 1)
                        load_enhanced(j + 1, s // 2)

            def conv_group(n, j, g):
                for s in range(4):
                    sp.wait_ge(conv_out, n * P + j * 16 + (4 * g + s + 1 + CR))
                    sp.dma_start(g_dram[bass.ds(j * 16 + (4 * g + s), 1)].rearrange("c y f -> (c y) f"), gst[s])\
                        .then_inc(g_out[s], 16)

            def phase_c(n, mix):
                if mix:
                    start_mix(n)
                with sp.Fori(0, J4 - 1) as j:
                    for g in range(4):
                        conv_group(n, j, g)
                        if mix:
                            mix_group(n, j, g, True)
                for g in range(4):
                    conv_group(n, J4 - 1, g)
                    if mix:
                        mix_group(n, J4 - 1, g, False)

            def phase_d(n):
                for s in range(4):
                    sp.wait_ge(g_out[s], n * (16 * P // 4) + 16 * (P // 4 + 1))
                sp.wait_ge(x_used, n * XQ + (CX + 2 * NCH))
                sp.sem_inc(passed["sp"], 1)

                def load_d(j, s):
                    sp.wait_ge(glo_done, n * NCH + j * 4 + (s + 1))
                    sp.sem_inc(passed["sp"], 1)
                    sp.dma_start(gl[s % 2].rearrange("p (y f) -> p y f", y=ROWS),
                                 g_dram[:, bass.ds((j * 4 + s) * ROWS, ROWS), :]).then_inc(g_in[s % 2], 16)
                    load_x(n, 2, j, s)

                def store_y(j, s):
                    sp.wait_ge(x_used, n * XQ + j * 4 + (s + 1 + 2 * NCH + CX))
                    sp.sem_inc(passed["sp"], 1)
                    sp.dma_start(y_dram[:, :, bass.ds((j * 4 + s) * CHUNK, CHUNK)].rearrange("h p x -> p h x"),
                                 yst[s % 2][:]).then_inc(y_out[s % 2], 16)

                load_d(0, 0)
                load_d(0, 1)
                with sp.Fori(0, J4 - 1) as j:
                    for s in range(4):
                        load_d(j + (s + 2) // 4, (s + 2) % 4)
                        store_y(j, s)
                for s in range(4):
                    if s < 2:
                        load_d(J4 - 1, s + 2)
                    store_y(J4 - 1, s)

            e_flat = e_dram.rearrange("m y x -> m (y x)")
            phase_a(0, False)
            for s in range(XSLOTS):
                sp.sem_inc(x_in[s], XI1)
            phase_c(0, False)
            phase_d(0)
            with sp.Fori(1, B) as n:
                phase_a(n, True)
                phase_c(n, True)
                phase_d(n)
            with sp.Fori(0, NOH // 2) as jj:
                for i in range(2):
                    load_onehot(B, jj, i)
            for s in range(XSLOTS):
                sp.sem_inc(x_in[s], XI1)
            start_mix(B)
            with sp.Fori(0, J4 - 1) as j:
                for g in range(4):
                    mix_group(B, j, g, True)
            for g in range(4):
                mix_group(B, J4 - 1, g, False)
            for s in range(2):
                sp.wait_ge(y_out[s], 16 + B * YI)

        @block.gpsimd
        def _(pool):
            PL = nc.gpsimd
            pool.sem_inc(glo_done, C2)
            pool.sem_inc(v_step, CS)
            for h in range(2):
                PL.memset(hT[h][:, :, 0:PAD], 0.0).then_inc(setup, 1)
                PL.memset(hT[h][:, :, PAD + P:YP], 0.0).then_inc(setup, 1)

            def load_taps(n, c, i):
                pool.wait_ge(v_step, n * VS + c * 6 + (3 * i + 1))
                pool.sem_inc(passed["pool"], 1)
                pool.dma_start(vbase[i][:], t["taps"][:, bass.ds((c * 2 + i) * VCH, VCH), :, :]).then_inc(v_in[i], 16)

            def split_taps(n, c, i, more=True):
                step = n * VS + c * 6 + 3 * i
                if more:
                    load_taps(n, c + i, 1 - i)
                pool.wait_ge(v_in[i], n * (16 * NV // 2) + c * 16 + 16)
                pool.wait_ge(v_step, step + CS)
                pool.sem_inc(passed["pool"], 1)
                PL.tensor_tensor(vsum[:], vbase[i][:], shifts[:].unsqueeze(1).to_broadcast([P, VCH, TSLOTS, PERIOD]),
                                 ALU.add).then_inc(v_step, 1)
                pool.wait_ge(t_ready, n * P + c * (2 * VCH) + (i * VCH + CV - VCH))
                pool.wait_ge(v_step, step + CS + 1)
                pool.sem_inc(passed["pool"], 1)
                PL.tensor_copy(vhl[i][0][:], vsum[:]).then_inc(v_step, 1)
                pool.wait_ge(v_step, step + CS + 2)
                PL.tensor_tensor(vhl[i][1][:], vsum[:], vhl[i][0][:], ALU.subtract).then_inc(v_step, 1)

            def add_block(n, j, s):
                pool.wait_ge(mix_out, (n - 1) * NCH + j * 4 + (s + 1 + C2))
                pool.wait_ge(x_in[s], n * XI + j * 16 + (XI1 + 16))
                PL.tensor_tensor(yst[s % 2][:], yst[s % 2][:], xr[s][:], ALU.add).then_inc(x_used, 1)

            def phase_c(n, mix):
                load_taps(n, 0, 0)
                pool.wait_ge(fc_dve, n * FD + 32)
                pool.sem_inc(passed["pool"], 1)
                split_taps(n, 0, 0)
                split_taps(n, 0, 1)
                with pool.Fori(0, J4 - 1) as j:
                    for i in range(2):
                        split_taps(n, j * 2 + (i + 1), 0)
                        split_taps(n, j * 2 + (i + 1), 1)
                        if mix:
                            add_block(n, j, 2 * i)
                            add_block(n, j, 2 * i + 1)
                split_taps(n, NV // 2 - 1, 0)
                split_taps(n, NV // 2 - 1, 1, more=False)
                if mix:
                    for s in range(4):
                        add_block(n, J4 - 1, s)

            def phase_d(n):
                with pool.Fori(0, J4) as j:
                    for s in range(4):
                        pool.wait_ge(gh_done, n * NCH + j * 4 + (s + 1))
                        PL.tensor_tensor(glo[s % 2], gl[s % 2], gh[s % 2], ALU.subtract).then_inc(glo_done, 1)

            phase_c(0, False)
            phase_d(0)
            with pool.Fori(1, B) as n:
                phase_c(n, True)
                phase_d(n)
            with pool.Fori(0, J4) as j:
                for s in range(4):
                    add_block(B, j, s)

        @block.scalar
        def _(act):
            S = nc.scalar
            for s in range(4):
                act.sem_inc(g_out[s], 16)
            for s in range(2):
                act.sem_inc(y_out[s], 16)
            act.sem_inc(ha_out, C2)
            act.sem_inc(conv_out, CR)
            act.sem_inc(mix_out, C2)
            act.wait_ge(consts_in, 16 * (len(names) + 2))
            S.copy(b1h[:, :], b1row).then_inc(setup, 1)
            S.copy(wo16[:, :], woT).then_inc(setup, 1)
            act.wait_ge(setup, SETUP)

            def flat(ap):
                return ap.rearrange("p m c -> p (m c)")

            def phase_a(n):
                with act.Fori(0, NCH // 2) as j:
                    for s in range(2):
                        act.wait_ge(ha_ready, n * NCH + j * 2 + (s + 1))
                        act.wait_ge(ha_out, n * NCH + j * 2 + (s + 1))
                        S.activation(relu_out[:, s, :], ps[s][:, :], ACT.Relu, bias=k["b1col"][:, 1:2],
                                     accum_out=relu_hi[:, bass.ds(j * 2 + s, 1)]).then_inc(ha_out, 1)
                        act.wait_ge(hb_ready, n * NCH + j * 2 + (s + 1 + CX))
                        S.activation(
                            hT[0][:, :, bass.ds((j * 2 + s) * ROWS + PAD, ROWS)].rearrange("p c y -> p y c"),
                            ps[2 + s][:, :].rearrange("p (y c) -> p y c", y=ROWS), ACT.Relu).then_inc(hi_done, 1)

            def phase_b(n):
                act.wait_ge(fc_dve, n * FD + 25)
                S.activation(offt[:, :], off[:, :], ACT.Tanh).then_inc(fc_act, 1)
                act.wait_ge(fc_act, n * FA + 1)
                S.activation(th[:, 0:3], offt[:, 0:3], ACT.Tanh, scale=0.5).then_inc(fc_act, 1)
                S.activation(th[:, 3:6], offt[:, 3:6], ACT.Tanh).then_inc(fc_act, 1)

            def mix_group(n, j, g):
                act.wait_ge(mix_ready, (n - 1) * NCH + j * 4 + (g + 1))
                act.wait_ge(y_out[g % 2], (n - 1) * YI + j * 32 + (YI // 2 + 16 * (g // 2 + 1)))
                for h in range(KH):
                    ins = S.copy(yst[g % 2][:, h, :], ps[4 + 2 * (g % 2) + h][:, :])
                ins.then_inc(mix_out, 1)

            def phase_c(n, mix):
                with act.Fori(0, J4) as j:
                    for g in range(4):
                        for s in range(4):
                            act.wait_ge(conv_ready, n * P + j * 16 + (4 * g + s + 1 + CR))
                            act.wait_ge(g_out[s], n * (16 * P // 4) + j * 64 + 16 * (g + 1))
                            S.copy(gst[s], ps[s][:, 0:OUT3]).then_inc(conv_out, 1)
                        if mix:
                            mix_group(n, j, g)

            def phase_d(n):
                with act.Fori(0, J4) as j:
                    for s in range(4):
                        g = s % 2
                        act.wait_ge(g_in[g], n * (16 * NCH // 2) + j * 32 + 16 * (s // 2 + 1))
                        act.wait_ge(pw_ready, n * NCH + j * 4 + (s + 1))
                        S.copy(gh[g], gl[g]).then_inc(gh_done, 1)
                        act.wait_ge(x_in[s], n * XI + j * 16 + (2 * XI1 + 16))
                        for h in range(KH):
                            S.activation(xr[s][:, h, :], xr[s][:, h, :], ACT.Identity,
                                         bias=k["pwb"][:, h:h + 1]).then_inc(xb_done, 1)

            def phase_e1(n):
                for g in range(0, 8, 2):
                    act.wait_ge(l_pe, n * LP + (g + 1))
                    S.copy(flat(f1[:, 2 * g:2 * g + 2, :]), ps[g % 4][:, :]).then_inc(l_act, 1)
                for g in range(4):
                    act.wait_ge(l_pe, n * LP + (9 + 2 * g))
                    S.copy(flat(f2[:, 0, 4 * g:4 * g + 4, :]), ps[4 + g % 2][:, :]).then_inc(l_act, 1)
                act.wait_ge(l_act, n * LA + 8)
                act.wait_ge(l_pe, n * LP + 16)
                S.activation(mag_a, flat(f2[:, 0, :, :]), ACT.Square).then_inc(l_act, 1)
                act.wait_ge(l_dve, n * LD + 10)
                S.activation(mag_b, mag_a, ACT.Sqrt).then_inc(l_act, 1)

            def phase_e2(n):
                for g in range(0, 8, 2):
                    act.wait_ge(l_pe, n * LP + (19 + g))
                    S.copy(flat(f1[:, 2 * g:2 * g + 2, :]), ps[g % 4][:, :]).then_inc(l_act, 1)
                for g in range(4):
                    act.wait_ge(l_pe, n * LP + (27 + g))
                    S.copy(flat(enh_hl[:, 0, 4 * g:4 * g + 4, :]), ps[4 + g % 3][:, :]).then_inc(l_act, 1)

            phase_a(0)
            phase_b(0)
            phase_c(0, False)
            phase_d(0)
            phase_e1(0)
            with act.Fori(1, B) as n:
                phase_a(n)
                phase_e2(n - 1)
                phase_b(n)
                phase_c(n, True)
                phase_d(n)
                phase_e1(n)
            phase_e2(B - 1)
            with act.Fori(0, J4) as j:
                for g in range(4):
                    mix_group(B, j, g)

        @block.vector
        def _(dve):
            V = nc.vector
            dve.sem_inc(x_used, CX)
            dve.sem_inc(lo_done, C2)
            dve.sem_inc(t_ready, CV)
            dve.sem_inc(xp_out, C2)
            V.memset(ones[:, :], 1.0).then_inc(setup, 1)
            V.memset(ones16[:, :], 1.0).then_inc(setup, 1)
            V.memset(zeros16[:, :], 0.0).then_inc(setup, 1)
            V.memset(hp[:, :], 0.0).then_inc(setup, 1)
            dve.wait_ge(setup, SETUP - 3)
            V.tensor_tensor(b1l[:, :], b1row, b1h[:, :], ALU.subtract).then_inc(setup, 1)
            V.tensor_copy(wol[0:2 * M, :], wo16[0:2 * M, :]).then_inc(setup, 1)
            V.tensor_tensor(wol[2 * M:3 * M, :], woT[2 * M:3 * M, :], wo16[2 * M:3 * M, :], ALU.subtract)\
                .then_inc(setup, 1)

            def flat(ap):
                return ap.rearrange("p m c -> p (m c)")

            def histogram_piece(n, jj, i):
                piece = magm[:, bass.ds((jj * 2 + i) * OHU, OHU)]
                dve.wait_ge(hist_done, n * NOH + jj * 2 + (i + 1))
                V.tensor_copy(ms[i][:, :, 0], piece).then_inc(ms_done, 1)
                dve.wait_ge(ms_done, n * (2 * NOH) + jj * 4 + (2 * i + 1))
                V.tensor_tensor(ms[i][:, :, 1], piece, ms[i][:, :, 0], ALU.subtract).then_inc(ms_done, 1)

            def phase_a(n, histogram):
                with dve.Fori(0, J4 // 2) as jj:
                    for i in range(2):
                        if histogram:
                            histogram_piece(n - 1, jj, i)
                        for s in range(4):
                            c = jj * 8 + (4 * i + s)
                            dve.wait_ge(x_in[s], n * XI + jj * 32 + 16 * (i + 1))
                            V.tensor_reduce(xs[:, :, bass.ds(c, 1)].rearrange("p h c -> p (h c)"), xr[s][:, :, :],
                                            AX.X, ALU.add).then_inc(x_used, 1)
                            dve.wait_ge(hi_done, n * NCH + jj * 8 + (4 * i + s + 1))
                            rows = bass.ds(c * ROWS + PAD, ROWS)
                            V.scalar_tensor_tensor(
                                out=hT[1][:, :, rows].rearrange("p c y -> p y c"),
                                in0=ps[2 + s % 2][:, :].rearrange("p (y c) -> p y c", y=ROWS), scalar=0.0,
                                in1=hT[0][:, :, rows].rearrange("p c y -> p y c"),
                                op0=ALU.max, op1=ALU.subtract).then_inc(lo_done, 1)

            def phase_b(n):
                steps = [0]

                def fc(ins):
                    steps[0] += 1
                    ins.then_inc(fc_dve, 1)
                    dve.wait_ge(fc_dve, n * FD + steps[0])

                def fc_products(i):
                    dve.wait_ge(fc_pe, n * 6 + i)

                dve.wait_ge(x_used, n * XQ + (CX + NCH))
                fc(V.tensor_reduce(xsum[:, :], xs[:, :, :], AX.X, ALU.add))
                dve.wait_ge(ha_out, n * NCH + (NCH + C2))
                fc(V.tensor_reduce(g2[:, 1:2], relu_hi[:, :], AX.X, ALU.add))
                fc_products(2)
                fc(V.scalar_tensor_tensor(out=gap[:, :], in0=ps[5][:, 0:KH], scalar=1.0 / PIX, in1=k["b1col"][:],
                                          op0=ALU.mult, op1=ALU.add))
                fc_products(3)
                fc(V.tensor_tensor(hid_raw[:, :], ps[5][:, KH:KH + HID // P], k["fc1b"][:], ALU.add))
                fc(V.tensor_scalar(hid[:, :], hid_raw[:, :], 0.0, None, ALU.max))
                for i in range(HID // P):
                    fc(V.tensor_scalar(hidb[:, i, :], ones[:, :], hid[:, i:i + 1], None, ALU.mult))
                fc_products(4)
                fc(V.tensor_tensor(z, ps[6][:, 0:C], k["fc2bB"][:], ALU.add))
                fc(V.tensor_scalar(zm, z, SATURATED, None, ALU.min))
                fc(V.tensor_tensor(zd, zm[:, 0:P], k["ident"][:], ALU.mult))
                fc(V.tensor_reduce(zc[:, :], zd, AX.X, ALU.add))
                fc(V.tensor_scalar(gt, zm, zc[:, 0:1], None, ALU.is_gt))
                fc(V.tensor_scalar(eq, zm, zc[:, 0:1], None, ALU.is_equal))
                fc(V.tensor_tensor(eq, eq, k["lower"][:], ALU.mult))
                fc(V.tensor_tensor(gt, gt, eq, ALU.add))
                fc(V.tensor_reduce(rank[:, :], gt, AX.X, ALU.add))
                fc(V.tensor_scalar(mask[:, :], rank[:, :], float(P) - 0.5, None, ALU.is_lt))
                fc_products(1)
                fc(V.tensor_reduce(s1row[:, :], ps[7][0:1, :].rearrange("p (c y) -> p c y", y=ROWS), AX.X, ALU.add))
                fc_products(5)
                fc(V.tensor_scalar(g2s[:, 0:1], ps[5][:, 6:7], 1.0 / PIX, None, ALU.mult))
                fc(V.tensor_scalar(g2s[:, 1:2], g2[:, 1:2], 1.0 / PIX, None, ALU.mult))
                for i in range(KH):
                    fc(V.tensor_scalar(g2b[:, i, :], ones[:, :], g2s[:, i:i + 1], None, ALU.mult))
                fc_products(6)
                fc(V.tensor_tensor(off[:, :], ps[5][:, 8:14], k["offbB"][:], ALU.add))
                dve.wait_ge(fc_act, n * FA + FA)
                fc(V.tensor_scalar(s1p[:, :], th[:, 0:3], 0.5, 1.5, ALU.mult, ALU.add))
                fc(V.reciprocal(rs[:, :], s1p[:, :]))
                fc(V.tensor_tensor(rq[:, :], th[:, 3:6], rs[:, :], ALU.mult))
                at = 0
                for q, rows_q in (3, 3), (2, 2), (1, 2):
                    fc(V.tensor_copy(R[:, at:at + rows_q * q].rearrange("p (a q) -> p a q", q=q),
                                     rq[:, 0:q].unsqueeze(1).to_broadcast([P, rows_q, q])))
                    at += rows_q * q
                fc(V.tensor_tensor(shifts[:], R[:, :].unsqueeze(2).to_broadcast([P, TSLOTS, PERIOD]), k["istap"][:], ALU.mult))
                fc(V.tensor_scalar(sc[:, :], s1p[:, :], mask[:, 0:1], PW_SCALE, ALU.mult, ALU.mult))
                for q in range(3):
                    fc(V.tensor_scalar(pwm[:, q, :], k["pwT"][:, q, :], sc[:, q:q + 1], None, ALU.mult))
                fc(V.tensor_copy(pwh[:, :, :], pwm))
                fc(V.tensor_tensor(pwl[:, :, :], pwm, pwh[:, :, :], ALU.subtract))
                assert steps[0] == FD, steps

            def phase_c(n):
                dve.sem_inc(passed["dve"], 1)
                with dve.Fori(0, NV // 2) as c:
                    for i in range(2):
                        dve.wait_ge(v_step, n * VS + c * 6 + (3 * i + CS + 3))
                        for ci in range(VCH):
                            u = ci % CR
                            dve.wait_ge(conv_ready, n * P + c * (2 * VCH) + (i * VCH + ci + 1))
                            for h in range(2):
                                ins = V.tensor_tensor(
                                    toep[u][h].rearrange("p (t a r) -> p t a r", t=TSLOTS, r=PERIOD),
                                    vhl[i][h][:, ci, :, :].unsqueeze(2).to_broadcast([P, TSLOTS, P // PERIOD, PERIOD]),
                                    k["band"][:].rearrange("p (a r) -> p a r", r=PERIOD).unsqueeze(1)
                                    .to_broadcast([P, TSLOTS, P // PERIOD, PERIOD]), ALU.mult)
                            ins.then_inc(t_ready, 1)

            def phase_d(n):
                def block_sum(j, s):
                    g = s % 2
                    dve.wait_ge(pw_ready, n * NCH + j * 4 + (s + 1 + C2))
                    dve.wait_ge(xb_done, n * (KH * NCH) + j * 8 + KH * (s + 1))
                    dve.wait_ge(y_out[g], n * YI + j * 32 + 16 * (s // 2 + 1))
                    dve.wait_ge(xp_ready, n * NCH + j * 4 + (s + 1))
                    for h in range(KH):
                        ins = V.scalar_tensor_tensor(out=yst[g][:, h, :], in0=ps[2 * g + h][:, :], scalar=1.0 / PW_SCALE,
                                                     in1=xr[s][:, h, :], op0=ALU.mult, op1=ALU.add)
                    ins.then_inc(x_used, 1)

                def project_out(j, s):
                    dve.wait_ge(xp_ready, n * NCH + j * 4 + (s + 1 + C2))
                    V.tensor_copy(xproj[:, :, bass.ds((j * 4 + s) * ROWS, ROWS)].rearrange("p m y -> p y m"),
                                  ps[4 + s % 2][:, 0:ROWS * M].rearrange("p (y m) -> p y m", y=ROWS)).then_inc(xp_out, 1)

                block_sum(0, 0)
                with dve.Fori(0, J4 - 1) as j:
                    for s in range(4):
                        block_sum(j + (s + 1) // 4, (s + 1) % 4)
                        project_out(j, s)
                for s in range(4):
                    if s < 3:
                        block_sum(J4 - 1, s + 1)
                    project_out(J4 - 1, s)

            done = [0]

            def st(n, ins):
                done[0] += 1
                ins.then_inc(l_dve, 1)

            def link(n, ins):
                st(n, ins)
                dve.wait_ge(l_dve, n * LD + done[0])

            def phase_e1(n):
                done[0] = 0
                for g in range(1, 8, 2):
                    dve.wait_ge(l_pe, n * LP + (g + 1))
                    st(n, V.tensor_copy(flat(f1[:, 2 * g:2 * g + 2, :]), ps[g % 4][:, :]))
                for g in range(4):
                    dve.wait_ge(l_pe, n * LP + (10 + 2 * g))
                    link(n, V.tensor_copy(flat(f2[:, 1, 4 * g:4 * g + 4, :]), ps[6 + g % 2][:, :]))
                link(n, V.tensor_tensor(mag_b, flat(f2[:, 1, :, :]), flat(f2[:, 1, :, :]), ALU.mult))
                dve.wait_ge(l_act, n * LA + 9)
                link(n, V.tensor_tensor(mag_a, mag_a, mag_b, ALU.add))
                dve.wait_ge(l_act, n * LA + 10)
                link(n, V.tensor_reduce(mag[:, :], mag_b.rearrange("p (m u) -> p u m", m=M), AX.X, ALU.add))
                link(n, V.tensor_tensor(magm[:, :], mag[:, :], k["high16"][:], ALU.mult))

            def phase_e2(n):
                done[0] = 12

                def ln(ins):
                    link(n, ins)

                dve.wait_ge(hist_done, n * NOH + (NOH + C2))
                ln(V.tensor_copy(h2[:, :], ps[4][0:2, 0:NBINS]))
                dve.wait_ge(l_pe, n * LP + 17)
                ln(V.tensor_copy(hp[:, 1:NBINS + 1], ps[5][0:1, 0:NBINS]))
                N = NBINS
                e, ra, rb, rc = (bins[:, i, :] for i in range(4))
                es = e[:, 1:N + 1]
                a_, b_, oh1 = bins[:, 4, 0:N], bins[:, 5, 0:N], bins[:, 6, 0:N]
                p1, msk, key = ra[:, 0:N], rb[:, 0:N], rc[:, 0:N]
                BIG = 1.0e30
                ln(V.tensor_scalar(a_, hp[:, 0:N], 0.25, None, ALU.mult))
                ln(V.scalar_tensor_tensor(out=b_, in0=hp[:, 1:N + 1], scalar=0.5, in1=a_, op0=ALU.mult, op1=ALU.add))
                ln(V.scalar_tensor_tensor(out=es, in0=hp[:, 2:N + 2], scalar=0.25, in1=b_, op0=ALU.mult, op1=ALU.add))
                ln(V.tensor_copy(e[:, 0:1], e[:, N:N + 1]))
                ln(V.tensor_copy(e[:, N + 1:N + 2], e[:, 1:2]))
                ln(V.tensor_reduce(pc[:, 0:1], es, AX.X, ALU.add))
                ln(V.tensor_scalar(pc[:, 1:2], pc[:, 0:1], 1.0 / N, None, ALU.mult))
                ln(V.tensor_scalar(p1, es, pc[:, 1:2], None, ALU.is_gt))
                ln(V.tensor_tensor(a_, es, e[:, 0:N], ALU.is_gt))
                ln(V.tensor_tensor(b_, es, e[:, 2:N + 2], ALU.is_gt))
                ln(V.tensor_tensor(p1, p1, a_, ALU.mult))
                ln(V.tensor_tensor(p1, p1, b_, ALU.mult))
                ln(V.tensor_reduce(pc[:, 2:3], p1, AX.X, ALU.add))
                ln(V.tensor_scalar(pc[:, 3:4], pc[:, 2:3], 0.5, None, ALU.is_lt))
                ln(V.tensor_scalar(p1, p1, pc[:, 3:4], None, ALU.max))
                ln(V.tensor_scalar(a_, p1, 1.0, BIG, ALU.subtract, ALU.mult))
                ln(V.tensor_tensor(b_, p1, es, ALU.mult))
                ln(V.tensor_tensor(msk, b_, a_, ALU.add))
                for i in range(2):
                    ln(V.tensor_reduce(pc[:, 4 + i:5 + i], msk, AX.X, ALU.max))
                    ln(V.tensor_scalar(a_, msk, pc[:, 4 + i:5 + i], None, ALU.is_equal))
                    ln(V.scalar_tensor_tensor(out=key, in0=a_, scalar=-1000.0, in1=k["binrow"][:], op0=ALU.mult, op1=ALU.add))
                    ln(V.tensor_reduce(pc[:, 6 + i:7 + i], key, AX.X, ALU.min))
                    ln(V.tensor_scalar(oh1, key, pc[:, 6 + i:7 + i], None, ALU.is_equal))
                    ln(V.tensor_tensor(b_, oh1, k["centers"][:], ALU.mult))
                    ln(V.tensor_reduce(pc[:, 8 + i:9 + i], b_, AX.X, ALU.add))
                    if i == 0:
                        ln(V.scalar_tensor_tensor(out=msk, in0=oh1, scalar=-2.0 * BIG, in1=msk, op0=ALU.mult, op1=ALU.add))
                ln(V.tensor_scalar(pc[:, 10:11], pc[:, 2:3], 1.5, None, ALU.is_gt))
                ln(V.tensor_scalar(pc[:, 11:12], pc[:, 10:11], -1.0, 1.0, ALU.mult, ALU.add))
                ln(V.tensor_tensor(pc[:, 12:13], pc[:, 8:9], pc[:, 11:12], ALU.mult))
                ln(V.scalar_tensor_tensor(out=pc[:, 9:10], in0=pc[:, 9:10], scalar=pc[:, 10:11], in1=pc[:, 12:13],
                                          op0=ALU.mult, op1=ALU.add))
                assert done[0] == 51, done
                dve.wait_ge(l_pe, n * LP + 18)
                ln(V.tensor_copy(pkb[:, :], ps[6][:, 0:2]))
                for i in range(2):
                    ln(V.tensor_scalar(gn[:, 2, :], k["theta"][:], pkb[:, i:i + 1], None, ALU.subtract))
                    ln(V.scalar_tensor_tensor(out=gn[:, 3, :], in0=gn[:, 2, :], scalar=-1.0, in1=gn[:, 2, :],
                                              op0=ALU.mult, op1=ALU.max))
                    ln(V.tensor_scalar(gn[:, 2, :], gn[:, 3, :], -1.0, float(np.float32(np.pi)), ALU.mult, ALU.add))
                    ln(V.tensor_tensor(gn[:, 3, :], gn[:, 3, :], gn[:, 2, :], ALU.min))
                    ln(V.tensor_scalar(gn[:, i, :], gn[:, 3, :], float(np.float32(np.radians(15.0))), None, ALU.is_le))
                ln(V.tensor_tensor(gn[:, 2, :], gn[:, 0, :], gn[:, 1, :], ALU.max))
                ln(V.tensor_tensor(gn[:, 3, :], gn[:, 2, :], k["gain_d"][:], ALU.mult))
                ln(V.tensor_tensor(gain[:, :], gn[:, 3, :], k["gain_lo"][:], ALU.add))
                for r in range(2):
                    ln(V.tensor_tensor(f2[:, r, :, :], f2[:, r, :, :], gain[:, :].unsqueeze(1).to_broadcast([P, M, P]),
                                       ALU.mult))
                for g in range(1, 8, 2):
                    dve.wait_ge(l_pe, n * LP + (19 + g))
                    st(n, V.tensor_copy(flat(f1[:, 2 * g:2 * g + 2, :]), ps[g % 4][:, :]))
                for g in range(4):
                    dve.wait_ge(l_act, n * LA + (15 + g))
                    st(n, V.tensor_tensor(flat(enh_hl[:, 1, 4 * g:4 * g + 4, :]), ps[4 + g % 3][:, :],
                                          flat(enh_hl[:, 0, 4 * g:4 * g + 4, :]), ALU.subtract))
                assert done[0] == LD, done

            phase_a(0, False)
            dve.wait_ge(x_used, CX + NCH)
            dve.sem_inc(x_used, NCH)
            phase_b(0)
            phase_c(0)
            phase_d(0)
            phase_e1(0)
            with dve.Fori(1, B) as n:
                phase_a(n, True)
                phase_e2(n - 1)
                phase_b(n)
                phase_c(n)
                phase_d(n)
                phase_e1(n)
            with dve.Fori(0, NOH // 2) as jj:
                for i in range(2):
                    histogram_piece(B - 1, jj, i)
            dve.sem_inc(x_used, NCH)
            phase_e2(B - 1)

        @block.tensor
        def _(pe):
            T = nc.tensor
            pe.sem_inc(hb_ready, CX)
            pe.sem_inc(conv_ready, CR)
            pe.sem_inc(pw_ready, C2)
            pe.sem_inc(xp_ready, C2)
            pe.sem_inc(hist_done, C2)
            pe.wait_ge(setup, SETUP)

            def histogram_piece(n, jj, i):
                pe.wait_ge(ms_done, n * (2 * NOH) + jj * 4 + 2 * (i + 1))
                pe.wait_ge(oh_in[i], n * (16 * NOH // 2) + jj * 16 + 16)
                for u in range(OHU):
                    mm = T.matmul(ps[4][0:2, 0:NBINS], ms[i][:, u, :], onehot[i][:, u, :], start=False, stop=False,
                                  skip_group_check=True)
                mm.then_inc(hist_done, 1)

            def start_histogram():
                pe.sem_inc(passed["pe"], 1)
                T.matmul(ps[4][0:2, 0:NBINS], ones16[0:1, 0:2], zeros16[:, :], start=True, stop=False, skip_group_check=True)

            def phase_a(n, histogram):
                if histogram:
                    pe.wait_ge(ms_done, (n - 1) * (2 * NOH) + 2)
                    start_histogram()
                with pe.Fori(0, J4 // 2) as jj:
                    for i in range(2):
                        for s in range(4):
                            g = s % 2
                            pe.wait_ge(x_in[s], n * XI + jj * 32 + 16 * (i + 1))
                            pe.wait_ge(ha_out, n * NCH + jj * 8 + (4 * i + s + 1))
                            for h in range(KH):
                                mm = T.matmul(ps[g][:, :], k["w1T"][:, h, P:C], xr[s][:, h, :], start=(h == 0),
                                              stop=(h == KH - 1))
                            mm.then_inc(ha_ready, 1)
                            pe.wait_ge(lo_done, n * NCH + jj * 8 + (4 * i + s + 1))
                            for part in (b1h, b1l):
                                T.matmul(ps[2 + g][:, :], ones16[0:1, :], part[:, :], start=(part is b1h), stop=False,
                                         skip_group_check=True)
                            for r in range(ROWS):
                                for h in range(KH):
                                    mm = T.matmul(ps[2 + g][:, r * P:(r + 1) * P], xr[s][:, h, r * P:(r + 1) * P],
                                                  k["w1T"][:, h, 0:P], start=False, stop=(r == ROWS - 1 and h == KH - 1),
                                                  skip_group_check=True)
                            mm.then_inc(hb_ready, 1)
                        if histogram:
                            histogram_piece(n - 1, jj, i)

            def pixel_sums(chunk, first, last):
                for h in range(2):
                    mm = T.matmul(ps[7][0:1, :], ones16[:, 0:1], hT[h][:, :, bass.ds(chunk * ROWS + PAD, ROWS)],
                                  start=(first and h == 0), stop=(last and h == 1), skip_group_check=True)
                return mm

            def phase_b1(n):
                pe.wait_ge(lo_done, n * NCH + (NCH + C2))
                pe.sem_inc(passed["pe"], 1)
                pixel_sums(0, True, False)
                with pe.Fori(1, NCH - 1) as c:
                    pixel_sums(c, False, False)
                pixel_sums(NCH - 1, False, True).then_inc(fc_pe, 1)

            def phase_b2(n):
                pe.wait_ge(fcw_in, n * 32 + 32)
                pe.wait_ge(fc_dve, n * FD + 1)
                for o in range(KH):
                    for h in range(KH):
                        mm = T.matmul(ps[5][:, o:o + 1], k["w1T"][:, h, o * P:(o + 1) * P], xsum[:, h:h + 1],
                                      start=(h == 0), stop=(h == KH - 1))
                mm.then_inc(fc_pe, 1)
                pe.wait_ge(fc_dve, n * FD + 3)
                for o in range(HID // P):
                    for h in range(KH):
                        mm = T.matmul(ps[5][:, KH + o:KH + o + 1], fc1T[:, h, o * P:(o + 1) * P], gap[:, h:h + 1],
                                      start=(h == 0), stop=(h == KH - 1))
                mm.then_inc(fc_pe, 1)
                pe.wait_ge(fc_dve, n * FD + 9)
                for i in range(HID // P):
                    mm = T.matmul(ps[6][:, 0:C], hidb[:, i, :], fc2T[:, i, :], start=(i == 0), stop=(i == HID // P - 1))
                mm.then_inc(fc_pe, 1)
                pe.wait_ge(fc_dve, n * FD + 20)
                T.matmul(ps[5][:, 6:7], s1row[:, :], ones[0:1, 0:1], start=True, stop=True).then_inc(fc_pe, 1)
                pe.wait_ge(fc_dve, n * FD + 24)
                for h in range(KH):
                    mm = T.matmul(ps[5][:, 8:14], g2b[:, h, :], k["offT"][:, h, :], start=(h == 0), stop=(h == KH - 1))
                mm.then_inc(fc_pe, 1)

            def mix_group(n, j, g):
                i = g // 2
                pe.wait_ge(e_in[i], (n - 1) * (32 * J4) + j * 32 + 32)
                pe.wait_ge(mix_out, (n - 1) * NCH + j * 4 + (g + 1))
                for h in range(KH):
                    mm = T.matmul(ps[4 + 2 * (g % 2) + h][:, :], wol[:, h * P:(h + 1) * P],
                                  enh_in[i][:, (g % 2) * CHUNK:(g % 2 + 1) * CHUNK], start=True, stop=True)
                mm.then_inc(mix_ready, 1)

            def phase_c(n, mix):
                with pe.Fori(0, J4) as j:
                    for c in range(16):
                        u = c % CR
                        pe.wait_ge(t_ready, n * P + j * 16 + (c + 1 + CV))
                        pe.wait_ge(conv_out, n * P + j * 16 + (c + 1))
                        col = 0
                        for i, (dy, q) in enumerate(TAP_ROWS):
                            for hd, hw in ((0, 0), (0, 1), (1, 0)):
                                mm = T.matmul(ps[u][:, 0:q * P],
                                              hT[hd][:, bass.ds(j * 16 + c, 1), PAD + dy:PAD + dy + P].rearrange("p c y -> p (c y)"),
                                              toep[u][hw][:, col:col + q * P],
                                              start=(i == 0 and hd + hw == 0), stop=(i == len(TAP_ROWS) - 1 and hd == 1),
                                              skip_group_check=True)
                            col += q * P
                        mm.then_inc(conv_ready, 1)
                        if mix and c % 4 == 3:
                            mix_group(n, j, c // 4)

            def phase_d(n):
                def pointwise(j, s):
                    g = s % 2
                    pe.wait_ge(glo_done, n * NCH + j * 4 + (s + 1 + C2))
                    pe.wait_ge(x_used, n * XQ + j * 4 + (s + CX + 2 * NCH - 1))
                    parts = [a.rearrange("p (y q x) -> p q y x", y=ROWS, q=3) for a in (gh[g], glo[g])]
                    for h in range(KH):
                        for i, (w, d) in enumerate(((pwh, 0), (pwl, 0), (pwh, 1))):
                            for q in range(3):
                                mm = T.matmul(ps[2 * g + h][:, :], w[:, q, h * P:(h + 1) * P], parts[d][:, q, :, :],
                                              start=(i == 0 and q == 0), stop=(i == 2 and q == 2))
                    mm.then_inc(pw_ready, 1)

                def project(j, s):
                    g = s % 2
                    pe.wait_ge(x_used, n * XQ + j * 4 + (s + 1 + CX + 2 * NCH))
                    pe.wait_ge(xp_out, n * NCH + j * 4 + (s + 1))
                    for r in range(ROWS):
                        for h in range(KH):
                            mm = T.matmul(ps[4 + g][:, r * M:(r + 1) * M], yst[g][:, h, r * P:(r + 1) * P], k["winT"][:, h, :],
                                          start=(h == 0), stop=(h == KH - 1))
                    mm.then_inc(xp_ready, 1)

                pe.wait_ge(fc_dve, n * FD + FD)
                pointwise(0, 0)
                with pe.Fori(0, J4 - 1) as j:
                    for s in range(4):
                        pointwise(j + (s + 1) // 4, (s + 1) % 4)
                        project(j, s)
                for s in range(4):
                    if s < 3:
                        pointwise(J4 - 1, s + 1)
                    project(J4 - 1, s)

            def phase_e1(n):
                pe.wait_ge(xp_out, n * NCH + (NCH + C2))
                for g in range(8):
                    if g >= 4:
                        pe.wait_ge(l_dve if g % 2 else l_act, n * (LD if g % 2 else LA) + ((g - 4) // 2 + 1))
                    for i in range(2):
                        mm = T.matmul(ps[g % 4][:, i * 2 * P:(i + 1) * 2 * P], xproj[:, 2 * g + i, :], k["dft_fwd"][:],
                                      start=True, stop=True)
                    mm.then_inc(l_pe, 1)
                pe.wait_ge(l_act, n * LA + 4)
                pe.wait_ge(l_dve, n * LD + 4)
                for g in range(4):
                    re, im = (f1[:, 4 * g:4 * g + 4, r * P:(r + 1) * P] for r in range(2))
                    if g >= 2:
                        pe.wait_ge(l_act, n * LA + (5 + g - 2))
                    T.matmul(ps[4 + g % 2][:, :], k["dft_c"][:], re, start=True, stop=False)
                    T.matmul(ps[4 + g % 2][:, :], k["dft_s"][:], im, start=False, stop=True).then_inc(l_pe, 1)
                    if g >= 2:
                        pe.wait_ge(l_dve, n * LD + (5 + g - 2))
                    T.matmul(ps[6 + g % 2][:, :], k["dft_c"][:], im, start=True, stop=False)
                    T.matmul(ps[6 + g % 2][:, :], k["dft_ns"][:], re, start=False, stop=True).then_inc(l_pe, 1)

            def phase_e2(n):
                pe.wait_ge(l_dve, n * LD + 51)
                pe.sem_inc(passed["pe"], 1)
                T.matmul(ps[6][:, 0:2], ones[0:1, :], pc[:, 8:10], start=True, stop=True).then_inc(l_pe, 1)
                pe.wait_ge(l_dve, n * LD + 67)
                for g in range(8):
                    if g >= 4:
                        pe.wait_ge(l_dve if g % 2 else l_act, n * (LD if g % 2 else LA) + ((68 if g % 2 else 11) + (g - 4) // 2))
                    for i in range(2):
                        m = 2 * g + i
                        T.matmul(ps[g % 4][:, i * 2 * P:(i + 1) * 2 * P], f2[:, 0, m, :], k["inv_cs"][:], start=True, stop=False)
                        mm = T.matmul(ps[g % 4][:, i * 2 * P:(i + 1) * 2 * P], f2[:, 1, m, :], k["inv_nsc"][:], start=False, stop=True)
                    mm.then_inc(l_pe, 1)
                pe.wait_ge(l_act, n * LA + 14)
                pe.wait_ge(l_dve, n * LD + 71)
                for g in range(4):
                    if g == 3:
                        pe.wait_ge(l_dve, n * LD + 72)
                    for i in range(4):
                        m = 4 * g + i
                        T.matmul(ps[4 + g % 3][:, i * P:(i + 1) * P], f1[:, m, 0:P], k["inv_c"][:], start=True, stop=False)
                        mm = T.matmul(ps[4 + g % 3][:, i * P:(i + 1) * P], f1[:, m, P:2 * P], k["inv_ns"][:], start=False, stop=True)
                    mm.then_inc(l_pe, 1)

            def histogram_sum(n):
                pe.wait_ge(l_dve, n * LD + 13)
                pe.sem_inc(passed["pe"], 1)
                T.matmul(ps[5][0:1, 0:NBINS], ones[0:2, 0:1], h2[:, :], start=True, stop=True).then_inc(l_pe, 1)

            phase_a(0, False)
            phase_b1(0)
            phase_b2(0)
            phase_c(0, False)
            phase_d(0)
            phase_e1(0)
            with pe.Fori(1, B) as n:
                phase_a(n, True)
                histogram_sum(n - 1)
                phase_b1(n)
                phase_e2(n - 1)
                phase_b2(n)
                phase_c(n, True)
                phase_d(n)
                phase_e1(n)
            pe.wait_ge(ms_done, (B - 1) * (2 * NOH) + 2)
            start_histogram()
            with pe.Fori(0, NOH // 2) as jj:
                for i in range(2):
                    histogram_piece(B - 1, jj, i)
            histogram_sum(B - 1)
            phase_e2(B - 1)
            with pe.Fori(0, J4) as j:
                for g in range(4):
                    mix_group(B, j, g)


def geometry():
    f = np.float32
    pi = f(np.pi)
    dy, dx = np.meshgrid(np.arange(-P // 2, P // 2, dtype=f), np.arange(-P // 2, P // 2, dtype=f), indexing="ij")
    angle = np.arctan2(dy.astype(np.float64), dx)
    theta = (angle.astype(f) + pi).astype(f)
    high = np.sqrt(dy * dy + dx * dx) > f(0.3 * (P // 2))
    step = (np.arange(NBINS, dtype=f) / f(NBINS)).astype(f)
    edges = np.concatenate([pi * step, [pi]]).astype(f)
    folded = np.mod((angle + np.pi).astype(f), pi)
    bins = np.clip(np.searchsorted(edges, folded.reshape(-1), side="left") - 1, 0, NBINS - 1).reshape(P, P)
    order = (np.arange(P) + P // 2) % P
    theta, high, bins = (a[np.ix_(order, order)] for a in (theta, high, bins))
    onehot = (bins[:, :, None] == np.arange(NBINS)).astype(np.float16)
    lo = np.where(high, f(0.8), f(1.0)).astype(f)
    hi = np.where(high, f(1.2), f(1.0)).astype(f)
    return {"theta": theta, "gain_lo": lo, "gain_d": (hi - lo).astype(f), "high16": high.astype(f) / f(M),
            "onehot": onehot, "binrow": np.arange(NBINS, dtype=f)[None],
            "centers": ((edges[:-1] + edges[1:]) * f(0.5)).astype(f)[None]}


def tables():
    g = np.arange(P)
    a = 2 * np.pi * np.outer(g, g) / P
    c, s = np.cos(a), np.sin(a)
    out = {"dft_fwd": np.concatenate([c, -s], 1) / P, "dft_c": c, "dft_s": s, "dft_ns": -s,
           "inv_cs": np.concatenate([c, s], 1), "inv_nsc": np.concatenate([-s, c], 1), "inv_c": c / P, "inv_ns": -s / P,
           "ident": np.eye(P), "lower": (np.arange(C)[None, :] < g[:, None])}
    out = {name: np.ascontiguousarray(v, dtype=np.float32) for name, v in out.items()}
    out["band"] = (np.abs(g[:, None] - g[None, :]) <= PAD).astype(np.float16)
    out["istap"] = tap_rows([np.ones((P, 1, size, size), np.float32) for size in (7, 5, 3)])[:, 0]
    out.update(geometry())
    return out


def halves(a):
    return np.ascontiguousarray(np.swapaxes(a.reshape((-1, P) + a.shape[1:]), 0, 1))


def tap_rows(dws):
    padded = []
    for dw in dws:
        size = dw.shape[-1]
        full = np.zeros((P, 2 * PAD + 1, PERIOD), np.float32)
        m = PAD - size // 2
        full[:, m:m + size, m:m + size] = dw[:P, 0]
        padded.append(full)
    rows = np.stack([padded[q][:, PAD + dy] for dy, kinds in TAP_ROWS for q in range(kinds)], 1)
    index = (np.arange(P)[:, None] - np.arange(PERIOD)[None, :] + PAD) % PERIOD
    return np.ascontiguousarray(np.moveaxis(rows[:, :, index], 2, 0))


def kernel(**inputs):
    import concourse.bacc as bacc
    from concourse.bass_utils import run_bass_kernel_spmd

    a = {name: np.asarray(v) for name, v in inputs.items()}
    L0 = "L0_conv_"
    order = [4, 2, 0, 5, 3, 1]
    pw = a[L0 + "pw_w"][:, :3 * P].reshape(C, 3, P)[:, ::-1]
    arrays = {
        "x": a["x"].reshape(B, KH, P, PIX),
        "w1T": halves(a[L0 + "pw1_w"].T), "b1col": halves(a[L0 + "pw1_b"]),
        "b1row": np.tile(a[L0 + "pw1_b"][:P], ROWS)[None],
        "fc1T": halves(a[L0 + "fc1_w"].T), "fc1b": halves(a[L0 + "fc1_b"]),
        "fc2T": halves(a[L0 + "fc2_w"].T), "fc2bB": np.tile(a[L0 + "fc2_b"][None], (P, 1)),
        "offT": halves(a[L0 + "off_w"][order].T), "offbB": np.tile(a[L0 + "off_b"][order][None], (P, 1)),
        "pwT": np.transpose(pw, (2, 1, 0)), "pwb": halves(a[L0 + "pw_b"]),
        "winT": halves(a["L1_conv_w_in"].T), "woT": np.tile(a["L1_conv_w_out"].T, (3, 1)),
        "taps": tap_rows([a[L0 + "dw7"], a[L0 + "dw5"], a[L0 + "dw3"]]),
        **tables(),
    }
    arrays = {name: np.ascontiguousarray(v) for name, v in arrays.items()}
    nc = bacc.Bacc("TRN2", target_bir_lowering=False, num_devices=1)
    t = {name: nc.dram_tensor("in_" + name, v.shape, mybir.dt.from_np(v.dtype), kind="ExternalInput").ap()
         for name, v in arrays.items()}
    t["out"] = nc.dram_tensor("out", (B, KH, P, PIX), F32, kind="ExternalOutput").ap()
    build(nc, t)
    r = run_bass_kernel_spmd(nc, [{"in_" + name: v for name, v in arrays.items()}], core_ids=[0])
    return r.results[0]["out"].reshape(B, C, P, P)
```

```python
from contextlib import ExitStack

import numpy as np

import concourse.bass as bass
from concourse import mybir

F32 = mybir.dt.float32
F16 = mybir.dt.float16
ALU = mybir.AluOpType
ACT = mybir.ActivationFunctionType
AX = mybir.AxisListType

P = 128
B, C = 8, 256
KH = C // P
PIX = P * P
ROWS = 4
CHUNK = ROWS * P
NCH = P // ROWS
XSLOTS = 4
PAD = 3
YP = P + 2 * PAD
TAP_ROWS = [(0, 3), (-1, 3), (1, 3), (-2, 2), (2, 2), (-3, 1), (3, 1)]
TSLOTS = sum(k for _, k in TAP_ROWS)
TCOLS = TSLOTS * P
PERIOD = 8
VCH = 4
BL = 32
HALF = NCH // 2
LATE = 3
CR = 4
NV = P // VCH
HID = 2 * C
M = 16
NBINS = 180
OUT3 = 3 * P
OHU = 16
NOH = P // OHU
PW_SCALE = 64.0
PW1_SCALE = 8.0
SATURATED = 16.63553

XQ = 3 * NCH
FD, FA = 37, 3
OFFSETS, SHIFTS = 24, 31
LP, LA, LD = 30, 22, 73


def build(nc, t):
    with ExitStack() as ctx:
        def sb(name, shape, dt=F32):
            return ctx.enter_context(nc.sbuf_tensor(name, shape, dt))

        def sem(name):
            return ctx.enter_context(nc.semaphore(name))

        names = ["w1T", "b1col", "fc1b", "fc2bB", "offT", "offbB", "pwT", "pwb", "winT",
                 "dft_fwd", "dft_c", "dft_s", "dft_ns", "inv_cs", "inv_nsc", "inv_c", "inv_ns",
                 "ident", "lower", "theta", "gain_lo", "gain_d", "high16", "band", "istap", "binrow", "centers"]
        k = {}
        for name in names:
            src = t[name]
            k[name] = sb("k_" + name, list(src.shape), F16 if name == "band" else F32)
        bias_hl = sb("bias_hl", [BL + 1, CHUNK], F16)
        w1h = sb("w1h", [P, KH, C], F16)
        w1l = sb("w1l", [P, KH, C], F16)
        ones16 = sb("ones16", [P, P], F16)
        ones = sb("ones", [P, P])
        wo16 = sb("wo16", [3 * M, C], F16)
        wol = sb("wol", [3 * M, C], F16)

        zeros16 = sb("zeros16", [1, NBINS], F16)

        arena = sb("arena", [P, 2 * P * YP], F16)
        hT = [arena[:, i * P * YP:(i + 1) * P * YP].rearrange("p (c y) -> p c y", y=YP) for i in range(2)]

        late = [arena[:, i * 2 * KH * CHUNK:(i + 1) * 2 * KH * CHUNK].bitcast(F32).rearrange("p (h x) -> p h x", h=KH)
                for i in range(4 * LATE)]

        work2 = sb("work2", [P, 2 * 2 * TCOLS + 4 * OUT3 * 2], F16)
        gst0 = 4 * TCOLS
        gst = [work2[:, gst0 + 2 * OUT3 * s:gst0 + 2 * OUT3 * (s + 1)].bitcast(F32) for s in range(4)]
        MP = M * P
        f1 = work2[:, 0:4 * MP].bitcast(F32).rearrange("p (m c) -> p m c", m=M)
        mag_a = work2[:, 0:2 * MP].bitcast(F32)
        mag_b = work2[:, 2 * MP:4 * MP].bitcast(F32)
        gn = work2[:, 0:8 * P].bitcast(F32).rearrange("p (i u) -> p i u", i=4)
        bins = work2[0:1, 4 * MP:4 * MP + 14 * (NBINS + 2)].bitcast(F32).rearrange("p (i b) -> p i b", i=7)
        b1row = work2[0:BL + 1, 0:2 * CHUNK].bitcast(F32)
        b1h = work2[0:BL + 1, 2 * CHUNK:3 * CHUNK]
        woT = work2[0:3 * M, 3 * CHUNK:3 * CHUNK + 2 * C].bitcast(F32)

        G = ROWS * OUT3
        work3 = sb("work3", [P, 8 * G], F16)
        late_end = 4 * LATE * 2 * KH * CHUNK
        gl = [work3[:, 2 * G * g:2 * G * (g + 1)].bitcast(F32) for g in range(2)] + \
             [arena[:, late_end + 2 * G * g:late_end + 2 * G * (g + 1)].bitcast(F32) for g in range(2)]
        gh = [work3[:, 4 * G + G * g:4 * G + G * (g + 1)] for g in range(2)]
        glo = [work3[:, 6 * G + G * g:6 * G + G * (g + 1)] for g in range(2)]
        f2 = work3[:, 0:4 * MP].bitcast(F32).rearrange("p (r m u) -> p r m u", r=2, m=M)
        t3 = 8 * G - 4 * TCOLS
        toep = [[work2[:, (2 * u + h) * TCOLS:(2 * u + h + 1) * TCOLS] for h in range(2)] for u in range(2)] + \
               [[work3[:, t3 + (2 * u + h) * TCOLS:t3 + (2 * u + h + 1) * TCOLS] for h in range(2)] for u in range(2)]
        EARLY = P - 16
        assert t3 >= 2 * G and CR == 4
        FC = 2 * KH * HID
        fc1T = work3[:, 4 * MP:4 * MP + FC].bitcast(F32).rearrange("p (h o) -> p h o", h=KH)
        fc2T = work3[:, 4 * MP + FC:4 * MP + 2 * FC].bitcast(F32).rearrange("p (h o) -> p h o", h=HID // P)
        work5 = sb("work5", [P, 2 * OHU * NBINS], F16)
        onehot = [work5[:, i * OHU * NBINS:(i + 1) * OHU * NBINS].rearrange("p (u b) -> p u b", u=OHU) for i in range(2)]
        at = [0]

        def temp(*shape):
            size = int(np.prod(shape))
            a = work5[:, at[0]:at[0] + 2 * size].bitcast(F32)
            at[0] += 2 * size
            return a.rearrange("p (a b) -> p a b", a=shape[0]) if len(shape) == 2 else a

        hidb, g2b, pwm = temp(HID // P, P), temp(KH, P), temp(3, C)
        z, zm, gt, eq, zd = temp(C), temp(C), temp(C), temp(C), temp(P)
        assert at[0] <= 2 * OHU * NBINS

        work4 = sb("work4", [P, 2 * MP], F16)
        xproj = work4[:, :].bitcast(F32).rearrange("p (m y) -> p m y", m=M)
        enh_hl = work4[:, :].rearrange("p (t m x) -> p t m x", t=2, m=M)
        enh_in = [sb(f"enh_in{i}", [3 * M, 2 * CHUNK], F16) for i in range(2)]

        xh, xl = ([work4[:, (2 * h + i) * KH * CHUNK:(2 * h + i + 1) * KH * CHUNK].rearrange("p (h x) -> p h x", h=KH)
                   for i in range(2)] for h in range(2))
        vbase = [sb(f"vbase{i}", [P, VCH, TSLOTS, PERIOD]) for i in range(2)]
        vsum = sb("vsum", [P, VCH, TSLOTS, PERIOD])
        vhl = [[sb(f"v{'hl'[h]}{i}", [P, VCH, TSLOTS, PERIOD], F16) for h in range(2)] for i in range(2)]
        xr = [sb(f"xr{s}", [P, KH, CHUNK]) for s in range(XSLOTS)]
        yst = [sb(f"yst{s}", [P, KH, CHUNK]) for s in range(2)]
        relu_out = sb("relu_out", [P, 2, CHUNK], F16)
        xs = sb("xs", [P, KH, NCH])
        relu_hi = sb("relu_hi", [P, NCH])
        xsum = sb("xsum", [P, KH])
        gap = sb("gap", [P, KH])
        hid_raw = sb("hid_raw", [P, HID // P])
        hid = sb("hid", [P, HID // P])
        zc = sb("zc", [P, 1])
        rank = sb("rank", [P, 1])
        mask = sb("mask", [P, 1])
        relu_lo = sb("relu_lo", [P, CHUNK])
        g2 = sb("g2", [P, KH])
        g2s = sb("g2s", [P, KH])
        off = sb("off", [P, 6])
        offt = sb("offt", [P, 6])
        th = sb("th", [P, 6])
        s1p = sb("s1p", [P, 3])
        rs = sb("rs", [P, 3])
        rq = sb("rq", [P, 3])
        R = sb("R", [P, TSLOTS])
        shifts = sb("shifts", [P, TSLOTS, PERIOD])
        sc = sb("sc", [P, 3])
        pwh = sb("pwh", [P, 3, C], F16)
        pwl = sb("pwl", [P, 3, C], F16)
        mag = sb("mag", [P, P])
        magm = sb("magm", [P, P])
        ms = [sb(f"ms{i}", [P, OHU, 2], F16) for i in range(2)]
        h2 = sb("h2", [2, NBINS])
        hp = sb("hp", [1, NBINS + 2])
        pc = sb("pc", [1, 16])
        pkb = sb("pkb", [P, 2])
        gain = sb("gain", [P, P])

        ps = [ctx.enter_context(nc.psum_tensor(f"ps{i}", [P, 512], F32)) for i in range(8)]

        g_dram = nc.dram_tensor("conv_out", [P, P, OUT3], F32, kind="Internal").ap()
        y_dram = nc.dram_tensor("block_out", [KH, P, PIX], F32, kind="Internal").ap()
        e_dram = nc.dram_tensor("enhanced", [2 * M, P, P], F16, kind="Internal").ap()
        x_in_d, out_d = t["x"], t["out"]

        consts_in = sem("consts_in")
        setup = sem("setup")
        x_in = [sem(f"x_in{s}") for s in range(XSLOTS)]
        xh_done = sem("xh_done")
        x_used = sem("x_used")
        ha_ready, ha_out = sem("ha_ready"), sem("ha_out")
        hb_ready, hi_done, lo_done = sem("hb_ready"), sem("hi_done"), sem("lo_done")
        fc_pe, fc_act, fc_dve = sem("fc_pe"), sem("fc_act"), sem("fc_dve")
        v_in = [sem(f"v_in{i}") for i in range(2)]
        v_step = sem("v_step")
        t_ready = sem("t_ready")
        conv_ready, conv_out = sem("conv_ready"), sem("conv_out")
        g_out = [sem(f"g_out{s}") for s in range(4)]
        g_in = [sem(f"g_in{s}") for s in range(4)]
        g_early = sem("g_early")
        gh_done, glo_done = sem("gh_done"), sem("glo_done")
        xb_done, pw_ready = sem("xb_done"), sem("pw_ready")
        y_out = [sem(f"y_out{s}") for s in range(2)]
        xp_ready, xp_out = sem("xp_ready"), sem("xp_out")
        oh_in = [sem(f"oh_in{i}") for i in range(2)]
        ms_done, hist_done = sem("ms_done"), sem("hist_done")
        fcw_in = sem("fcw_in")
        pads = sem("pads")
        sum_step = sem("sum_step")
        l_pe, l_act, l_dve = sem("l_pe"), sem("l_act"), sem("l_dve")
        e_out, e_in = sem("e_out"), [sem(f"e_in{i}") for i in range(2)]
        mix_ready, mix_out = sem("mix_ready"), sem("mix_out")
        passed = {e: sem("passed_" + e) for e in ("sp", "pool", "act", "dve", "pe")}
        SETUP = 17
        CX, C2, CV, CS = XSLOTS, 2, 2 * VCH, 6

        XI = 16 * XQ // XSLOTS
        XI1 = 16 * NCH // XSLOTS
        YI = 16 * NCH
        J4 = NCH // 4
        VS = 3 * NV
        SS = 1 + 2 * NCH

        def staged(j, s):
            return late[4 * (j - (J4 - LATE)) + s] if isinstance(j, int) and j >= J4 - LATE else yst[s % 2]

        block = ctx.enter_context(nc.Block())

        @block.sync
        def _(sp):
            for name in names:
                sp.dma_start(k[name][:], t[name]).then_inc(consts_in, 16)
            sp.dma_start(b1row, t["b1row"]).then_inc(consts_in, 16)
            sp.dma_start(woT, t["woT"]).then_inc(consts_in, 16)

            def load_x(n, phase, j, s):
                sp.wait_ge(x_used, n * XQ + j * 4 + (phase * NCH + 1 + s))
                src = x_in_d[bass.ds(n, 1), :, :, bass.ds((j * 4 + s) * CHUNK, CHUNK)].rearrange("n h p x -> p (n h) x")
                sp.dma_start(xr[s][:], src).then_inc(x_in[s], 16)

            def phase_a(n, onehots):
                sp.wait_ge(pw_ready, n * NCH + C2)
                sp.sem_inc(passed["sp"], 1)
                sp.dma_start(fc1T, t["fc1T"]).then_inc(fcw_in, 16)
                sp.dma_start(fc2T, t["fc2T"]).then_inc(fcw_in, 16)
                with sp.Fori(0, J4 // 4) as jj:
                    for i in range(8):
                        load_x(n, 0, jj * 2 + i // 4, i % 4)
                        if onehots and i % 2 == 0:
                            load_onehot(n, jj, i // 2)
                with sp.Fori(J4 // 4, J4 // 2) as jj:
                    for i in range(8):
                        load_x(n, 0, jj * 2 + i // 4, i % 4)
                sp.wait_ge(hb_ready, n * NCH + (NCH + CX))
                sp.wait_ge(x_used, n * XQ + (CX + NCH))
                sp.sem_inc(passed["sp"], 1)

            def load_onehot(n, jj, i):
                sp.wait_ge(hist_done, (n - 1) * NOH + jj * 4 + (i + 1))
                sp.sem_inc(passed["sp"], 1)
                sp.dma_start(onehot[i % 2], t["onehot"][:, bass.ds((jj * 4 + i) * OHU, OHU), :]).then_inc(oh_in[i % 2], 16)

            def load_enhanced(j, i):
                px = bass.ds((j * 4 + 2 * i) * CHUNK, 2 * CHUNK)
                sp.dma_start(enh_in[i][0:2 * M, :], e_flat[:, px]).then_inc(e_in[i], 16)
                sp.dma_start(enh_in[i][2 * M:3 * M, :], e_flat[0:M, px]).then_inc(e_in[i], 16)

            def load_y(n, j, s):
                sp.wait_ge(x_used, n * XQ + j * 4 + (NCH + 1 + s))
                sp.sem_inc(passed["sp"], 1)
                sp.dma_start(xr[s][:], y_dram[:, :, bass.ds((j * 4 + s) * CHUNK, CHUNK)].rearrange("h p x -> p h x"))\
                    .then_inc(x_in[s], 16)

            def store_out(n, j, s):
                sp.wait_ge(x_used, n * XQ + j * 4 + (NCH + CX + 1 + s))
                sp.sem_inc(passed["sp"], 1)
                sp.dma_start(out_d[bass.ds(n - 1, 1), :, :, bass.ds((j * 4 + s) * CHUNK, CHUNK)]
                             .rearrange("n h p x -> p (n h) x"), yst[s % 2][:]).then_inc(y_out[s % 2], 16)

            def start_mix(n):
                for i in range(2):
                    sp.wait_ge(y_out[i], (n - 1) * YI + (YI // 2 + 16))
                    sp.sem_inc(passed["sp"], 1)
                for s in range(4):
                    load_y(n, 0, s)
                sp.wait_ge(l_dve, (n - 1) * LD + LD)
                sp.wait_ge(l_act, (n - 1) * LA + LA)
                sp.sem_inc(passed["sp"], 1)
                sp.dma_start(e_dram.rearrange("m y x -> y m x"), enh_hl.rearrange("p t m x -> p (t m) x"))\
                    .then_inc(e_out, 16)
                sp.wait_ge(e_out, (n - 1) * 16 + 16)
                sp.sem_inc(passed["sp"], 1)
                for i in range(2):
                    load_enhanced(0, i)

            def mix_group(n, j, s, more):
                store_out(n, j, s)
                if more:
                    load_y(n, j + 1, s)
                    if s % 2:
                        sp.wait_ge(mix_ready, (n - 1) * NCH + j * 4 + (s + 1))
                        sp.sem_inc(passed["sp"], 1)
                        load_enhanced(j + 1, s // 2)

            def conv_group(n, j, g):
                for s in range(4):
                    sp.wait_ge(conv_out, n * P + j * 16 + (4 * g + s + 1 + CR))
                    sp.dma_start(g_dram[bass.ds(j * 16 + (4 * g + s), 1)].rearrange("c y f -> (c y) f"), gst[s])\
                        .then_inc(g_out[s], 16)

            def phase_c(n, mix):
                if mix:
                    start_mix(n)
                with sp.Fori(0, J4 - 1) as j:
                    for g in range(4):
                        conv_group(n, j, g)
                        if mix:
                            mix_group(n, j, g, True)
                for g in range(4):
                    conv_group(n, J4 - 1, g)
                    if mix:
                        mix_group(n, J4 - 1, g, False)
                    if g == 1:
                        for s in range(4):
                            sp.wait_ge(g_out[s], n * (16 * P // 4) + 16 * (EARLY // 4 + 1))
                            sp.sem_inc(passed["sp"], 1)
                        sp.dma_start(gl[0].rearrange("p (y f) -> p y f", y=ROWS)[0:EARLY], g_dram[0:EARLY, 0:ROWS, :])\
                            .then_inc(g_early, 16)

            def phase_d(n):
                for s in range(4):
                    sp.wait_ge(g_out[s], n * (16 * P // 4) + 16 * (P // 4 + 1))
                sp.wait_ge(x_used, n * XQ + (CX + 2 * NCH))
                sp.sem_inc(passed["sp"], 1)

                def load_d(j, s):
                    load_g(j, s)
                    load_x(n, 2, j, s)

                def load_g(j, s):
                    sp.wait_ge(glo_done, n * NCH + j * 4 + (s + 1))
                    sp.sem_inc(passed["sp"], 1)
                    sp.dma_start(gl[s].rearrange("p (y f) -> p y f", y=ROWS),
                                 g_dram[:, bass.ds((j * 4 + s) * ROWS, ROWS), :]).then_inc(g_in[s], 16)

                def store_y(j, s):
                    sp.wait_ge(x_used, n * XQ + j * 4 + (s + 1 + 2 * NCH + CX))
                    sp.sem_inc(passed["sp"], 1)
                    sp.dma_start(y_dram[:, :, bass.ds((j * 4 + s) * CHUNK, CHUNK)].rearrange("h p x -> p h x"),
                                 staged(j, s)[:]).then_inc(y_out[s % 2], 16)

                sp.dma_start(gl[0].rearrange("p (y f) -> p y f", y=ROWS)[EARLY:P], g_dram[EARLY:P, 0:ROWS, :])\
                    .then_inc(g_in[0], 16)
                load_g(0, 1)
                load_x(n, 2, 0, 0)
                load_x(n, 2, 0, 1)
                load_d(0, 2)
                load_d(0, 3)
                with sp.Fori(0, J4 - LATE) as j:
                    for s in range(4):
                        load_d(j + 1, s)
                        store_y(j, s)
                for c in range(NCH - 4 * LATE + 4, NCH):
                    load_d(c // 4, c % 4)
                for c in range(NCH - 4 * LATE, NCH):
                    store_y(c // 4, c % 4)

            e_flat = e_dram.rearrange("m y x -> m (y x)")
            phase_a(0, False)
            for s in range(XSLOTS):
                sp.sem_inc(x_in[s], XI1)
            phase_c(0, False)
            phase_d(0)
            with sp.Fori(1, B) as n:
                phase_a(n, True)
                phase_c(n, True)
                phase_d(n)
            with sp.Fori(0, NOH // 4) as jj:
                for i in range(4):
                    load_onehot(B, jj, i)
            for s in range(XSLOTS):
                sp.sem_inc(x_in[s], XI1)
            start_mix(B)
            with sp.Fori(0, J4 - 1) as j:
                for g in range(4):
                    mix_group(B, j, g, True)
            for g in range(4):
                mix_group(B, J4 - 1, g, False)
            for s in range(2):
                sp.wait_ge(y_out[s], 16 + B * YI)

        @block.gpsimd
        def _(pool):
            PL = nc.gpsimd
            pool.sem_inc(glo_done, CR)
            pool.sem_inc(v_step, CS)
            for h in range(2):
                PL.memset(hT[h][:, :, 0:PAD], 0.0).then_inc(setup, 1)
                PL.memset(hT[h][:, :, PAD + P:YP], 0.0).then_inc(setup, 1)

            def clear_pads(n):
                for i in range(2):
                    pool.wait_ge(y_out[i], (n - 1) * YI + (YI // 2 + 16))
                pool.wait_ge(xp_ready, (n - 1) * NCH + (NCH + C2))
                pool.sem_inc(passed["pool"], 1)
                for h in range(2):
                    PL.memset(hT[h][:, :, 0:PAD], 0.0).then_inc(pads, 1)
                    PL.memset(hT[h][:, :, PAD + P:YP], 0.0).then_inc(pads, 1)

            def phase_a(n):
                pool.wait_ge(fc_pe, n * 5 + 1)
                pool.sem_inc(passed["pool"], 1)
                PL.memset(relu_lo[:, :], 0.0).then_inc(sum_step, 1)
                with pool.Fori(0, NCH) as c:
                    for h in range(2):
                        if h == 0:
                            pool.wait_ge(hi_done, n * NCH + (c + 1))
                        else:
                            pool.wait_ge(lo_done, n * NCH + (c + 1 + C2))
                        pool.sem_inc(passed["pool"], 1)
                        pool.wait_ge(sum_step, n * SS + c * 2 + (1 + h))
                        PL.tensor_tensor(relu_lo[:, :].rearrange("p (y c) -> p y c", y=ROWS),
                                         relu_lo[:, :].rearrange("p (y c) -> p y c", y=ROWS),
                                         hT[h][:, :, bass.ds(c * ROWS + PAD, ROWS)].rearrange("p c y -> p y c"), ALU.add)\
                            .then_inc(sum_step, 1)

            def load_taps(n, c, i):
                pool.wait_ge(v_step, n * VS + c * 6 + (3 * i + 1))
                pool.sem_inc(passed["pool"], 1)
                pool.dma_start(vbase[i][:], t["taps"][:, bass.ds((c * 2 + i) * VCH, VCH), :, :]).then_inc(v_in[i], 16)

            def split_taps(n, c, i, more=True):
                step = n * VS + c * 6 + 3 * i
                if more:
                    load_taps(n, c + i, 1 - i)
                pool.wait_ge(v_in[i], n * (16 * NV // 2) + c * 16 + 16)
                pool.wait_ge(v_step, step + CS)
                pool.sem_inc(passed["pool"], 1)
                PL.tensor_tensor(vsum[:], vbase[i][:], shifts[:].unsqueeze(1).to_broadcast([P, VCH, TSLOTS, PERIOD]),
                                 ALU.add).then_inc(v_step, 1)
                pool.wait_ge(t_ready, n * P + c * (2 * VCH) + (i * VCH + CV - VCH))
                pool.wait_ge(v_step, step + CS + 1)
                pool.sem_inc(passed["pool"], 1)
                PL.tensor_copy(vhl[i][0][:], vsum[:]).then_inc(v_step, 1)
                pool.wait_ge(v_step, step + CS + 2)
                PL.tensor_tensor(vhl[i][1][:], vsum[:], vhl[i][0][:], ALU.subtract).then_inc(v_step, 1)

            def add_block(n, j, s):
                pool.wait_ge(mix_out, (n - 1) * NCH + j * 4 + (s + 1 + C2))
                pool.wait_ge(x_in[s], n * XI + j * 16 + (XI1 + 16))
                PL.tensor_tensor(yst[s % 2][:], yst[s % 2][:], xr[s][:], ALU.add).then_inc(x_used, 1)

            def phase_c(n, mix):
                load_taps(n, 0, 0)
                pool.wait_ge(fc_dve, n * FD + SHIFTS)
                pool.sem_inc(passed["pool"], 1)
                split_taps(n, 0, 0)
                split_taps(n, 0, 1)
                with pool.Fori(0, J4 - 1) as j:
                    for i in range(2):
                        split_taps(n, j * 2 + (i + 1), 0)
                        split_taps(n, j * 2 + (i + 1), 1)
                        if mix:
                            add_block(n, j, 2 * i)
                            add_block(n, j, 2 * i + 1)
                split_taps(n, NV // 2 - 1, 0)
                split_taps(n, NV // 2 - 1, 1, more=False)
                if mix:
                    for s in range(4):
                        add_block(n, J4 - 1, s)

            def phase_d(n):
                with pool.Fori(0, J4) as j:
                    for s in range(4):
                        pool.wait_ge(gh_done, n * NCH + j * 4 + (s + 1))
                        PL.tensor_tensor(glo[s % 2], gl[s], gh[s % 2], ALU.subtract).then_inc(glo_done, 1)

            phase_a(0)
            phase_c(0, False)
            phase_d(0)
            with pool.Fori(1, B) as n:
                clear_pads(n)
                phase_a(n)
                phase_c(n, True)
                phase_d(n)
            with pool.Fori(0, J4) as j:
                for s in range(4):
                    add_block(B, j, s)

        @block.scalar
        def _(act):
            S = nc.scalar
            for s in range(4):
                act.sem_inc(g_out[s], 16)
            for s in range(2):
                act.sem_inc(y_out[s], 16)
            act.sem_inc(ha_out, C2)
            act.sem_inc(conv_out, CR)
            act.sem_inc(mix_out, C2)
            act.wait_ge(consts_in, 16 * (len(names) + 2))
            S.copy(wo16[:, :], woT).then_inc(setup, 1)
            act.wait_ge(setup, SETUP)

            def flat(ap):
                return ap.rearrange("p m c -> p (m c)")

            def high_input(n, j, s):
                act.wait_ge(x_in[s], n * XI + j * 16 + 16)
                for h in range(KH):
                    ins = S.activation(xh[s % 2][:, h, :], xr[s][:, h, :], ACT.Identity,
                                       accum_out=xs[:, h, bass.ds(j * 4 + s, 1)])
                ins.then_inc(xh_done, 1)

            def relu_chunk(n, j, s):
                g = s % 2
                act.wait_ge(ha_ready, n * NCH + j * 4 + (s + 1))
                act.wait_ge(ha_out, n * NCH + j * 4 + (s + 1))
                S.activation(relu_out[:, g, :], ps[g][:, :], ACT.Relu, bias=k["b1col"][:, 1:2], scale=1.0 / PW1_SCALE,
                             accum_out=relu_hi[:, bass.ds(j * 4 + s, 1)]).then_inc(ha_out, 1)
                act.wait_ge(hb_ready, n * NCH + j * 4 + (s + 1 + CX))
                S.activation(
                    hT[0][:, :, bass.ds((j * 4 + s) * ROWS + PAD, ROWS)].rearrange("p c y -> p y c"),
                    ps[2 + g][:, :].rearrange("p (y c) -> p y c", y=ROWS), ACT.Relu).then_inc(hi_done, 1)

            def phase_a(n):
                with act.Fori(0, J4 - 1) as j:
                    for s in range(4):
                        relu_chunk(n, j, s)
                        high_input(n, j + (s + 2) // 4, (s + 2) % 4)
                for s in range(4):
                    relu_chunk(n, J4 - 1, s)
                    if s < 2:
                        high_input(n, J4 - 1, s + 2)

            def phase_b(n):
                act.wait_ge(fc_dve, n * FD + OFFSETS)
                S.activation(offt[:, :], off[:, :], ACT.Tanh).then_inc(fc_act, 1)
                act.wait_ge(fc_act, n * FA + 1)
                S.activation(th[:, 0:3], offt[:, 0:3], ACT.Tanh, scale=0.5).then_inc(fc_act, 1)
                S.activation(th[:, 3:6], offt[:, 3:6], ACT.Tanh).then_inc(fc_act, 1)

            def mix_group(n, j, g):
                act.wait_ge(mix_ready, (n - 1) * NCH + j * 4 + (g + 1))
                act.wait_ge(y_out[g % 2], (n - 1) * YI + j * 32 + (YI // 2 + 16 * (g // 2 + 1)))
                for h in range(KH):
                    ins = S.copy(yst[g % 2][:, h, :], ps[4 + 2 * (g % 2) + h][:, :])
                ins.then_inc(mix_out, 1)

            def phase_c(n, mix):
                with act.Fori(0, J4) as j:
                    for g in range(4):
                        for s in range(4):
                            act.wait_ge(conv_ready, n * P + j * 16 + (4 * g + s + 1 + CR))
                            act.wait_ge(g_out[s], n * (16 * P // 4) + j * 64 + 16 * (g + 1))
                            S.copy(gst[s], ps[s][:, 0:OUT3]).then_inc(conv_out, 1)
                        if mix:
                            mix_group(n, j, g)

            def phase_d(n):
                act.wait_ge(g_early, n * 16 + 16)
                act.sem_inc(passed["act"], 1)
                with act.Fori(0, J4) as j:
                    for s in range(4):
                        g = s % 2
                        act.wait_ge(g_in[s], n * (16 * NCH // 4) + j * 16 + 16)
                        act.wait_ge(pw_ready, n * NCH + j * 4 + (s + 1))
                        S.copy(gh[g], gl[s]).then_inc(gh_done, 1)
                        act.wait_ge(x_in[s], n * XI + j * 16 + (2 * XI1 + 16))
                        for h in range(KH):
                            S.activation(xr[s][:, h, :], xr[s][:, h, :], ACT.Identity,
                                         bias=k["pwb"][:, h:h + 1]).then_inc(xb_done, 1)

            def phase_e1(n):
                for g in range(0, 8, 2):
                    act.wait_ge(l_pe, n * LP + (g + 1))
                    S.copy(flat(f1[:, 2 * g:2 * g + 2, :]), ps[g % 4][:, :]).then_inc(l_act, 1)
                for g in range(4):
                    act.wait_ge(l_pe, n * LP + (9 + 2 * g))
                    S.copy(flat(f2[:, 0, 4 * g:4 * g + 4, :]), ps[4 + g % 2][:, :]).then_inc(l_act, 1)

            def magnitudes(n):
                act.wait_ge(l_act, n * LA + 8)
                act.wait_ge(l_pe, n * LP + 16)
                S.activation(mag_a, flat(f2[:, 0, :, :]), ACT.Square).then_inc(l_act, 1)
                act.wait_ge(l_dve, n * LD + 10)
                S.activation(mag_b, mag_a, ACT.Sqrt).then_inc(l_act, 1)

            def columns_back(n, g):
                act.wait_ge(l_pe, n * LP + (19 + g))
                S.copy(flat(f1[:, 2 * g:2 * g + 2, :]), ps[g % 4][:, :]).then_inc(l_act, 1)

            def rows_back(n):
                for g in range(4):
                    act.wait_ge(l_pe, n * LP + (27 + g))
                    S.copy(flat(enh_hl[:, 0, 4 * g:4 * g + 4, :]), ps[4 + g % 3][:, :]).then_inc(l_act, 1)

            high_input(0, 0, 0)
            high_input(0, 0, 1)
            phase_a(0)
            phase_b(0)
            phase_c(0, False)
            phase_d(0)
            phase_e1(0)
            with act.Fori(1, B) as n:
                high_input(n, 0, 0)
                high_input(n, 0, 1)
                magnitudes(n - 1)
                for i in range(2):
                    act.wait_ge(y_out[i], (n - 1) * YI + (YI // 2 + 16))
                act.sem_inc(passed["act"], 1)
                phase_a(n)
                for g in range(5):
                    columns_back(n - 1, g)
                phase_b(n)
                for g in range(5, 8):
                    columns_back(n - 1, g)
                rows_back(n - 1)
                phase_c(n, True)
                phase_d(n)
                phase_e1(n)
            magnitudes(B - 1)
            for g in range(8):
                columns_back(B - 1, g)
            rows_back(B - 1)
            with act.Fori(0, J4) as j:
                for g in range(4):
                    mix_group(B, j, g)

        @block.vector
        def _(dve):
            V = nc.vector
            dve.sem_inc(x_used, CX)
            dve.sem_inc(lo_done, C2)
            dve.sem_inc(t_ready, CV)
            dve.sem_inc(xp_out, C2)
            V.memset(ones[:, :], 1.0).then_inc(setup, 1)
            V.memset(ones16[:, :], 1.0).then_inc(setup, 1)
            V.memset(zeros16[:, :], 0.0).then_inc(setup, 1)
            V.memset(hp[:, :], 0.0).then_inc(setup, 1)
            V.memset(bias_hl[:, :], 0.0).then_inc(setup, 1)
            dve.wait_ge(setup, SETUP - 7)
            V.tensor_scalar(b1h, b1row, PW1_SCALE, None, ALU.mult).then_inc(setup, 1)
            V.tensor_scalar(w1h[:, :, :], k["w1T"][:], PW1_SCALE, None, ALU.mult).then_inc(setup, 1)
            dve.wait_ge(setup, SETUP - 5)
            V.tensor_copy(bias_hl[0:1, :], b1h[0:1, :]).then_inc(setup, 1)
            V.scalar_tensor_tensor(out=bias_hl[BL:BL + 1, :], in0=b1row[BL:BL + 1, :], scalar=PW1_SCALE,
                                   in1=b1h[BL:BL + 1, :], op0=ALU.mult, op1=ALU.subtract).then_inc(setup, 1)
            V.scalar_tensor_tensor(out=w1l[:, :, :], in0=k["w1T"][:], scalar=PW1_SCALE, in1=w1h[:, :, :],
                                   op0=ALU.mult, op1=ALU.subtract).then_inc(setup, 1)
            V.tensor_copy(wol[0:2 * M, :], wo16[0:2 * M, :]).then_inc(setup, 1)
            V.tensor_tensor(wol[2 * M:3 * M, :], woT[2 * M:3 * M, :], wo16[2 * M:3 * M, :], ALU.subtract)\
                .then_inc(setup, 1)

            def flat(ap):
                return ap.rearrange("p m c -> p (m c)")

            def histogram_piece(n, jj, i):
                piece = magm[:, bass.ds((jj * 4 + i) * OHU, OHU)]
                dve.wait_ge(hist_done, n * NOH + jj * 4 + (i + 1))
                V.tensor_copy(ms[i % 2][:, :, 0], piece).then_inc(ms_done, 1)
                dve.wait_ge(ms_done, n * (2 * NOH) + jj * 8 + (2 * i + 1))
                V.tensor_tensor(ms[i % 2][:, :, 1], piece, ms[i % 2][:, :, 0], ALU.subtract).then_inc(ms_done, 1)

            def low_input(n, j, s):
                dve.wait_ge(xh_done, n * NCH + j * 4 + (s + 1))
                V.tensor_tensor(xl[s % 2], xr[s][:], xh[s % 2], ALU.subtract).then_inc(x_used, 1)

            def chunk(n, jj, i, more=True):
                dve.wait_ge(hi_done, n * NCH + jj * 8 + (i + 1))
                rows = bass.ds((jj * 8 + i) * ROWS + PAD, ROWS)
                V.scalar_tensor_tensor(
                    out=hT[1][:, :, rows].rearrange("p c y -> p y c"),
                    in0=ps[2 + i % 2][:, :].rearrange("p (y c) -> p y c", y=ROWS), scalar=0.0,
                    in1=hT[0][:, :, rows].rearrange("p c y -> p y c"),
                    op0=ALU.max, op1=ALU.subtract).then_inc(lo_done, 1)
                if more:
                    low_input(n, jj * 2 + (i + 2) // 4, (i + 2) % 4)

            def phase_a(n, enhance):
                if not enhance:
                    with dve.Fori(0, J4 // 2 - 1) as jj:
                        for i in range(8):
                            chunk(n, jj, i)
                    for i in range(8):
                        chunk(n, J4 // 2 - 1, i, more=i < 6)
                    return
                with dve.Fori(0, NOH // 4) as jj:
                    for i in range(8):
                        if i % 2 == 0:
                            histogram_piece(n - 1, jj, i // 2)
                        chunk(n, jj, i)
                for c in range(NCH // 2, NCH):
                    chunk(n, c // 8, c % 8, more=c < NCH - 2)
                    if c == HALF:
                        histogram_out(n - 1)
                    if c == HALF + 2:
                        smooth(n - 1)
                    if c == HALF + 3:
                        find_peaks(n - 1)
                    if c == HALF + 4:
                        candidates(n - 1)
                    if c == HALF + 5:
                        take_largest(n - 1, 0)
                    if c == HALF + 6:
                        take_largest(n - 1, 1)
                    if c == HALF + 7:
                        single_peak(n - 1)
                    if c == HALF + 10:
                        near_peak(n - 1, 0)
                    if c == HALF + 11:
                        near_peak(n - 1, 1)
                    if c == HALF + 12:
                        gain_map(n - 1)
                    if c >= HALF + 12:
                        apply_gain(n - 1, c - HALF - 12)

            def phase_b(n):
                steps = [0]

                def step(ins):
                    steps[0] += 1
                    ins.then_inc(fc_dve, 1)

                def fc(ins):
                    step(ins)
                    dve.wait_ge(fc_dve, n * FD + steps[0])

                def fc_products(i):
                    dve.wait_ge(fc_pe, n * 5 + (i + 1))

                dve.wait_ge(xh_done, n * NCH + NCH)
                fc(V.tensor_reduce(xsum[:, :], xs[:, :, :], AX.X, ALU.add))
                fc_products(1)
                fc(V.scalar_tensor_tensor(out=gap[:, :], in0=ps[7][:, 0:KH], scalar=1.0 / PIX, in1=k["b1col"][:],
                                          op0=ALU.mult, op1=ALU.add))
                fc_products(2)
                fc(V.tensor_tensor(hid_raw[:, :], ps[7][:, KH:KH + HID // P], k["fc1b"][:], ALU.add))
                fc(V.tensor_scalar(hid[:, :], hid_raw[:, :], 0.0, None, ALU.max))
                for i in range(HID // P):
                    fc(V.tensor_scalar(hidb[:, i, :], ones[:, :], hid[:, i:i + 1], None, ALU.mult))
                assert steps[0] == 8, steps
                dve.wait_ge(ha_out, n * NCH + (NCH + C2))
                fc(V.tensor_reduce(g2[:, 1:2], relu_hi[:, :], AX.X, ALU.add))
                fc_products(3)
                step(V.tensor_scalar(g2s[:, 0:1], ps[7][:, 6:7], 1.0 / (PW1_SCALE * PIX), None, ALU.mult))
                fc(V.tensor_scalar(g2s[:, 1:2], g2[:, 1:2], 1.0 / PIX, None, ALU.mult))
                for i in range(KH):
                    fc(V.tensor_scalar(g2b[:, i, :], ones[:, :], g2s[:, i:i + 1], None, ALU.mult))
                assert steps[0] == 13, steps
                fc_products(4)
                fc(V.tensor_tensor(z, ps[7][:, 2 * P:2 * P + C], k["fc2bB"][:], ALU.add))
                fc(V.tensor_scalar(zm, z, SATURATED, None, ALU.min))
                fc(V.tensor_tensor(zd, zm[:, 0:P], k["ident"][:], ALU.mult))
                fc(V.tensor_reduce(zc[:, :], zd, AX.X, ALU.add))
                fc(V.tensor_scalar(gt, zm, zc[:, 0:1], None, ALU.is_gt))
                fc(V.tensor_scalar(eq, zm, zc[:, 0:1], None, ALU.is_equal))
                fc(V.tensor_tensor(eq, eq, k["lower"][:], ALU.mult))
                fc(V.tensor_tensor(gt, gt, eq, ALU.add))
                fc(V.tensor_reduce(rank[:, :], gt, AX.X, ALU.add))
                fc(V.tensor_scalar(mask[:, :], rank[:, :], float(P) - 0.5, None, ALU.is_lt))
                fc_products(5)
                fc(V.tensor_tensor(off[:, :], ps[7][:, 8:14], k["offbB"][:], ALU.add))
                assert steps[0] == OFFSETS, steps
                dve.wait_ge(fc_act, n * FA + FA)
                fc(V.tensor_scalar(s1p[:, :], th[:, 0:3], 0.5, 1.5, ALU.mult, ALU.add))
                fc(V.reciprocal(rs[:, :], s1p[:, :]))
                fc(V.tensor_tensor(rq[:, :], th[:, 3:6], rs[:, :], ALU.mult))
                at = 0
                for q, rows_q in (3, 3), (2, 2), (1, 2):
                    step(V.tensor_copy(R[:, at:at + rows_q * q].rearrange("p (a q) -> p a q", q=q),
                                       rq[:, 0:q].unsqueeze(1).to_broadcast([P, rows_q, q])))
                    at += rows_q * q
                dve.wait_ge(fc_dve, n * FD + steps[0])
                fc(V.tensor_tensor(shifts[:], R[:, :].unsqueeze(2).to_broadcast([P, TSLOTS, PERIOD]), k["istap"][:], ALU.mult))
                assert steps[0] == SHIFTS, steps
                fc(V.tensor_scalar(sc[:, :], s1p[:, :], mask[:, 0:1], PW_SCALE, ALU.mult, ALU.mult))
                for q in range(3):
                    step(V.tensor_scalar(pwm[:, q, :], k["pwT"][:, q, :], sc[:, q:q + 1], None, ALU.mult))
                dve.wait_ge(fc_dve, n * FD + steps[0])
                fc(V.tensor_copy(pwh[:, :, :], pwm))
                fc(V.tensor_tensor(pwl[:, :, :], pwm, pwh[:, :, :], ALU.subtract))
                assert steps[0] == FD, steps

            def phase_c(n):
                dve.sem_inc(passed["dve"], 1)
                with dve.Fori(0, NV // 2) as c:
                    for i in range(2):
                        dve.wait_ge(v_step, n * VS + c * 6 + (3 * i + CS + 3))
                        for ci in range(VCH):
                            u = ci % CR
                            dve.wait_ge(conv_ready, n * P + c * (2 * VCH) + (i * VCH + ci + 1))
                            for h in range(2):
                                ins = V.tensor_tensor(
                                    toep[u][h].rearrange("p (t a r) -> p t a r", t=TSLOTS, r=PERIOD),
                                    vhl[i][h][:, ci, :, :].unsqueeze(2).to_broadcast([P, TSLOTS, P // PERIOD, PERIOD]),
                                    k["band"][:].rearrange("p (a r) -> p a r", r=PERIOD).unsqueeze(1)
                                    .to_broadcast([P, TSLOTS, P // PERIOD, PERIOD]), ALU.mult)
                            ins.then_inc(t_ready, 1)

            def phase_d(n):
                def block_sum(j, s):
                    g = s % 2
                    dve.wait_ge(pw_ready, n * NCH + j * 4 + (s + 1 + C2))
                    dve.wait_ge(xb_done, n * (KH * NCH) + j * 8 + KH * (s + 1))
                    if staged(j, s) is yst[g]:
                        dve.wait_ge(y_out[g], n * YI + j * 32 + 16 * (s // 2 + 1))
                    dve.wait_ge(xp_ready, n * NCH + j * 4 + (s + 1))
                    for h in range(KH):
                        ins = V.scalar_tensor_tensor(out=staged(j, s)[:, h, :], in0=ps[2 * g + h][:, :], scalar=1.0 / (PW1_SCALE * PW_SCALE),
                                                     in1=xr[s][:, h, :], op0=ALU.mult, op1=ALU.add)
                    ins.then_inc(x_used, 1)

                def project_out(j, s):
                    dve.wait_ge(xp_ready, n * NCH + j * 4 + (s + 1 + C2))
                    V.tensor_copy(xproj[:, :, bass.ds((j * 4 + s) * ROWS, ROWS)].rearrange("p m y -> p y m"),
                                  ps[4 + s % 2][:, 0:ROWS * M].rearrange("p (y m) -> p y m", y=ROWS)).then_inc(xp_out, 1)

                block_sum(0, 0)
                with dve.Fori(0, J4 - LATE - 1) as j:
                    for s in range(4):
                        block_sum(j + (s + 1) // 4, (s + 1) % 4)
                        project_out(j, s)
                for c in range(NCH - 4 * LATE - 4, NCH):
                    if c < NCH - 1:
                        block_sum((c + 1) // 4, (c + 1) % 4)
                    project_out(c // 4, c % 4)

            done = [0]

            def st(n, ins):
                done[0] += 1
                ins.then_inc(l_dve, 1)

            def link(n, ins):
                st(n, ins)
                dve.wait_ge(l_dve, n * LD + done[0])

            def phase_e1(n):
                done[0] = 0
                for g in range(1, 8, 2):
                    dve.wait_ge(l_pe, n * LP + (g + 1))
                    st(n, V.tensor_copy(flat(f1[:, 2 * g:2 * g + 2, :]), ps[g % 4][:, :]))
                for g in range(4):
                    dve.wait_ge(l_pe, n * LP + (10 + 2 * g))
                    st(n, V.tensor_copy(flat(f2[:, 1, 4 * g:4 * g + 4, :]), ps[6 + g % 2][:, :]))

            def magnitudes(n):
                done[0] = 8
                dve.wait_ge(l_dve, n * LD + 8)
                dve.wait_ge(l_pe, n * LP + 16)
                link(n, V.tensor_tensor(mag_b, flat(f2[:, 1, :, :]), flat(f2[:, 1, :, :]), ALU.mult))
                dve.wait_ge(l_act, n * LA + 9)
                link(n, V.tensor_tensor(mag_a, mag_a, mag_b, ALU.add))
                dve.wait_ge(l_act, n * LA + 10)
                link(n, V.tensor_reduce(mag[:, :], mag_b.rearrange("p (m u) -> p u m", m=M), AX.X, ALU.add))
                link(n, V.tensor_tensor(magm[:, :], mag[:, :], k["high16"][:], ALU.mult))
                dve.sem_inc(passed["dve"], 1)

            N = NBINS
            e, ra, rb, rc = (bins[:, i, :] for i in range(4))
            es = e[:, 1:N + 1]
            a_, b_, oh1 = bins[:, 4, 0:N], bins[:, 5, 0:N], bins[:, 6, 0:N]
            p1, msk, key = ra[:, 0:N], rb[:, 0:N], rc[:, 0:N]
            BIG = 1.0e30

            def histogram_out(n):
                done[0] = 12
                dve.wait_ge(hist_done, n * NOH + (NOH + C2))
                link(n, V.tensor_copy(h2[:, :], ps[4][0:2, 0:NBINS]))

            def smooth(n):
                dve.wait_ge(l_pe, n * LP + 17)
                link(n, V.tensor_copy(hp[:, 1:NBINS + 1], ps[5][0:1, 0:NBINS]))
                link(n, V.tensor_scalar(a_, hp[:, 0:N], 0.25, None, ALU.mult))
                link(n, V.scalar_tensor_tensor(out=b_, in0=hp[:, 1:N + 1], scalar=0.5, in1=a_, op0=ALU.mult, op1=ALU.add))
                link(n, V.scalar_tensor_tensor(out=es, in0=hp[:, 2:N + 2], scalar=0.25, in1=b_, op0=ALU.mult, op1=ALU.add))
                link(n, V.tensor_copy(e[:, 0:1], e[:, N:N + 1]))
                link(n, V.tensor_copy(e[:, N + 1:N + 2], e[:, 1:2]))

            def find_peaks(n):
                link(n, V.tensor_reduce(pc[:, 0:1], es, AX.X, ALU.add))
                link(n, V.tensor_scalar(pc[:, 1:2], pc[:, 0:1], 1.0 / N, None, ALU.mult))
                link(n, V.tensor_scalar(p1, es, pc[:, 1:2], None, ALU.is_gt))
                link(n, V.tensor_tensor(a_, es, e[:, 0:N], ALU.is_gt))
                link(n, V.tensor_tensor(b_, es, e[:, 2:N + 2], ALU.is_gt))
                link(n, V.tensor_tensor(p1, p1, a_, ALU.mult))
                link(n, V.tensor_tensor(p1, p1, b_, ALU.mult))

            def candidates(n):
                link(n, V.tensor_reduce(pc[:, 2:3], p1, AX.X, ALU.add))
                link(n, V.tensor_scalar(pc[:, 3:4], pc[:, 2:3], 0.5, None, ALU.is_lt))
                link(n, V.tensor_scalar(p1, p1, pc[:, 3:4], None, ALU.max))
                link(n, V.tensor_scalar(a_, p1, 1.0, BIG, ALU.subtract, ALU.mult))
                link(n, V.tensor_tensor(b_, p1, es, ALU.mult))
                link(n, V.tensor_tensor(msk, b_, a_, ALU.add))

            def take_largest(n, i):
                link(n, V.tensor_reduce(pc[:, 4 + i:5 + i], msk, AX.X, ALU.max))
                link(n, V.tensor_scalar(a_, msk, pc[:, 4 + i:5 + i], None, ALU.is_equal))
                link(n, V.scalar_tensor_tensor(out=key, in0=a_, scalar=-1000.0, in1=k["binrow"][:], op0=ALU.mult, op1=ALU.add))
                link(n, V.tensor_reduce(pc[:, 6 + i:7 + i], key, AX.X, ALU.min))
                link(n, V.tensor_scalar(oh1, key, pc[:, 6 + i:7 + i], None, ALU.is_equal))
                link(n, V.tensor_tensor(b_, oh1, k["centers"][:], ALU.mult))
                link(n, V.tensor_reduce(pc[:, 8 + i:9 + i], b_, AX.X, ALU.add))
                if i == 0:
                    link(n, V.scalar_tensor_tensor(out=msk, in0=oh1, scalar=-2.0 * BIG, in1=msk, op0=ALU.mult, op1=ALU.add))

            def single_peak(n):
                link(n, V.tensor_scalar(pc[:, 10:11], pc[:, 2:3], 1.5, None, ALU.is_gt))
                link(n, V.tensor_scalar(pc[:, 11:12], pc[:, 10:11], -1.0, 1.0, ALU.mult, ALU.add))
                link(n, V.tensor_tensor(pc[:, 12:13], pc[:, 8:9], pc[:, 11:12], ALU.mult))
                link(n, V.scalar_tensor_tensor(out=pc[:, 9:10], in0=pc[:, 9:10], scalar=pc[:, 10:11], in1=pc[:, 12:13],
                                               op0=ALU.mult, op1=ALU.add))
                assert done[0] == 51, done

            def near_peak(n, i):
                if i == 0:
                    dve.wait_ge(l_pe, n * LP + 18)
                    link(n, V.tensor_copy(pkb[:, :], ps[6][:, 0:2]))
                link(n, V.tensor_scalar(gn[:, 2, :], k["theta"][:], pkb[:, i:i + 1], None, ALU.subtract))
                link(n, V.scalar_tensor_tensor(out=gn[:, 3, :], in0=gn[:, 2, :], scalar=-1.0, in1=gn[:, 2, :],
                                               op0=ALU.mult, op1=ALU.max))
                link(n, V.tensor_scalar(gn[:, 2, :], gn[:, 3, :], -1.0, float(np.float32(np.pi)), ALU.mult, ALU.add))
                link(n, V.tensor_tensor(gn[:, 3, :], gn[:, 3, :], gn[:, 2, :], ALU.min))
                link(n, V.tensor_scalar(gn[:, i, :], gn[:, 3, :], float(np.float32(np.radians(15.0))), None, ALU.is_le))

            def gain_map(n):
                link(n, V.tensor_tensor(gn[:, 2, :], gn[:, 0, :], gn[:, 1, :], ALU.max))
                link(n, V.tensor_tensor(gn[:, 3, :], gn[:, 2, :], k["gain_d"][:], ALU.mult))
                link(n, V.tensor_tensor(gain[:, :], gn[:, 3, :], k["gain_lo"][:], ALU.add))

            def apply_gain(n, q):
                maps = f2[:, :, q * (M // 4):(q + 1) * (M // 4), :]
                st(n, V.tensor_tensor(maps, maps, gain[:, :].unsqueeze(1).unsqueeze(1).to_broadcast([P, 2, M // 4, P]),
                                      ALU.mult))

            def rows_back(n):
                assert done[0] == 69, done
                for g in range(4):
                    dve.wait_ge(l_act, n * LA + (19 + g))
                    st(n, V.tensor_tensor(flat(enh_hl[:, 1, 4 * g:4 * g + 4, :]), ps[4 + g % 3][:, :],
                                          flat(enh_hl[:, 0, 4 * g:4 * g + 4, :]), ALU.subtract))
                assert done[0] == LD, done

            low_input(0, 0, 0)
            low_input(0, 0, 1)
            phase_a(0, False)
            dve.wait_ge(x_used, CX + NCH)
            dve.sem_inc(x_used, NCH)
            phase_b(0)
            phase_c(0)
            phase_d(0)
            phase_e1(0)
            with dve.Fori(1, B) as n:
                low_input(n, 0, 0)
                low_input(n, 0, 1)
                magnitudes(n - 1)
                phase_a(n, True)
                phase_b(n)
                rows_back(n - 1)
                phase_c(n)
                phase_d(n)
                phase_e1(n)
            magnitudes(B - 1)
            with dve.Fori(0, NOH // 4) as jj:
                for i in range(4):
                    histogram_piece(B - 1, jj, i)
            dve.sem_inc(x_used, NCH)
            histogram_out(B - 1)
            smooth(B - 1)
            find_peaks(B - 1)
            candidates(B - 1)
            take_largest(B - 1, 0)
            take_largest(B - 1, 1)
            single_peak(B - 1)
            near_peak(B - 1, 0)
            near_peak(B - 1, 1)
            gain_map(B - 1)
            for q in range(4):
                apply_gain(B - 1, q)
            rows_back(B - 1)

        @block.tensor
        def _(pe):
            T = nc.tensor
            pe.sem_inc(hb_ready, CX)
            pe.sem_inc(conv_ready, CR)
            pe.sem_inc(pw_ready, C2)
            pe.sem_inc(xp_ready, C2)
            pe.sem_inc(hist_done, C2)
            pe.sem_inc(fc_pe, 1)
            pe.wait_ge(setup, SETUP)

            def histogram_piece(n, jj, i):
                pe.wait_ge(ms_done, n * (2 * NOH) + jj * 8 + 2 * (i + 1))
                pe.wait_ge(oh_in[i % 2], n * (16 * NOH // 2) + jj * 32 + 16 * (i // 2 + 1))
                for u in range(OHU):
                    mm = T.matmul(ps[4][0:2, 0:NBINS], ms[i % 2][:, u, :], onehot[i % 2][:, u, :], start=False, stop=False,
                                  skip_group_check=True)
                mm.then_inc(hist_done, 1)

            def start_histogram():
                pe.sem_inc(passed["pe"], 1)
                T.matmul(ps[4][0:2, 0:NBINS], ones16[0:1, 0:2], zeros16[:, :], start=True, stop=False, skip_group_check=True)

            def chunk(n, jj, i):
                g = i % 2
                pe.wait_ge(xh_done, n * NCH + jj * 8 + (i + 1))
                pe.wait_ge(ha_out, n * NCH + jj * 8 + (i + 1))
                for w in (w1h, w1l):
                    for h in range(KH):
                        T.matmul(ps[g][:, :], w[:, h, P:C], xh[g][:, h, :], start=(w is w1h and h == 0), stop=False,
                                 skip_group_check=True)
                pe.wait_ge(x_used, n * XQ + jj * 8 + (i + 1 + CX))
                pe.sem_inc(passed["pe"], 1)
                for h in range(KH):
                    mm = T.matmul(ps[g][:, :], w1h[:, h, P:C], xl[g][:, h, :], start=False, stop=(h == KH - 1),
                                  skip_group_check=True)
                mm.then_inc(ha_ready, 1)
                pe.wait_ge(lo_done, n * NCH + jj * 8 + (i + 1))
                T.matmul(ps[2 + g][:, :], ones16[0:BL + 1, :], bias_hl[:, :], start=True, stop=False, skip_group_check=True)
                for r in range(ROWS):
                    for h in range(KH):
                        for part, w in ((xh, w1h), (xh, w1l), (xl, w1h)):
                            mm = T.matmul(ps[2 + g][:, r * P:(r + 1) * P], part[g][:, h, r * P:(r + 1) * P], w[:, h, 0:P],
                                          start=False, stop=(r == ROWS - 1 and h == KH - 1 and part is xl),
                                          skip_group_check=True)
                mm.then_inc(hb_ready, 1)

            def phase_a(n, enhance):
                if enhance:
                    for c in range(NCH):
                        chunk(n, c // 8, c % 8)
                        if c == 1:
                            pe.wait_ge(ms_done, (n - 1) * (2 * NOH) + 2)
                            start_histogram()
                        if c < HALF and c % 2:
                            histogram_piece(n - 1, c // 8, c % 8 // 2)
                        if c == HALF + 1:
                            histogram_sum(n - 1)
                        if c == HALF + 9:
                            spread_peaks(n - 1)
                else:
                    with pe.Fori(0, J4 // 2) as jj:
                        for i in range(8):
                            chunk(n, jj, i)
                pe.wait_ge(ha_out, n * NCH + (NCH + C2))
                pe.wait_ge(lo_done, n * NCH + (NCH + C2))
                pe.sem_inc(passed["pe"], 1)

            def relu_sums(n):
                pe.wait_ge(sum_step, n * SS + SS)
                pe.wait_ge(fc_dve, n * FD + 3)
                pe.sem_inc(passed["pe"], 1)
                for y in range(ROWS):
                    mm = T.matmul(ps[7][:, 6:7], relu_lo[:, y * P:(y + 1) * P], ones[:, 0:1], start=(y == 0), stop=(y == ROWS - 1))
                mm.then_inc(fc_pe, 1)

            def offset_products(n):
                pe.wait_ge(fc_dve, n * FD + 14)
                for h in range(KH):
                    mm = T.matmul(ps[7][:, 8:14], g2b[:, h, :], k["offT"][:, h, :], start=(h == 0), stop=(h == KH - 1))
                mm.then_inc(fc_pe, 1)

            def mean_products(n):
                pe.wait_ge(fc_dve, n * FD + 1)
                for o in range(KH):
                    for h in range(KH):
                        mm = T.matmul(ps[7][:, o:o + 1], k["w1T"][:, h, o * P:(o + 1) * P], xsum[:, h:h + 1],
                                      start=(h == 0), stop=(h == KH - 1))
                mm.then_inc(fc_pe, 1)

            def fc1_products(n):
                pe.wait_ge(fcw_in, n * 32 + 32)
                pe.wait_ge(fc_dve, n * FD + 2)
                for o in range(HID // P):
                    for h in range(KH):
                        mm = T.matmul(ps[7][:, KH + o:KH + o + 1], fc1T[:, h, o * P:(o + 1) * P], gap[:, h:h + 1],
                                      start=(h == 0), stop=(h == KH - 1))
                mm.then_inc(fc_pe, 1)

            def fc2_products(n):
                pe.wait_ge(fc_dve, n * FD + 10)
                for i in range(HID // P):
                    mm = T.matmul(ps[7][:, 2 * P:2 * P + C], hidb[:, i, :], fc2T[:, i, :], start=(i == 0), stop=(i == HID // P - 1))
                mm.then_inc(fc_pe, 1)

            def mix_group(n, j, g):
                i = g // 2
                pe.wait_ge(e_in[i], (n - 1) * (32 * J4) + j * 32 + 32)
                pe.wait_ge(mix_out, (n - 1) * NCH + j * 4 + (g + 1))
                for h in range(KH):
                    mm = T.matmul(ps[4 + 2 * (g % 2) + h][:, :], wol[:, h * P:(h + 1) * P],
                                  enh_in[i][:, (g % 2) * CHUNK:(g % 2 + 1) * CHUNK], start=True, stop=True)
                mm.then_inc(mix_ready, 1)

            def phase_c(n, mix):
                with pe.Fori(0, J4) as j:
                    for c in range(16):
                        u = c % CR
                        pe.wait_ge(t_ready, n * P + j * 16 + (c + 1 + CV))
                        pe.wait_ge(conv_out, n * P + j * 16 + (c + 1))
                        col = 0
                        for i, (dy, q) in enumerate(TAP_ROWS):
                            for hd, hw in ((0, 0), (0, 1), (1, 0)):
                                mm = T.matmul(ps[u][:, 0:q * P],
                                              hT[hd][:, bass.ds(j * 16 + c, 1), PAD + dy:PAD + dy + P].rearrange("p c y -> p (c y)"),
                                              toep[u][hw][:, col:col + q * P],
                                              start=(i == 0 and hd + hw == 0), stop=(i == len(TAP_ROWS) - 1 and hd == 1),
                                              skip_group_check=True)
                            col += q * P
                        mm.then_inc(conv_ready, 1)
                        if mix and c % 4 == 3:
                            mix_group(n, j, c // 4)

            def phase_d(n):
                def pointwise(j, s):
                    g = s % 2
                    pe.wait_ge(gh_done, n * NCH + j * 4 + (s + 1))
                    pe.wait_ge(x_used, n * XQ + j * 4 + (s + CX + 2 * NCH - 1))
                    parts = [a.rearrange("p (y q x) -> p q y x", y=ROWS, q=3) for a in (gh[g], glo[g])]
                    for i, (w, d) in enumerate(((pwh, 0), (pwl, 0), (pwh, 1))):
                        if d == 1:
                            pe.wait_ge(glo_done, n * NCH + j * 4 + (s + 1 + CR))
                            pe.sem_inc(passed["pe"], 1)
                        for h in range(KH):
                            for q in range(3):
                                mm = T.matmul(ps[2 * g + h][:, :], w[:, q, h * P:(h + 1) * P], parts[d][:, q, :, :],
                                              start=(i == 0 and q == 0), stop=(i == 2 and q == 2), skip_group_check=True)
                    mm.then_inc(pw_ready, 1)

                def project(j, s):
                    g = s % 2
                    pe.wait_ge(x_used, n * XQ + j * 4 + (s + 1 + CX + 2 * NCH))
                    pe.wait_ge(xp_out, n * NCH + j * 4 + (s + 1))
                    for r in range(ROWS):
                        for h in range(KH):
                            mm = T.matmul(ps[4 + g][:, r * M:(r + 1) * M], staged(j, s)[:, h, r * P:(r + 1) * P], k["winT"][:, h, :],
                                          start=(h == 0), stop=(h == KH - 1))
                    mm.then_inc(xp_ready, 1)

                pe.wait_ge(fc_dve, n * FD + FD)
                pointwise(0, 0)
                with pe.Fori(0, J4 - LATE - 1) as j:
                    for s in range(4):
                        pointwise(j + (s + 1) // 4, (s + 1) % 4)
                        project(j, s)
                for c in range(NCH - 4 * LATE - 4, NCH):
                    if c < NCH - 1:
                        pointwise((c + 1) // 4, (c + 1) % 4)
                    project(c // 4, c % 4)

            def phase_e1(n):
                pe.wait_ge(xp_out, n * NCH + (NCH + C2))
                for g in range(8):
                    if g >= 4:
                        pe.wait_ge(l_dve if g % 2 else l_act, n * (LD if g % 2 else LA) + ((g - 4) // 2 + 1))
                    for i in range(2):
                        mm = T.matmul(ps[g % 4][:, i * 2 * P:(i + 1) * 2 * P], xproj[:, 2 * g + i, :], k["dft_fwd"][:],
                                      start=True, stop=True)
                    mm.then_inc(l_pe, 1)
                pe.wait_ge(l_act, n * LA + 4)
                pe.wait_ge(l_dve, n * LD + 4)
                for g in range(4):
                    re, im = (f1[:, 4 * g:4 * g + 4, r * P:(r + 1) * P] for r in range(2))
                    if g >= 2:
                        pe.wait_ge(l_act, n * LA + (5 + g - 2))
                    T.matmul(ps[4 + g % 2][:, :], k["dft_c"][:], re, start=True, stop=False)
                    T.matmul(ps[4 + g % 2][:, :], k["dft_s"][:], im, start=False, stop=True).then_inc(l_pe, 1)
                    if g >= 2:
                        pe.wait_ge(l_dve, n * LD + (5 + g - 2))
                    T.matmul(ps[6 + g % 2][:, :], k["dft_c"][:], im, start=True, stop=False)
                    T.matmul(ps[6 + g % 2][:, :], k["dft_ns"][:], re, start=False, stop=True).then_inc(l_pe, 1)

            def histogram_sum(n):
                pe.wait_ge(l_dve, n * LD + 13)
                pe.sem_inc(passed["pe"], 1)
                T.matmul(ps[5][0:1, 0:NBINS], ones[0:2, 0:1], h2[:, :], start=True, stop=True).then_inc(l_pe, 1)

            def spread_peaks(n):
                pe.wait_ge(l_dve, n * LD + 51)
                pe.sem_inc(passed["pe"], 1)
                T.matmul(ps[6][:, 0:2], ones[0:1, :], pc[:, 8:10], start=True, stop=True).then_inc(l_pe, 1)

            def columns_back(n, g):
                pe.wait_ge(l_dve, n * LD + (66 + g // 2))
                pe.sem_inc(passed["pe"], 1)
                if g >= 4:
                    pe.wait_ge(l_act, n * LA + (11 + g - 4))
                for i in range(2):
                    m = 2 * g + i
                    T.matmul(ps[g % 4][:, i * 2 * P:(i + 1) * 2 * P], f2[:, 0, m, :], k["inv_cs"][:], start=True, stop=False)
                    mm = T.matmul(ps[g % 4][:, i * 2 * P:(i + 1) * 2 * P], f2[:, 1, m, :], k["inv_nsc"][:], start=False, stop=True)
                mm.then_inc(l_pe, 1)

            def rows_back(n):
                pe.wait_ge(l_act, n * LA + 18)
                for g in range(4):
                    if g == 3:
                        pe.wait_ge(l_dve, n * LD + 70)
                    for i in range(4):
                        m = 4 * g + i
                        T.matmul(ps[4 + g % 3][:, i * P:(i + 1) * P], f1[:, m, 0:P], k["inv_c"][:], start=True, stop=False)
                        mm = T.matmul(ps[4 + g % 3][:, i * P:(i + 1) * P], f1[:, m, P:2 * P], k["inv_ns"][:], start=False, stop=True)
                    mm.then_inc(l_pe, 1)

            phase_a(0, False)
            mean_products(0)
            fc1_products(0)
            relu_sums(0)
            fc2_products(0)
            offset_products(0)
            phase_c(0, False)
            phase_d(0)
            phase_e1(0)
            with pe.Fori(1, B) as n:
                phase_a(n, True)
                columns_back(n - 1, 0)
                mean_products(n)
                columns_back(n - 1, 1)
                fc1_products(n)
                columns_back(n - 1, 2)
                relu_sums(n)
                columns_back(n - 1, 3)
                fc2_products(n)
                columns_back(n - 1, 4)
                offset_products(n)
                for g in range(5, 8):
                    columns_back(n - 1, g)
                rows_back(n - 1)
                phase_c(n, True)
                phase_d(n)
                phase_e1(n)
            pe.wait_ge(ms_done, (B - 1) * (2 * NOH) + 2)
            start_histogram()
            with pe.Fori(0, NOH // 4) as jj:
                for i in range(4):
                    histogram_piece(B - 1, jj, i)
            histogram_sum(B - 1)
            spread_peaks(B - 1)
            for g in range(8):
                columns_back(B - 1, g)
            rows_back(B - 1)
            with pe.Fori(0, J4) as j:
                for g in range(4):
                    mix_group(B, j, g)


def geometry():
    f = np.float32
    pi = f(np.pi)
    dy, dx = np.meshgrid(np.arange(-P // 2, P // 2, dtype=f), np.arange(-P // 2, P // 2, dtype=f), indexing="ij")
    angle = np.arctan2(dy.astype(np.float64), dx)
    theta = (angle.astype(f) + pi).astype(f)
    high = np.sqrt(dy * dy + dx * dx) > f(0.3 * (P // 2))
    step = (np.arange(NBINS, dtype=f) / f(NBINS)).astype(f)
    edges = np.concatenate([pi * step, [pi]]).astype(f)
    folded = np.mod((angle + np.pi).astype(f), pi)
    bins = np.clip(np.searchsorted(edges, folded.reshape(-1), side="left") - 1, 0, NBINS - 1).reshape(P, P)
    order = (np.arange(P) + P // 2) % P
    theta, high, bins = (a[np.ix_(order, order)] for a in (theta, high, bins))
    onehot = (bins[:, :, None] == np.arange(NBINS)).astype(np.float16)
    lo = np.where(high, f(0.8), f(1.0)).astype(f)
    hi = np.where(high, f(1.2), f(1.0)).astype(f)
    return {"theta": theta, "gain_lo": lo, "gain_d": (hi - lo).astype(f), "high16": high.astype(f) / f(M),
            "onehot": onehot, "binrow": np.arange(NBINS, dtype=f)[None],
            "centers": ((edges[:-1] + edges[1:]) * f(0.5)).astype(f)[None]}


def tables():
    g = np.arange(P)
    a = 2 * np.pi * np.outer(g, g) / P
    c, s = np.cos(a), np.sin(a)
    out = {"dft_fwd": np.concatenate([c, -s], 1) / P, "dft_c": c, "dft_s": s, "dft_ns": -s,
           "inv_cs": np.concatenate([c, s], 1), "inv_nsc": np.concatenate([-s, c], 1), "inv_c": c / P, "inv_ns": -s / P,
           "ident": np.eye(P), "lower": (np.arange(C)[None, :] < g[:, None])}
    out = {name: np.ascontiguousarray(v, dtype=np.float32) for name, v in out.items()}
    out["band"] = (np.abs(g[:, None] - g[None, :]) <= PAD).astype(np.float16)
    out["istap"] = tap_rows([np.ones((P, 1, size, size), np.float32) for size in (7, 5, 3)])[:, 0]
    out.update(geometry())
    return out


def halves(a):
    return np.ascontiguousarray(np.swapaxes(a.reshape((-1, P) + a.shape[1:]), 0, 1))


def tap_rows(dws):
    padded = []
    for dw in dws:
        size = dw.shape[-1]
        full = np.zeros((P, 2 * PAD + 1, PERIOD), np.float32)
        m = PAD - size // 2
        full[:, m:m + size, m:m + size] = dw[:P, 0]
        padded.append(full)
    rows = np.stack([padded[q][:, PAD + dy] for dy, kinds in TAP_ROWS for q in range(kinds)], 1)
    index = (np.arange(P)[:, None] - np.arange(PERIOD)[None, :] + PAD) % PERIOD
    return np.ascontiguousarray(np.moveaxis(rows[:, :, index], 2, 0))


def kernel(**inputs):
    import concourse.bacc as bacc
    from concourse.bass_utils import run_bass_kernel_spmd

    a = {name: np.asarray(v) for name, v in inputs.items()}
    L0 = "L0_conv_"
    order = [4, 2, 0, 5, 3, 1]
    pw = a[L0 + "pw_w"][:, :3 * P].reshape(C, 3, P)[:, ::-1]
    arrays = {
        "x": a["x"].reshape(B, KH, P, PIX),
        "w1T": halves(a[L0 + "pw1_w"].T), "b1col": halves(a[L0 + "pw1_b"]),
        "b1row": np.tile(a[L0 + "pw1_b"][:P], (BL + 1, ROWS)),
        "fc1T": halves(a[L0 + "fc1_w"].T), "fc1b": halves(a[L0 + "fc1_b"]),
        "fc2T": halves(a[L0 + "fc2_w"].T), "fc2bB": np.tile(a[L0 + "fc2_b"][None], (P, 1)),
        "offT": halves(a[L0 + "off_w"][order].T), "offbB": np.tile(a[L0 + "off_b"][order][None], (P, 1)),
        "pwT": np.transpose(pw, (2, 1, 0)), "pwb": halves(a[L0 + "pw_b"]),
        "winT": halves(a["L1_conv_w_in"].T), "woT": np.tile(a["L1_conv_w_out"].T, (3, 1)),
        "taps": tap_rows([a[L0 + "dw7"], a[L0 + "dw5"], a[L0 + "dw3"]]),
        **tables(),
    }
    arrays = {name: np.ascontiguousarray(v) for name, v in arrays.items()}
    nc = bacc.Bacc("TRN2", target_bir_lowering=False, num_devices=1)
    t = {name: nc.dram_tensor("in_" + name, v.shape, mybir.dt.from_np(v.dtype), kind="ExternalInput").ap()
         for name, v in arrays.items()}
    t["out"] = nc.dram_tensor("out", (B, KH, P, PIX), F32, kind="ExternalOutput").ap()
    build(nc, t)
    r = run_bass_kernel_spmd(nc, [{"in_" + name: v for name, v in arrays.items()}], core_ids=[0])
    return r.results[0]["out"].reshape(B, C, P, P)
```
